# Optimizing a Trainium2 kernel written in Bass

```python
import numpy as np
import jax
import jax.numpy as jnp

def _softmax(x, axis=-1):
    return jax.nn.softmax(x, axis=axis)

def _gelu(x):
    return jax.nn.gelu(x, approximate=True)

def _silu(x):
    return jax.nn.silu(x)

def _sigmoid(x):
    return jax.nn.sigmoid(x)

def _layernorm(x, axis=-1, eps=1e-05):
    m = jnp.mean(x, axis=axis, keepdims=True)
    v = jnp.var(x, axis=axis, keepdims=True)
    return (x - m) / jnp.sqrt(v + eps)

def _scatter_add(tgt, idx, src, axis=0):
    return tgt.at[idx].add(src)

def _segment_sum(src, seg, n):
    return jax.ops.segment_sum(src, seg, n)
kernel_name = 'mk_decoder_postln_d1_seqx_r2_d645f7'

def setup_inputs(seed: int=0):
    np.random.seed(seed)
    _w = jnp.asarray

    def _rec_inputs():
        import jax
        import jax.numpy as jnp
        _rk = jax.random.key(seed)
        x = -0.003407 + 1.001 * jax.random.normal(jax.random.fold_in(_rk, 1), (32, 100, 512), jnp.float32)
        _lenS = 100 - jax.random.randint(jax.random.fold_in(_rk, 7), (32,), 0, max(1, 100 // 4) + 1, jnp.int32)
        _lenS2 = 722 - jax.random.randint(jax.random.fold_in(_rk, 8), (32,), 0, max(1, 722 // 4) + 1, jnp.int32)
        _ctx_1024P = jax.random.normal(jax.random.fold_in(_rk, 11), (32, 16, 512), jnp.float32)
        _ctx_1024c = jax.random.dirichlet(jax.random.fold_in(_rk, 511), 0.3 * jnp.ones((16,), jnp.float32), (32, 722))
        _ctx_1024t = jnp.einsum('bsk,bkd->bsd', _ctx_1024c, _ctx_1024P)
        _ctx_1024t = _ctx_1024t * jax.lax.rsqrt(jnp.mean(jnp.square(_ctx_1024t)) + 1e-12) * 0.953939
        ctx_1024 = -5.72187e-05 + 0.999849 * (_ctx_1024t + 0.3 * jax.random.normal(jax.random.fold_in(_rk, 611), (32, 722, 512), jnp.float32))
        return (x, ctx_1024)
    x, ctx_1024 = _rec_inputs()

    def _L0_attn_setup():
        import jax, jax.numpy as jnp
        import numpy as np
        B, N, D_IN, D_OUT, H = (2, 1024, 512, 512, 16)
        HEAD_DIM = D_OUT // H
        key = jax.random.key(seed)
        ks = jax.random.split(key, 8)
        s = 0.02
        return {'x': jax.random.normal(ks[0], (B, N, D_IN), dtype=jnp.float32), 'Wq': jax.random.normal(ks[1], (D_IN, D_OUT), dtype=jnp.float32) * s, 'Wk': jax.random.normal(ks[2], (D_IN, D_OUT), dtype=jnp.float32) * s, 'Wv': jax.random.normal(ks[3], (D_IN, D_OUT), dtype=jnp.float32) * s, 'Wo': jax.random.normal(ks[4], (D_OUT, D_OUT), dtype=jnp.float32) * s, 'bo': jnp.zeros((D_OUT,), dtype=jnp.float32), 'w': jax.random.uniform(ks[5], (H,), dtype=jnp.float32), 'v': jax.random.uniform(ks[6], (H,), dtype=jnp.float32)}
    _L0_attn_all = _L0_attn_setup()
    _L0_attn_in = {k: v for k, v in _L0_attn_all.items() if k in ('Wq', 'Wk', 'Wv', 'Wo', 'bo', 'w', 'v')}
    del _L0_attn_all

    def _L0_xattn_setup():
        import jax, jax.numpy as jnp
        import numpy as np
        import math
        HIDDEN = 512
        HEADS = 16
        HEAD_DIM = HIDDEN // HEADS
        B, LQ, LK = (8, 16, 4096)
        key = jax.random.key(seed)
        ks = jax.random.split(key, 8)
        s = 1.0 / math.sqrt(HIDDEN)
        return {'query': jax.random.normal(ks[0], (B, LQ, HIDDEN), jnp.float32), 'key': jax.random.normal(ks[1], (B, LK, HIDDEN), jnp.float32), 'value': jax.random.normal(ks[2], (B, LK, HIDDEN), jnp.float32), 'Wq': jax.random.normal(ks[3], (HIDDEN, HIDDEN), jnp.float32) * s, 'bq': jnp.zeros((HIDDEN,), jnp.float32), 'Wk': jax.random.normal(ks[4], (HIDDEN, HIDDEN), jnp.float32) * s, 'bk': jnp.zeros((HIDDEN,), jnp.float32), 'Wv': jax.random.normal(ks[5], (HIDDEN, HIDDEN), jnp.float32) * s, 'bv': jnp.zeros((HIDDEN,), jnp.float32), 'Wo': jax.random.normal(ks[6], (HIDDEN, HIDDEN), jnp.float32) * s, 'bo': jnp.zeros((HIDDEN,), jnp.float32)}
    _L0_xattn_all = _L0_xattn_setup()
    _L0_xattn_in = {k: v for k, v in _L0_xattn_all.items() if k in ('Wq', 'bq', 'Wk', 'bk', 'Wv', 'bv', 'Wo', 'bo')}
    del _L0_xattn_all

    def _L0_ffn_setup():
        import jax, jax.numpy as jnp
        import numpy as np
        DIM = 512
        HIDDEN = 1536
        SCALE = 1.0 / 127.0

        def _dequant(w_int, dtype):
            return w_int.astype(dtype) * jnp.asarray(SCALE, dtype)
        key = jax.random.key(seed)
        k_x, k_g, k_u, k_d = jax.random.split(key, 4)
        x = jax.random.normal(k_x, (4, 1024, DIM), dtype=jnp.float32)
        w_gate = jax.random.randint(k_g, (HIDDEN, DIM), -127, 128, dtype=jnp.int32)
        w_up = jax.random.randint(k_u, (HIDDEN, DIM), -127, 128, dtype=jnp.int32)
        w_down = jax.random.randint(k_d, (DIM, HIDDEN), -127, 128, dtype=jnp.int32)
        return {'x': x, 'w_gate': w_gate, 'w_up': w_up, 'w_down': w_down}
    _L0_ffn_all = _L0_ffn_setup()
    _L0_ffn_in = {k: v for k, v in _L0_ffn_all.items() if k in ('w_gate', 'w_up', 'w_down')}
    del _L0_ffn_all
    return {'x': x, 'ctx_1024': ctx_1024, 'L0_attn_Wq': _L0_attn_in['Wq'], 'L0_attn_Wk': _L0_attn_in['Wk'], 'L0_attn_Wv': _L0_attn_in['Wv'], 'L0_attn_Wo': _L0_attn_in['Wo'], 'L0_attn_bo': _L0_attn_in['bo'], 'L0_attn_w': _L0_attn_in['w'], 'L0_attn_v': _L0_attn_in['v'], 'L0_xattn_Wq': _L0_xattn_in['Wq'], 'L0_xattn_bq': _L0_xattn_in['bq'], 'L0_xattn_Wk': _L0_xattn_in['Wk'], 'L0_xattn_bk': _L0_xattn_in['bk'], 'L0_xattn_Wv': _L0_xattn_in['Wv'], 'L0_xattn_bv': _L0_xattn_in['bv'], 'L0_xattn_Wo': _L0_xattn_in['Wo'], 'L0_xattn_bo': _L0_xattn_in['bo'], 'L0_ffn_w_gate': _L0_ffn_in['w_gate'], 'L0_ffn_w_up': _L0_ffn_in['w_up'], 'L0_ffn_w_down': _L0_ffn_in['w_down']}

def reference(x, ctx_1024, L0_attn_Wq, L0_attn_Wk, L0_attn_Wv, L0_attn_Wo, L0_attn_bo, L0_attn_w, L0_attn_v, L0_xattn_Wq, L0_xattn_bq, L0_xattn_Wk, L0_xattn_bk, L0_xattn_Wv, L0_xattn_bv, L0_xattn_Wo, L0_xattn_bo, L0_ffn_w_gate, L0_ffn_w_up, L0_ffn_w_down):
    import jax
    import jax.numpy as jnp

    def _L0_attn_ref(x, Wq, Wk, Wv, Wo, bo, w, v):
        import jax, jax.numpy as jnp
        import numpy as np
        B, N, D_IN, D_OUT, H = (2, 1024, 512, 512, 16)
        HEAD_DIM = D_OUT // H
        b, n, _ = x.shape
        h = w.shape[0]
        hd = Wq.shape[1] // h

        def proj(W):
            return (x @ W).reshape(b, n, h, hd).transpose(0, 2, 1, 3)
        q, k, val = (proj(Wq), proj(Wk), proj(Wv))
        pos = jnp.arange(n)
        R = jnp.abs(pos[:, None] - pos[None, :]).astype(x.dtype)
        wv = w[:, None, None]
        vv = v[:, None, None]
        R_hat = (1.0 + jnp.exp(vv)) / (1.0 + jnp.exp(vv - wv * R))
        scores = jax.nn.relu(jnp.einsum('bhqd,bhkd->bhqk', q, k)) * R_hat[None]
        causal = jnp.triu(jnp.ones((n, n), dtype=bool), k=1)
        scores = jnp.where(causal[None, None], -jnp.inf, scores)
        attn = jax.nn.softmax(scores / np.sqrt(hd).astype(x.dtype), axis=-1)
        ctx = jnp.einsum('bhqk,bhkd->bhqd', attn, val)
        ctx = ctx.transpose(0, 2, 1, 3).reshape(b, n, h * hd)
        return ctx @ Wo + bo

    def _L0_xattn_ref(query, key, value, Wq, bq, Wk, bk, Wv, bv, Wo, bo):
        import jax, jax.numpy as jnp
        import numpy as np
        import math
        HIDDEN = 512
        HEADS = 16
        HEAD_DIM = HIDDEN // HEADS
        B, LQ, LK = (8, 16, 4096)
        b, lq, _ = query.shape
        lk = key.shape[1]
        q = (query @ Wq.T + bq).reshape(b, lq, HEADS, HEAD_DIM)
        k = (key @ Wk.T + bk).reshape(b, lk, HEADS, HEAD_DIM)
        v = (value @ Wv.T + bv).reshape(b, lk, HEADS, HEAD_DIM)
        scale = 1.0 / math.sqrt(HEAD_DIM)
        scores = jnp.einsum('bqhd,bkhd->bhqk', q * scale, k)
        probs = jax.nn.softmax(scores, axis=-1)
        attn = jnp.einsum('bhqk,bkhd->bqhd', probs, v).reshape(b, lq, HIDDEN)
        return attn @ Wo.T + bo

    def _L0_ffn_ref(x, w_gate, w_up, w_down):
        import jax, jax.numpy as jnp
        import numpy as np
        DIM = 512
        HIDDEN = 1536
        SCALE = 1.0 / 127.0

        def _dequant(w_int, dtype):
            return w_int.astype(dtype) * jnp.asarray(SCALE, dtype)
        wg = _dequant(w_gate, x.dtype)
        wu = _dequant(w_up, x.dtype)
        wd = _dequant(w_down, x.dtype)
        gate = jnp.einsum('bsd,hd->bsh', x, wg)
        up = jnp.einsum('bsd,hd->bsh', x, wu)
        h = jax.nn.silu(gate) * up
        return jnp.einsum('bsh,dh->bsd', h, wd)
    x = _layernorm(x + _L0_attn_ref(x, L0_attn_Wq, L0_attn_Wk, L0_attn_Wv, L0_attn_Wo, L0_attn_bo, L0_attn_w, L0_attn_v), axis=-1)
    x = _layernorm(x + _L0_xattn_ref(x, ctx_1024, ctx_1024, L0_xattn_Wq, L0_xattn_bq, L0_xattn_Wk, L0_xattn_bk, L0_xattn_Wv, L0_xattn_bv, L0_xattn_Wo, L0_xattn_bo), axis=-1)
    x = _layernorm(x + _L0_ffn_ref(x, L0_ffn_w_gate, L0_ffn_w_up, L0_ffn_w_down), axis=-1)
    return x

_drawn_inputs = setup_inputs


def setup_inputs(seed=0):
    import zlib

    import numpy as np

    out = dict(_drawn_inputs(seed))
    spreads = {'L0_attn_bo': (0.0, 0.1),
     'L0_xattn_bq': (0.0, 0.309),
     'L0_xattn_bk': (0.0, 0.8),
     'L0_xattn_bv': (0.0, 0.1),
     'L0_xattn_bo': (0.0, 0.1)}
    factors = {'L0_attn_Wq': 3.077, 'L0_attn_Wk': 3.061, 'L0_attn_w': 8.0, 'L0_attn_v': 8.0}
    for name, (base, spread) in spreads.items():
        noise = np.random.default_rng([zlib.crc32(name.encode()), seed]).standard_normal(out[name].shape)
        drawn = base * np.exp(spread * noise) if base else spread * noise
        out[name] = jnp.asarray(drawn.astype(out[name].dtype))
    for name, factor in factors.items():
        out[name] = (out[name] * factor).astype(out[name].dtype)
    return out
```

```python
from contextlib import ExitStack

import concourse.bass as bass
from concourse import mybir

B, T, S, D, H = 32, 100, 722, 512, 16
HD = D // H
F = 1536
P = 128
KD = D // P
KF = F // P
N = B * T
GT = 640
NG = N // GT
TT = GT // P
HALF = GT // 2
QUADS = H // 4
QT = 4 * T
EPS = 1e-5
FSCALE = 1.0 / 127.0
ISQ = float(HD) ** -0.5
EXACT = 4096.0
MASKED = -3.0e38

F32 = mybir.dt.float32
F32R = mybir.dt.float32r
I32 = mybir.dt.int32
ALU = mybir.AluOpType
ACT = mybir.ActivationFunctionType
AX = mybir.AxisListType


def wait(eng, sem, value):
    if isinstance(value, int) and value <= 0:
        return
    eng.wait_ge(sem, value)


def wait_apart(eng, sem, value, passed):
    wait(eng, sem, value)
    eng.sem_inc(passed, 1)


def later(g):
    return not isinstance(g, int) or g > 0


def col(base, width):
    return slice(base, base + width) if isinstance(base, int) else bass.ds(base, width)


def products(pe, out, terms, chunks, lhs, rhs):
    last = None
    for k in range(chunks):
        for n, (a, b) in enumerate(terms):
            last = pe.matmul(out, lhs(a, k), rhs(b, k),
                             start=(k == 0 and n == 0), stop=(k == chunks - 1 and n == len(terms) - 1))
    return last


SPLIT = ((0, 0), (0, 1), (1, 0))


class Split:

    def __init__(self, sb, name, shape):
        self.parts = [sb(name + "_high", shape, F32R), sb(name + "_low", shape, F32R)]

    def __getitem__(self, part):
        return self.parts[part]


def split_weights(raws, targets, staging, sem_loaded, sem_high, sem_low):

    every = range(len(raws))

    def load(sp, which=every):
        for n in which:
            wait(sp, sem_high, n - 1)
            wait(sp, sem_low, n - 1)
            sp.dma_start(staging[n % 2], raws[n]).then_inc(sem_loaded[n % 2], 16)

    def high(act, which=every):
        for n in which:
            wait(act, sem_loaded[n % 2], 16 * (n // 2 + 1))
            act.activation(targets[n][0][:, :, :], staging[n % 2], ACT.Copy).then_inc(sem_high, 1)

    def low(dve, which=every):
        for n in which:
            t = targets[n]
            wait(dve, sem_high, n + 1)
            wait(dve, sem_loaded[n % 2], 16 * (n // 2 + 1))
            dve.tensor_tensor(t[1][:, :, :], staging[n % 2], t[0][:, :, :].bitcast(F32),
                              ALU.subtract).then_inc(sem_low, 1)

    return load, high, low


def phase_qkv(nc, sem, xT, wq, wk, wv, q_d, k_d, v_d):
    UNITS = 2 * KD * 2 + TT
    RING = 7
    assert UNITS % RING == 0
    with ExitStack() as ctx:
        def sb(name, shape, dt=F32):
            return ctx.enter_context(nc.sbuf_tensor("A_" + name, shape, dt))

        W = [Split(sb, n, [P, KD, D]) for n in ("wq", "wk", "wv")]
        staging = [sb(f"wstage{i}", [P, KD, D]) for i in range(2)]
        xraw = sb("xraw", [P, KD, GT])
        xs = [Split(sb, f"x{i}", [P, KD, GT]) for i in range(2)]
        qk = [[sb(f"{n}{i}", [P, KD, GT]) for n in "qk"] for i in range(2)]
        vo = [sb(f"v{i}", [P, TT, D]) for i in range(2)]
        ps = [ctx.enter_context(nc.psum_tensor(f"A_ps{i}", [P, 512], F32)) for i in range(RING)]

        w_loaded = [sem("A_w_loaded0"), sem("A_w_loaded1")]
        w_high, w_low = sem("A_w_high"), sem("A_w_low")
        x_loaded, x_high, x_low = sem("A_x_loaded"), sem("A_x_high"), sem("A_x_low")
        unit_done, passed = sem("A_unit_done"), sem("A_passed")
        act_out, dve_out = sem("A_act_out"), sem("A_dve_out")
        stored = [sem("A_stored0"), sem("A_stored1")]

        def of_act(u):
            return u % 2 == 0

        ACTS = sum(of_act(u) for u in range(UNITS))
        DVES = UNITS - ACTS

        def count(u):
            return sum(of_act(v) == of_act(u) for v in range(u + 1))

        def wait_out(eng, g, u):
            if u < 0:
                if isinstance(g, int):
                    return
                g, u = g - 1, u + UNITS
            eng.wait_ge(act_out if of_act(u) else dve_out, g * (ACTS if of_act(u) else DVES) + count(u))

        def groups(eng, body):
            body(0, 0)
            with eng.Fori(0, (NG - 1) // 2) as i:
                for k in range(2):
                    body(2 * i + (1 + k), (1 + k) % 2)

        def unit_out(u, par):
            if u < 16:
                w, m, h = u // 8, u // 2 % 4, u % 2
                return qk[par][w][:, m, h * HALF:(h + 1) * HALF], ps[u % RING][:, 0:HALF]
            return vo[par][:, u - 16, :], ps[u % RING][:, 0:D]

        with nc.Block() as block:
            load_w, high_w, low_w = split_weights(
                [w.rearrange("(k p) n -> p k n", p=P) for w in (wq, wk, wv)], W,
                [s[:, :, :] for s in staging], w_loaded, w_high, w_low)

            @block.sync
            def _(sp):
                x_cols = xT.rearrange("(k p) t -> p k t", p=P)

                def load_x(g):
                    sp.dma_start(xraw[:, :, :], x_cols[:, :, col(g * GT, GT)]).then_inc(x_loaded, 16)

                def store(g, par):
                    wait_apart(sp, act_out, (g + 1) * ACTS, passed)
                    wait_apart(sp, dve_out, (g + 1) * DVES, passed)
                    for n, dst in ((0, q_d), (1, k_d)):
                        sp.dma_start(dst.rearrange("(m p) t -> p m t", p=P)[:, :, col(g * GT, GT)],
                                     qk[par][n][:, :, :]).then_inc(stored[par], 16)
                    sp.dma_start(v_d[col(g * GT, GT), :].rearrange("(i p) n -> p i n", p=P), vo[par][:, :, :])\
                      .then_inc(stored[par], 16)

                load_x(0)
                load_w(sp)

                def body(g, par):
                    if isinstance(g, int):
                        return
                    sp.wait_ge(x_low, g)
                    load_x(g)
                    store(g - 1, 1 - par)

                groups(sp, body)
                store(NG - 1, (NG - 1) % 2)
                sp.wait_ge(stored[0], 48 * ((NG + 1) // 2))
                sp.wait_ge(stored[1], 48 * (NG // 2))

            @block.gpsimd
            def _(pool):
                def body(g, par):
                    pool.wait_ge(x_loaded, 16 * g + 16)
                    wait_apart(pool, unit_done, (g - 1) * UNITS, passed)
                    pool.tensor_copy(xs[par][0][:, :, :], xraw[:, :, :]).then_inc(x_high, 1)
                    pool.wait_ge(x_high, g + 1)
                    pool.tensor_tensor(xs[par][1][:, :, :], xraw[:, :, :], xs[par][0][:, :, :].bitcast(F32),
                                       ALU.subtract).then_inc(x_low, 1)

                groups(pool, body)

            @block.scalar
            def _(act):
                high_w(act)

                def body(g, par):
                    if later(g):
                        act.wait_ge(stored[par], 24 * (g - par))
                    for u in range(0, UNITS, 2):
                        dst, src = unit_out(u, par)
                        act.wait_ge(unit_done, g * UNITS + u + 1)
                        act.activation(dst, src, ACT.Copy).then_inc(act_out, 1)

                groups(act, body)

            @block.vector
            def _(dve):
                low_w(dve)

                def body(g, par):
                    if later(g):
                        dve.wait_ge(stored[par], 24 * (g - par))
                    for u in range(1, UNITS, 2):
                        dst, src = unit_out(u, par)
                        dve.wait_ge(unit_done, g * UNITS + u + 1)
                        dve.tensor_copy(dst, src).then_inc(dve_out, 1)

                groups(dve, body)

            @block.tensor
            def _(pe):
                def body(g, par):
                    pe.wait_ge(x_low, g + 1)
                    for u in range(UNITS):
                        wait_out(pe, g, u - RING)
                        if isinstance(g, int):
                            pe.wait_ge(w_low, min(u // 8, 2) + 1)
                        x = xs[par]
                        if u < 16:
                            w, m, h = u // 8, u // 2 % 4, u % 2
                            last = products(pe, ps[u % RING][:, 0:HALF], SPLIT, KD,
                                            lambda a, k: W[w][a][:, k, m * P:(m + 1) * P],
                                            lambda b, k: x[b][:, k, h * HALF:(h + 1) * HALF])
                        else:
                            i = u - 16
                            last = products(pe, ps[u % RING][:, 0:D], SPLIT, KD,
                                            lambda a, k: x[a][:, k, i * P:(i + 1) * P],
                                            lambda b, k: W[2][b][:, k, :])
                        last.then_inc(unit_done, 1)

                groups(pe, body)


def phase_self_attention(nc, sem, q_d, k_d, v_d, w, v, o_d):
    STEPS = 2 * QUADS
    with ExitStack() as ctx:
        def sb(name, shape, dt=F32):
            return ctx.enter_context(nc.sbuf_tensor("B_" + name, shape, dt))

        def psum(name):
            return ctx.enter_context(nc.psum_tensor("B_" + name, [P, 512], F32))

        qs = [sb(f"q{i}", [P, QUADS, T]) for i in range(2)]
        kd = [sb(f"kdiag{i}", [P, QUADS, 4, T]) for i in range(2)]
        vs = [sb(f"v{i}", [T, D]) for i in range(2)]
        rhat = sb("rhat", [T, H, T])
        masked = sb("masked", [T, T])
        keep = sb("keep", [T, T])
        dist_i = sb("dist_i", [T, T], I32)
        dist = sb("dist", [T, T])
        arg = sb("arg", [T, H, T])
        wb, vb, neg_w, ev = (sb(n, [T, H]) for n in ("wb", "vb", "neg_w", "ev"))
        ident = sb("ident", [P, P])
        s_rel = [sb(f"s_rel{i}", [T, 4, T]) for i in range(2)]
        s_msk = [sb(f"s_msk{i}", [T, 4, T]) for i in range(2)]
        e = [sb(f"e{i}", [T, 4, T]) for i in range(2)]
        pn = [sb(f"pn{i}", [T, 4, T]) for i in range(2)]
        pT = [sb(f"pT{i}", [T, 4, T]) for i in range(2)]
        neg_max = sb("neg_max", [T, 4, 4])
        rowsum = sb("rowsum", [T, 4, 4])
        inv = sb("inv", [T, 4, 4])
        oo = [sb(f"o{i}", [P, QUADS, 2 * T]) for i in range(2)]
        ps_s = [psum(f"ps_s{i}") for i in range(2)]
        ps_t = [psum(f"ps_t{i}") for i in range(2)]
        ps_o = [psum(f"ps_o{i}") for i in range(2)]

        wv_loaded, consts, zeroed = sem("B_wv_loaded"), sem("B_consts"), sem("B_zeroed")
        table = sem("B_table")
        table_exp = sem("B_table_exp")
        qk_loaded = [sem("B_qk_loaded0"), sem("B_qk_loaded1")]
        v_loaded = [sem("B_v_loaded0"), sem("B_v_loaded1")]
        s_done, rel_done, max_done, msk_done = sem("B_s_done"), sem("B_rel_done"), sem("B_max_done"), sem("B_msk_done")
        exp_done, inv_done, norm_done = sem("B_exp_done"), sem("B_inv_done"), sem("B_norm_done")
        t_done, pT_done, pv_done, o_done = sem("B_t_done"), sem("B_pT_done"), sem("B_pv_done"), sem("B_o_done")
        stored, passed = [sem("B_stored0"), sem("B_stored1")], sem("B_passed")

        def batches(eng, body, drain=None):
            for k in range(2):
                body(k, k)
            with eng.Fori(1, B // 2) as i:
                for k in range(2):
                    body(2 * i + k, k)

        with nc.Block() as block:

            @block.sync
            def _(sp):
                sp.dma_start(wb[:, :], w.rearrange("(a h) -> a h", a=1).broadcast_to([T, H])).then_inc(wv_loaded, 16)
                sp.dma_start(vb[:, :], v.rearrange("(a h) -> a h", a=1).broadcast_to([T, H])).then_inc(wv_loaded, 16)
                q_rows = q_d.rearrange("(m p) t -> p m t", p=P)
                k_rows = k_d.rearrange("(m p) t -> p m t", p=P)
                o_rows = o_d.rearrange("(m p) t -> p m t", p=P)

                def load_qk(b, par):
                    sp.dma_start(qs[par][:, :, :], q_rows[:, :, col(b * T, T)]).then_inc(qk_loaded[par], 16)
                    for j in range(4):
                        sp.dma_start(kd[par][HD * j:HD * j + HD, :, j, :],
                                     k_rows[HD * j:HD * j + HD, :, col(b * T, T)]).then_inc(qk_loaded[par], 16)

                def load_v(b, par):
                    sp.dma_start(vs[par][:, :], v_d[col(b * T, T), :]).then_inc(v_loaded[par], 16)

                def store(b, par):
                    wait_apart(sp, o_done, QUADS * (b + 1), passed)
                    for r in range(4):
                        sp.dma_start(o_rows[HD * r:HD * r + HD, :, col(b * T, T)],
                                     oo[par][HD * r:HD * r + HD, :, (r % 2) * T:(r % 2) * T + T])\
                          .then_inc(stored[par], 16)

                sp.wait_ge(zeroed, 2)
                for b in range(2):
                    load_qk(b, b)
                    load_v(b, b)
                with sp.Fori(0, B // 2 - 1) as i:
                    for k in range(2):
                        b = 2 * i + k
                        sp.wait_ge(s_done, QUADS * (b + 1))
                        load_qk(b + 2, k)
                        sp.wait_ge(pv_done, QUADS * (b + 1))
                        load_v(b + 2, k)
                        store(b, k)
                for b in (B - 2, B - 1):
                    store(b, b % 2)
                for par in range(2):
                    sp.wait_ge(stored[par], 64 * (B // 2))

            @block.gpsimd
            def _(pool):
                for i in range(2):
                    pool.memset(kd[i][:, :, :, :], 0.0).then_inc(zeroed, 1)
                pool.iota(dist_i[:, :], [[-1, T]], base=0, channel_multiplier=1).then_inc(consts, 1)
                pool.memset(keep[:, :], ISQ).then_inc(consts, 1)
                pool.memset(masked[:, :], 0.0).then_inc(consts, 1)
                pool.memset(ident[:, :], 0.0).then_inc(consts, 1)
                pool.wait_ge(consts, 4)
                pool.affine_select(out=keep[:, :], in_=keep[:, :], compare_op=ALU.is_ge, fill=0.0,
                                   base=0, pattern=[[-1, T]], channel_multiplier=1).then_inc(consts, 1)
                pool.affine_select(out=masked[:, :], in_=masked[:, :], compare_op=ALU.is_ge, fill=MASKED,
                                   base=0, pattern=[[-1, T]], channel_multiplier=1).then_inc(consts, 1)
                pool.affine_select(out=ident[:, :], in_=ident[:, :], compare_op=ALU.not_equal, fill=1.0,
                                   base=0, pattern=[[-1, P]], channel_multiplier=1).then_inc(consts, 1)
                pool.wait_ge(consts, 7)

                def add_mask(n, s):
                    pool.wait_ge(rel_done, n + 1)
                    wait(pool, exp_done, 4 * n - 4)
                    pool.tensor_tensor(s_msk[s % 2][:, :, :], s_rel[s % 2][:, :, :],
                                       masked[:, :].unsqueeze(1).broadcast_to([T, 4, T]), ALU.add).then_inc(msk_done, 1)

                def normalise(n, s):
                    pool.wait_ge(inv_done, n + 1)
                    pool.wait_ge(exp_done, 4 * n + 4)
                    wait(pool, t_done, n - 1)
                    pool.tensor_tensor(pn[s % 2][:, :, :], e[s % 2][:, :, :],
                                       inv[:, s % 4, :].unsqueeze(2).broadcast_to([T, 4, T]), ALU.mult)\
                        .then_inc(norm_done, 1)

                def body(b, par):
                    for m in range(QUADS):
                        n, s = QUADS * b + m, QUADS * par + m
                        add_mask(n, s)
                        if not (isinstance(n, int) and n < 1):
                            normalise(n - 1, s - 1)

                batches(pool, body)
                normalise(QUADS * B - 1, STEPS - 1)

            @block.scalar
            def _(act):
                act.wait_ge(wv_loaded, 32)
                act.activation(ev[:, :], vb[:, :], ACT.Exp).then_inc(table_exp, 1)
                act.wait_ge(table, 5)
                act.activation(arg[:, :, :], arg[:, :, :], ACT.Exp).then_inc(table_exp, 1)

                def exps(n, s):
                    act.wait_ge(msk_done, n + 1)
                    act.wait_ge(max_done, n + 1)
                    wait(act, norm_done, n - 1)
                    for j in range(4):
                        act.activation(e[s % 2][:, j, :], s_msk[s % 2][:, j, :], ACT.Exp,
                                       bias=neg_max[:, s % 4, j:j + 1],
                                       accum_out=rowsum[:, s % 4, j:j + 1]).then_inc(exp_done, 1)

                def body(b, par):
                    for m in range(QUADS):
                        n, s = QUADS * b + m, QUADS * par + m
                        exps(n, s)
                        if not (isinstance(n, int) and n < 4):
                            m4, par4 = m, 1 - par
                            act.wait_ge(pv_done, n - 3)
                            if m == 0 and not (isinstance(b, int)):
                                act.wait_ge(stored[par4], 32 * (b - 1 - par4))
                            act.activation(oo[par4][:, m4, :], ps_o[m4 % 2][:, 0:2 * T], ACT.Copy)\
                               .then_inc(o_done, 1)

                batches(act, body)
                act.wait_ge(stored[1], 32 * (B - 2))
                for m in range(QUADS):
                    act.wait_ge(pv_done, QUADS * (B - 1) + m + 1)
                    act.activation(oo[1][:, m, :], ps_o[m % 2][:, 0:2 * T], ACT.Copy).then_inc(o_done, 1)

            @block.vector
            def _(dve):
                dve.wait_ge(wv_loaded, 32)
                dve.wait_ge(consts, 7)
                dve.tensor_scalar(neg_w[:, :], wb[:, :], -1.0, None, ALU.mult).then_inc(table, 1)
                dve.tensor_scalar(dist[:, :], dist_i[:, :], 0.0, None, ALU.max).then_inc(table, 1)
                dve.wait_ge(table, 2)
                for h in range(H):
                    last = dve.tensor_scalar(arg[:, h, :], dist[:, :], neg_w[:, h:h + 1], vb[:, h:h + 1],
                                             ALU.mult, ALU.add)
                last.then_inc(table, 3)
                dve.wait_ge(table_exp, 2)
                dve.tensor_scalar(arg[:, :, :], arg[:, :, :], 1.0, None, ALU.add).then_inc(table, 1)
                dve.tensor_scalar(ev[:, :], ev[:, :], 1.0, None, ALU.add).then_inc(table, 1)
                dve.wait_ge(table, 7)
                dve.reciprocal(rhat[:, :, :], arg[:, :, :]).then_inc(table, 1)
                dve.wait_ge(table, 8)
                dve.tensor_tensor(rhat[:, :, :], rhat[:, :, :], ev[:, :].unsqueeze(2).broadcast_to([T, H, T]),
                                  ALU.mult).then_inc(table, 1)
                dve.wait_ge(table, 9)
                dve.tensor_tensor(rhat[:, :, :], rhat[:, :, :], keep[:, :].unsqueeze(1).broadcast_to([T, H, T]),
                                  ALU.mult).then_inc(table, 1)
                dve.wait_ge(table, 10)

                def scale_max(n, s, m):
                    dve.wait_ge(s_done, n + 1)
                    wait(dve, msk_done, n - 1)
                    dve.scalar_tensor_tensor(
                        s_rel[s % 2][:, :, :], ps_s[s % 2][0:T, 0:QT].rearrange("p (j t) -> p j t", j=4), 0.0,
                        rhat[:, 4 * m:4 * m + 4, :], ALU.max, ALU.mult).then_inc(rel_done, 1)
                    dve.wait_ge(rel_done, n + 1)
                    wait(dve, exp_done, 4 * n - 12)
                    dve.tensor_reduce(neg_max[:, s % 4, :], s_rel[s % 2][:, :, :], AX.X, ALU.max, negate=True)\
                        .then_inc(max_done, 1)

                def invert(n, s):
                    dve.wait_ge(exp_done, 4 * n + 4)
                    wait(dve, norm_done, n - 3)
                    dve.reciprocal(inv[:, s % 4, :], rowsum[:, s % 4, :]).then_inc(inv_done, 1)

                def take_transposed(n, s):
                    dve.wait_ge(t_done, n + 1)
                    wait(dve, pv_done, n - 1)
                    dve.tensor_copy(pT[s % 2][:, :, :], ps_t[s % 2][0:T, 0:QT].rearrange("p (j t) -> p j t", j=4))\
                       .then_inc(pT_done, 1)

                def body(b, par):
                    for m in range(QUADS):
                        n, s = QUADS * b + m, QUADS * par + m
                        scale_max(n, s, m)
                        if not (isinstance(n, int) and n < 1):
                            invert(n - 1, s - 1)
                        if not (isinstance(n, int) and n < 2):
                            take_transposed(n - 2, s - 2)

                batches(dve, body)
                end = QUADS * B
                invert(end - 1, STEPS - 1)
                take_transposed(end - 2, STEPS - 2)
                take_transposed(end - 1, STEPS - 1)

            @block.tensor
            def _(pe):
                pe.wait_ge(consts, 7)

                def scores(b, par, n, s, m):
                    if m == 0:
                        pe.wait_ge(qk_loaded[par], 40 * (b - par) + 80)
                    wait(pe, rel_done, n - 1)
                    pe.matmul(ps_s[s % 2][0:T, 0:QT], qs[par][:, m, :], kd[par][:, m, :, :],
                              start=True, stop=True).then_inc(s_done, 1)

                def transposes(n, s):
                    pe.wait_ge(norm_done, n + 1)
                    wait(pe, pT_done, n - 1)
                    for j in range(4):
                        last = pe.transpose(ps_t[s % 2][0:T, j * T:(j + 1) * T], pn[s % 2][:, j, :], ident[0:T, 0:T])
                    last.then_inc(t_done, 1)

                def weighted_sum(n, s, v_count):
                    m, par = s % STEPS % QUADS, s % STEPS // QUADS
                    if m == 0:
                        pe.wait_ge(v_loaded[par], v_count)
                    pe.wait_ge(pT_done, n + 1)
                    wait(pe, o_done, n - 1)
                    for g in range(2):
                        c = (2 * m + g) * 2 * HD
                        last = pe.matmul(ps_o[m % 2][2 * HD * g:2 * HD * (g + 1), 0:2 * T], vs[par][:, c:c + 2 * HD],
                                         pT[s % 2][:, 2 * g:2 * g + 2, :], start=True, stop=True,
                                         tile_position=(0, 2 * HD * g))
                    last.then_inc(pv_done, 1)

                def v_count(b, par):
                    return 8 * (b - par) + 16

                def body(b, par):
                    for m in range(QUADS):
                        n, s = QUADS * b + m, QUADS * par + m
                        scores(b, par, n, s, m)
                        if not (isinstance(n, int) and n < 2):
                            transposes(n - 2, s - 2)
                        if not (isinstance(n, int) and n < 3):
                            back = m < 3
                            weighted_sum(n - 3, s - 3, v_count(b - 1, 1 - par) if back else v_count(b, par))

                batches(pe, body)
                end = QUADS * B
                for n in (end - 2, end - 1):
                    weighted_sum(n - 1, STEPS + n - 1 - end, v_count(B - 1, 1))
                    transposes(n, STEPS + n - end)
                weighted_sum(end - 1, STEPS - 1, v_count(B - 1, 1))


def phase_norm_and_queries(nc, sem, o_d, x, wo, bo, wq, bq, x1_d, cq_d):
    QU = KD * 2
    with ExitStack() as ctx:
        def sb(name, shape, dt=F32):
            return ctx.enter_context(nc.sbuf_tensor("C_" + name, shape, dt))

        def psum(name):
            return ctx.enter_context(nc.psum_tensor("C_" + name, [P, 512], F32))

        W = [Split(sb, n, [P, KD, D]) for n in ("wo", "wq")]
        staging = [sb(f"wstage{i}", [P, KD, D]) for i in range(2)]
        bo_b, bq_c = sb("bo_b", [P, D]), sb("bq_c", [P, KD])
        oraw, os = sb("oraw", [P, KD, GT]), Split(sb, "o", [P, KD, GT])
        xb = sb("xb", [P, TT, D])
        r = [sb(f"r{i}", [P, D]) for i in range(2)]
        stats = [sb(f"stats{i}", [P, 6]) for i in range(2)]
        mv = [sb(f"mv{i}", [P, 2]) for i in range(2)]
        var_eps = [sb(f"var_eps{i}", [P, 1]) for i in range(2)]
        rstd = [sb(f"rstd{i}", [P, 1]) for i in range(2)]
        minus_half = sb("minus_half", [P, 1])
        x1 = sb("x1", [P, TT, D])
        x1s = Split(sb, "x1s", [P, KD, GT])
        qf = [sb(f"qf{i}", [P, HALF]) for i in range(2)]
        qo = Split(sb, "qo", [P, KD, GT])
        ident = sb("ident", [P, P])
        ps_y = [psum(f"ps_y{i}") for i in range(2)]
        ps_t = [psum(f"ps_t{i}") for i in range(2)]
        ps_q = [psum(f"ps_q{i}") for i in range(4)]

        w_loaded = [sem("C_w_loaded0"), sem("C_w_loaded1")]
        w_high, w_low = sem("C_w_high"), sem("C_w_low")
        b_loaded, consts = sem("C_b_loaded"), sem("C_consts")
        o_loaded, o_high, o_low = sem("C_o_loaded"), sem("C_o_high"), sem("C_o_low")
        x_loaded, xb_done = sem("C_x_loaded"), sem("C_xb_done")
        y_done, r_done, stat_done, mv_done, eps_done = (sem("C_" + n) for n in
                                                        ("y_done", "r_done", "stat_done", "mv_done", "eps_done"))
        rstd_done, x1_done, x1_stored = sem("C_rstd_done"), sem("C_x1_done"), sem("C_x1_stored")
        t_done, th_done, tl_done = sem("C_t_done"), sem("C_th_done"), sem("C_tl_done")
        q_done, qf_done, qh_done, ql_done = sem("C_q_done"), sem("C_qf_done"), sem("C_qh_done"), sem("C_ql_done")
        q_stored, passed = sem("C_q_stored"), sem("C_passed")

        def former(n, i):
            return n if i == 0 else n - 1

        with nc.Block() as block:
            load_w, high_w, low_w = split_weights(
                [w.rearrange("(k p) n -> p k n", p=P) for w in (wo, wq)], W,
                [s[:, :, :] for s in staging], w_loaded, w_high, w_low)

            @block.sync
            def _(sp):
                def load(g):
                    if later(g):
                        sp.wait_ge(o_low, g)
                    sp.dma_start(oraw[:, :, :], o_d.rearrange("(k p) t -> p k t", p=P)[:, :, col(g * GT, GT)])\
                      .then_inc(o_loaded, 16)
                    if later(g):
                        sp.wait_ge(r_done, TT * g)
                    sp.dma_start(xb[:, :, :], x[col(g * GT, GT), :].rearrange("(i p) n -> p i n", p=P))\
                      .then_inc(x_loaded, 16)

                def store(g):
                    wait_apart(sp, x1_done, TT * (g + 1), passed)
                    sp.dma_start(x1_d[col(g * GT, GT), :].rearrange("(i p) n -> p i n", p=P), x1[:, :, :])\
                      .then_inc(x1_stored, 16)

                def store_q(g):
                    wait_apart(sp, ql_done, QU * (g + 1), passed)
                    wait_apart(sp, qh_done, QU * (g + 1), passed)
                    for part in range(2):
                        sp.dma_start(cq_d[part].rearrange("(m p) t -> p m t", p=P)[:, :, col(g * GT, GT)],
                                     qo[part][:, :, :].bitcast(F32)).then_inc(q_stored, 16)

                load(0)
                load_w(sp)
                sp.dma_start(bo_b[:, :], bo.rearrange("(a n) -> a n", a=1).broadcast_to([P, D])).then_inc(b_loaded, 16)
                sp.dma_start(bq_c[:, :], bq).then_inc(b_loaded, 16)
                with sp.Fori(0, NG - 1) as g:
                    load(g + 1)
                    store(g)
                    store_q(g)
                store(NG - 1)
                store_q(NG - 1)
                sp.wait_ge(x1_stored, 16 * NG)
                sp.wait_ge(q_stored, 32 * NG)

            @block.gpsimd
            def _(pool):
                pool.memset(minus_half[:, :], -0.5).then_inc(consts, 1)
                pool.memset(ident[:, :], 0.0).then_inc(consts, 1)
                pool.wait_ge(consts, 2)
                pool.affine_select(out=ident[:, :], in_=ident[:, :], compare_op=ALU.not_equal, fill=1.0,
                                   base=0, pattern=[[-1, P]], channel_multiplier=1).then_inc(consts, 1)
                pool.wait_ge(b_loaded, 32)

                def prepare(g):
                    pool.wait_ge(o_high, g + 1)
                    pool.wait_ge(o_loaded, 16 * g + 16)
                    if later(g):
                        pool.wait_ge(y_done, TT * g)
                    pool.tensor_tensor(os[1][:, :, :], oraw[:, :, :], os[0][:, :, :].bitcast(F32),
                                       ALU.subtract).then_inc(o_low, 1)
                    pool.wait_ge(x_loaded, 16 * g + 16)
                    pool.tensor_tensor(xb[:, :, :], xb[:, :, :], bo_b[:, :].unsqueeze(1).broadcast_to([P, TT, D]),
                                       ALU.add).then_inc(xb_done, 1)

                def rstds(g):
                    for i in range(TT):
                        n, s = TT * g + i, i % 2
                        pool.wait_ge(eps_done, n + 1)
                        wait(pool, x1_done, former(n, i))
                        pool.tensor_tensor(rstd[s][:, :], var_eps[s][:, :], minus_half[:, :], ALU.pow)\
                            .then_inc(rstd_done, 1)

                def low_q(g):
                    for u in range(QU):
                        n = QU * g + u
                        pool.wait_ge(qh_done, n + 1)
                        pool.wait_ge(qf_done, n + 1)
                        if later(g) and u == 0:
                            pool.wait_ge(q_stored, 32 * g)
                        pool.tensor_tensor(qo[1][:, u // 2, u % 2 * HALF:(u % 2 + 1) * HALF], qf[u % 2][:, :],
                                           qo[0][:, u // 2, u % 2 * HALF:(u % 2 + 1) * HALF].bitcast(F32),
                                           ALU.subtract).then_inc(ql_done, 1)

                prepare(0)
                rstds(0)
                with pool.Fori(0, NG - 1) as g:
                    prepare(g + 1)
                    rstds(g + 1)
                    low_q(g)
                low_q(NG - 1)

            @block.scalar
            def _(act):
                def high_o(g):
                    act.wait_ge(o_loaded, 16 * g + 16)
                    if later(g):
                        act.wait_ge(y_done, TT * g)
                    act.activation(os[0][:, :, :], oraw[:, :, :], ACT.Copy).then_inc(o_high, 1)

                def high_x1(g):
                    for i in range(TT):
                        n = TT * g + i
                        act.wait_ge(t_done, n + 1)
                        if later(g) and i == 0:
                            act.wait_ge(q_done, QU * g)
                        act.activation(x1s[0][:, :, i * P:(i + 1) * P],
                                       ps_t[i % 2][:, :].rearrange("p (k c) -> p k c", k=KD), ACT.Copy)\
                           .then_inc(th_done, 1)

                def high_q(g):
                    for u in range(QU):
                        act.wait_ge(qf_done, QU * g + u + 1)
                        if later(g) and u == 0:
                            act.wait_ge(q_stored, 32 * g)
                        act.activation(qo[0][:, u // 2, u % 2 * HALF:(u % 2 + 1) * HALF], qf[u % 2][:, :], ACT.Copy)\
                           .then_inc(qh_done, 1)

                high_o(0)
                high_w(act)
                with act.Fori(0, NG - 1) as g:
                    high_x1(g)
                    high_o(g + 1)
                    high_q(g)
                high_x1(NG - 1)
                high_q(NG - 1)

            @block.vector
            def _(dve):
                low_w(dve)

                def normalise(n, i, s):
                    dve.wait_ge(rstd_done, n + 1)
                    dve.tensor_scalar(x1[:, i, :], r[s][:, :], mv[s][:, 0:1], rstd[s][:, 0:1],
                                      ALU.subtract, ALU.mult).then_inc(x1_done, 1)

                def layer_norm(g):
                    for i in range(TT):
                        n, s = TT * g + i, i % 2
                        dve.wait_ge(y_done, n + 1)
                        if i == 0:
                            dve.wait_ge(xb_done, g + 1)
                        wait(dve, x1_done, former(n, i))
                        dve.tensor_tensor(r[s][:, :], ps_y[s][:, :], xb[:, i, :], ALU.add).then_inc(r_done, 1)
                        dve.wait_ge(r_done, n + 1)
                        dve.bn_stats(stats[s][:, :], r[s][:, :]).then_inc(stat_done, 1)
                        wait_apart(dve, stat_done, n + 1, passed)
                        dve.bn_aggr(mv[s][:, :], stats[s][:, :]).then_inc(mv_done, 1)
                        dve.wait_ge(mv_done, n + 1)
                        dve.tensor_scalar(var_eps[s][:, :], mv[s][:, 1:2], EPS, None, ALU.add).then_inc(eps_done, 1)
                        if later(g) and i == 1:
                            dve.wait_ge(x1_stored, 16 * g)
                        if i:
                            normalise(n - 1, i - 1, 1 - s)
                    normalise(TT * g + TT - 1, TT - 1, (TT - 1) % 2)

                def low_x1(g):
                    for i in range(TT):
                        n = TT * g + i
                        dve.wait_ge(t_done, n + 1)
                        dve.wait_ge(th_done, n + 1)
                        dve.tensor_tensor(x1s[1][:, :, i * P:(i + 1) * P],
                                          ps_t[i % 2][:, :].rearrange("p (k c) -> p k c", k=KD),
                                          x1s[0][:, :, i * P:(i + 1) * P].bitcast(F32), ALU.subtract)\
                           .then_inc(tl_done, 1)

                def scale_q(g):
                    for u in range(QU):
                        n = QU * g + u
                        dve.wait_ge(q_done, n + 1)
                        wait(dve, ql_done, n - 1)
                        dve.tensor_scalar(qf[u % 2][:, :], ps_q[u % 4][:, 0:HALF], bq_c[:, u // 2:u // 2 + 1], ISQ,
                                          ALU.add, ALU.mult).then_inc(qf_done, 1)

                dve.wait_ge(b_loaded, 32)
                layer_norm(0)
                low_x1(0)
                layer_norm(1)
                scale_q(0)
                with dve.Fori(1, NG - 1) as g:
                    low_x1(g)
                    layer_norm(g + 1)
                    scale_q(g)
                low_x1(NG - 1)
                scale_q(NG - 1)

            @block.tensor
            def _(pe):
                def project_o(g):
                    pe.wait_ge(o_low, g + 1)
                    for i in range(TT):
                        n = TT * g + i
                        wait(pe, r_done, former(n, i))
                        products(pe, ps_y[i % 2][:, :], SPLIT, KD,
                                 lambda a, k: os[a][:, k, i * P:(i + 1) * P],
                                 lambda b, k: W[0][b][:, k, :]).then_inc(y_done, 1)

                def transpose_x1(g):
                    for i in range(TT):
                        n = TT * g + i
                        pe.wait_ge(x1_done, n + 1)
                        wait(pe, tl_done, former(n, i))
                        for k in range(KD):
                            last = pe.transpose(ps_t[i % 2][:, k * P:(k + 1) * P], x1[:, i, k * P:(k + 1) * P],
                                                ident[:, :])
                        last.then_inc(t_done, 1)

                def project_q(g):
                    pe.wait_ge(tl_done, TT * (g + 1))
                    for u in range(QU):
                        n, m, h = QU * g + u, u // 2, u % 2
                        wait(pe, qf_done, n - 3)
                        products(pe, ps_q[u % 4][:, 0:HALF], SPLIT, KD,
                                 lambda a, k: W[1][a][:, k, m * P:(m + 1) * P],
                                 lambda b, k: x1s[b][:, k, h * HALF:(h + 1) * HALF]).then_inc(q_done, 1)

                pe.wait_ge(w_low, 1)
                project_o(0)
                pe.wait_ge(consts, 3)
                transpose_x1(0)
                project_o(1)
                pe.wait_ge(w_low, 2)
                project_q(0)
                with pe.Fori(1, NG - 1) as g:
                    transpose_x1(g)
                    project_o(g + 1)
                    project_q(g)
                transpose_x1(NG - 1)
                project_q(NG - 1)


def phase_cross_attention(nc, sem, ctxT, cq_d, wk, bk, wv, bv, o_d):
    ST = -(-S // P)
    LAST = S - (ST - 1) * P
    KC = (S // 2 + 1, S // 2 - 1)
    SH = S // 2
    PAIRS = H // 2
    KU = 2 * QUADS
    U = KU + ST
    assert U <= H
    with ExitStack() as ctx:
        def sb(name, shape, dt=F32):
            return ctx.enter_context(nc.sbuf_tensor("D_" + name, shape, dt))

        W = [Split(sb, n, [P, KD, D]) for n in ("wk", "wv")]
        craw = [sb(f"craw{i}", [P, S]) for i in range(2)]
        cs = [Split(sb, f"ctx{i}", [P, KD, S]) for i in range(2)]
        ks = [sb(f"keys{i}", [P, PAIRS, S], F32R) for i in range(2)]
        vs = [sb(f"values{i}", [P, ST, D]) for i in range(2)]
        qs = sb("queries", [P, PAIRS, 2, 2, T], F32R)
        e = [sb(f"e{i}", [T, ST * P]) for i in range(4)]
        pT = [sb(f"pT{i}", [P, ST, QT]) for i in range(2)]
        oo = [sb(f"o{i}", [P, QUADS, 2 * T]) for i in range(2)]
        bk_c, bv_c = sb("bk_c", [P, KD]), sb("bv_c", [P, KD])
        neg_max, rowsum, inv = (sb(n, [T, 4]) for n in ("neg_max", "rowsum", "inv"))
        ident = sb("ident", [P, P])
        ps_s = [ctx.enter_context(nc.psum_tensor(f"D_ps_s{i}", [P, 1024], F32)) for i in range(2)]
        ps_t = [ctx.enter_context(nc.psum_tensor(f"D_ps_t{i}", [P, 512], F32)) for i in range(2)]
        ps_p = [ctx.enter_context(nc.psum_tensor(f"D_ps_p{i}", [P, 512], F32)) for i in range(2)]

        w_loaded = [sem("D_w_loaded0"), sem("D_w_loaded1")]
        w_high, w_low, b_loaded, consts = sem("D_w_high"), sem("D_w_low"), sem("D_b_loaded"), sem("D_consts")
        c_loaded = [sem("D_c_loaded0"), sem("D_c_loaded1")]
        c_high, c_low = sem("D_c_high"), sem("D_c_low")
        q_loaded = [sem("D_q_loaded0"), sem("D_q_loaded1")]
        u_done, kh_done, kl_done, v_done = sem("D_u_done"), sem("D_kh_done"), sem("D_kl_done"), sem("D_v_done")
        s_done, max_done, exp_done = sem("D_s_done"), sem("D_max_done"), sem("D_exp_done")
        inv_done, norm_done, t_done = sem("D_inv_done"), sem("D_norm_done"), sem("D_t_done")
        taken, pv_done, o_done = sem("D_taken"), sem("D_pv_done"), sem("D_o_done")
        stored, passed = [sem("D_stored0"), sem("D_stored1")], sem("D_passed")

        def both_banks(s):
            t = ps_s[s % 2][0:T, :]
            return bass.AP(t.tensor, t.offset, [list(t.ap[0]), [513, 2], [1, SH]])

        def batches(eng, step):
            for b in range(2):
                for h in range(H):
                    step(b, b, h)
            with eng.Fori(1, B // 2 - 1) as i:
                for k in range(2):
                    for h in range(H):
                        step(2 * i + k, k, h)
            for b in (B - 2, B - 1):
                for h in range(H):
                    step(b, b % 2, h)

        def bank(u):
            return (u + u // 4) % 2

        def bank_of_quad(h):
            return (h + h // 4 + 1) % 2 if h < U else 1

        def unit_here(b, h):
            return h < U and not (isinstance(b, int) and b == B - 1)

        def started(n, back):
            return not (isinstance(n, int) and n < back)

        with nc.Block() as block:
            staging = [t[:, :, :].rearrange("p a b -> p (a b)")[:, 0:KD * D].rearrange("p (k n) -> p k n", k=KD)
                       for t in pT]
            load_w, high_w, low_w = split_weights(
                [w.rearrange("(k p) n -> p k n", p=P) for w in (wk, wv)], W, staging, w_loaded, w_high, w_low)

            @block.sync
            def _(sp):
                c_rows = ctxT.rearrange("b (k p) t -> b p k t", p=P)
                o_rows = o_d.rearrange("(m p) t -> p m t", p=P)
                q_rows = cq_d.rearrange("a (g j r) t -> r j g a t", j=2, r=HD)

                def load_ctx(b, chunks=range(KD)):
                    for k in chunks:
                        n = KD * b + k
                        wait(sp, c_low, n - 1)
                        src = c_rows[b, :, k, :] if isinstance(b, int) else \
                            c_rows[bass.ds(b, 1), :, k, :].rearrange("a p t -> (a p) t")
                        sp.dma_start(craw[k % 2][:, :], src).then_inc(c_loaded[k % 2], 16)

                def load_q(b, half):
                    g = slice(PAIRS // 2 * half, PAIRS // 2 * (half + 1))
                    for c in range(2):
                        for j in range(2):
                            rows = slice(HD * (j + 2 * c), HD * (j + 2 * c + 1))
                            for a in range(2):
                                sp.dma_start(qs[rows, g, j, a, :].bitcast(F32),
                                             q_rows[:, j, g, a, col(b * T, T)]).then_inc(q_loaded[half], 16)

                def store(b, par):
                    wait_apart(sp, o_done, QUADS * (b + 1), passed)
                    for r in range(4):
                        sp.dma_start(o_rows[HD * r:HD * r + HD, :, col(b * T, T)],
                                     oo[par][HD * r:HD * r + HD, :, (r % 2) * T:(r % 2) * T + T])\
                          .then_inc(stored[par], 16)

                load_ctx(0, (0, 1))
                load_w(sp)
                sp.dma_start(bk_c[:, :], bk).then_inc(b_loaded, 16)
                sp.dma_start(bv_c[:, :], bv).then_inc(b_loaded, 16)
                load_ctx(0, (2, 3))
                sp.wait_ge(consts, 2)
                load_q(0, 0)
                load_q(0, 1)
                load_ctx(1)

                def body(b, par, first, last):
                    if not first:
                        sp.wait_ge(s_done, H * b)
                        load_q(b, 1)
                    if not last:
                        load_ctx(b + 2)
                    if not first:
                        store(b - 1, 1 - par)
                    if not (isinstance(b, int) and b == B - 1):
                        sp.wait_ge(s_done, H * b + H // 2)
                        load_q(b + 1, 0)

                body(0, 0, True, False)
                body(1, 1, False, False)
                with sp.Fori(1, B // 2 - 1) as i:
                    for k in range(2):
                        body(2 * i + k, k, False, False)
                body(B - 2, 0, False, True)
                body(B - 1, 1, False, True)
                store(B - 1, 1)
                for par in range(2):
                    sp.wait_ge(stored[par], 64 * (B // 2))

            @block.gpsimd
            def _(pool):
                pool.memset(ident[:, :], 0.0).then_inc(consts, 1)
                pool.memset(qs[:, :, :, :, :].bitcast(F32), 0.0).then_inc(consts, 1)
                pool.wait_ge(consts, 2)
                pool.affine_select(out=ident[:, :], in_=ident[:, :], compare_op=ALU.not_equal, fill=1.0,
                                   base=0, pattern=[[-1, P]], channel_multiplier=1).then_inc(consts, 1)
                for i in range(4):
                    pool.memset(e[i][:, S:ST * P], 0.0).then_inc(consts, 1)
                for i in range(2):
                    pool.memset(vs[i][:, ST - 1, :], 0.0).then_inc(consts, 1)

                def split(b, par):
                    for k in range(KD):
                        n = KD * b + k
                        if k == 0:
                            wait(pool, u_done, U * (b - 1))
                        wait_apart(pool, c_loaded[k % 2], 32 * b + 16 * (k // 2) + 16, passed)
                        pool.tensor_copy(cs[par][0][:, k, :], craw[k % 2][:, :]).then_inc(c_high, 1)
                        pool.wait_ge(c_high, n + 1)
                        pool.tensor_tensor(cs[par][1][:, k, :], craw[k % 2][:, :],
                                           cs[par][0][:, k, :].bitcast(F32), ALU.subtract).then_inc(c_low, 1)

                pool.wait_ge(c_low, KD)
                split(1, 1)
                with pool.Fori(1, B // 2) as i:
                    for k in range(2):
                        split(2 * i + k, k)

            def key_rows(u):
                return ((2 * (u // 2), slice(0, 64), slice(64, P)), (2 * (u // 2) + 1, slice(64, P), slice(0, 64)))

            def key_cols(u):
                return (0, KC[0]) if u % 2 == 0 else (KC[0], S)

            @block.scalar
            def _(act):
                def unit(b, par, u):
                    act.wait_ge(u_done, U * b + u + 1)
                    if u < KU:
                        c0, c1 = key_cols(u)
                        for pair, rows, _ in key_rows(u):
                            if u == 0:
                                wait(act, s_done, H * (b - 1))
                            act.activation(ks[par][rows, pair, c0:c1], ps_p[bank(u)][rows, 0:c1 - c0], ACT.Identity,
                                           bias=bk_c[rows, u // 2:u // 2 + 1]).then_inc(kh_done, 1)
                        return
                    i = u - KU
                    rows = P if i < ST - 1 else LAST
                    if i == 0:
                        wait(act, pv_done, QUADS * (b - 1))
                    act.activation(vs[par][0:rows, i, :], ps_p[bank(u)][0:rows, 0:D], ACT.Copy).then_inc(v_done, 1)

                def take_tiles(b, h):
                    n, quad = H * b + h, QUADS * b + h // 4
                    for half in range(2):
                        act.wait_ge(t_done, 2 * n + 1 + half)
                        if h % 4 == 0 and half == 0:
                            wait(act, pv_done, quad - 1)
                        act.activation(pT[h // 4 % 2][:, 3 * half:3 * half + 3, h % 4 * T:(h % 4 + 1) * T],
                                       ps_t[half][:, 0:3 * T].rearrange("p (a t) -> p a t", a=3),
                                       ACT.Copy).then_inc(taken, 1)

                def exps(n, h):
                    act.wait_ge(max_done, n + 1)
                    act.wait_ge(s_done, n + 1)
                    wait(act, t_done, 2 * n - 6)
                    wait(act, inv_done, n - 3)
                    act.activation(e[h % 4][:, 0:S].rearrange("p (a b) -> p a b", a=2), both_banks(h), ACT.Exp,
                                   bias=neg_max[:, h % 4:h % 4 + 1],
                                   accum_out=rowsum[:, h % 4:h % 4 + 1]).then_inc(exp_done, 1)

                def step(b, par, h):
                    exps(H * b + h, h)
                    if unit_here(b, h):
                        unit(b + 1, 1 - par, h)
                    if started(H * b + h, 2):
                        take_tiles(b, h - 2)

                def high_ctx(k):
                    act.wait_ge(c_loaded[k % 2], 16 * (k // 2) + 16)
                    act.activation(cs[0][0][:, k, :], craw[k % 2][:, :], ACT.Copy).then_inc(c_high, 1)

                high_ctx(0)
                high_ctx(1)
                high_w(act, [0])
                high_ctx(2)
                high_ctx(3)
                high_w(act, [1])
                act.wait_ge(w_low, 2)
                act.wait_ge(b_loaded, 32)
                act.wait_ge(consts, 9)
                for u in range(U):
                    unit(0, 0, u)
                batches(act, step)
                take_tiles(B - 1, H - 2)
                take_tiles(B - 1, H - 1)

            @block.vector
            def _(dve):
                def unit(b, par, u):
                    if u >= KU:
                        return
                    c0, c1 = key_cols(u)
                    for i, (pair, rows, low_rows) in enumerate(key_rows(u)):
                        dve.wait_ge(kh_done, 2 * (KU * b + u) + i + 1)
                        dve.wait_ge(u_done, U * b + u + 1)
                        if u == 0:
                            wait(dve, s_done, H * (b - 1))
                        dve.scalar_tensor_tensor(
                            ks[par][low_rows, pair, c0:c1], ps_p[bank(u)][rows, 0:c1 - c0], bk_c[rows, u // 2:u // 2 + 1],
                            ks[par][rows, pair, c0:c1].bitcast(F32), ALU.add, ALU.subtract).then_inc(kl_done, 1)

                def maximum(n, h):
                    dve.wait_ge(s_done, n + 1)
                    wait(dve, exp_done, n - 3)
                    dve.tensor_reduce(neg_max[:, h % 4:h % 4 + 1], both_banks(h), AX.XY, ALU.max, negate=True)\
                       .then_inc(max_done, 1)

                def normalise(n, h):
                    dve.wait_ge(exp_done, n + 1)
                    wait(dve, norm_done, n - 3)
                    dve.reciprocal(inv[:, h % 4:h % 4 + 1], rowsum[:, h % 4:h % 4 + 1]).then_inc(inv_done, 1)
                    dve.wait_ge(inv_done, n + 1)
                    dve.tensor_scalar(e[h % 4][:, 0:S], e[h % 4][:, 0:S], inv[:, h % 4:h % 4 + 1], None, ALU.mult)\
                       .then_inc(norm_done, 1)

                def take_result(b, par, m, at):
                    dve.wait_ge(pv_done, QUADS * b + m + 1)
                    if m == 0:
                        wait(dve, stored[par], 32 * (b - par))
                    dve.tensor_scalar(oo[par][:, m, :], ps_p[bank_of_quad(at)][:, 0:2 * T], bv_c[:, m:m + 1], None, ALU.add)\
                       .then_inc(o_done, 1)

                def step(b, par, h):
                    n = H * b + h
                    if h > 0 and unit_here(b, h - 1):
                        unit(b + 1, 1 - par, h - 1)
                    maximum(n, h)
                    if started(n, 1):
                        normalise(n - 1, h - 1)
                    if h % 4 == 0 and started(n, 8):
                        if h > 4:
                            take_result(b, par, h // 4 - 2, h - 1)
                        else:
                            take_result(b - 1, 1 - par, QUADS - 2 + h // 4, (h - 1) % H)

                def low_ctx(k):
                    dve.wait_ge(c_high, k + 1)
                    dve.wait_ge(c_loaded[k % 2], 16 * (k // 2) + 16)
                    dve.tensor_tensor(cs[0][1][:, k, :], craw[k % 2][:, :], cs[0][0][:, k, :].bitcast(F32),
                                      ALU.subtract).then_inc(c_low, 1)

                low_ctx(0)
                low_ctx(1)
                low_w(dve, [0])
                low_ctx(2)
                low_ctx(3)
                low_w(dve, [1])
                dve.wait_ge(w_high, 2)
                dve.wait_ge(b_loaded, 32)
                dve.wait_ge(consts, 9)
                for u in range(U):
                    unit(0, 0, u)
                batches(dve, step)
                normalise(H * B - 1, H - 1)
                take_result(B - 1, 1, QUADS - 2, H - 1)
                take_result(B - 1, 1, QUADS - 1, 3)

            @block.tensor
            def _(pe):
                def unit_read(b, u):
                    if 0 <= u < KU:
                        pe.wait_ge(kl_done, 2 * (KU * b + u + 1))
                    else:
                        wait(pe, v_done, ST * b + max(u - KU + 1, 0))

                def unit(b, par, u):
                    if u == 0:
                        pe.wait_ge(c_low, KD * (b + 1))
                    if isinstance(b, int) and b == 0 and u in (0, KU):
                        pe.wait_ge(w_low, 1 + u // KU)
                    unit_read(b, u - (1 if u % 4 == 0 else 2))
                    if u % 4 == 1:
                        wait(pe, o_done, QUADS * (b - 1) - 1 + u // 4)
                    c = cs[par]
                    if u < KU:
                        m, (c0, c1) = u // 2, key_cols(u)
                        last = products(pe, ps_p[bank(u)][:, 0:c1 - c0], SPLIT, KD,
                                        lambda a, k: W[0][a][:, k, m * P:(m + 1) * P],
                                        lambda a, k: c[a][:, k, c0:c1])
                    else:
                        i = u - KU
                        rows = P if i < ST - 1 else LAST
                        last = products(pe, ps_p[bank(u)][0:rows, 0:D], SPLIT, KD,
                                        lambda a, k: c[a][:, k, i * P:i * P + rows],
                                        lambda a, k: W[1][a][:, k, :])
                    last.then_inc(u_done, 1)

                def scores(b, par, n, h):
                    if h == 0:
                        pe.wait_ge(kl_done, 2 * KU * (b + 1))
                    if h % (H // 2) == 0:
                        pe.wait_ge(q_loaded[h // (H // 2)], 128 * (b + 1))
                    wait(pe, exp_done, n - 1)
                    g, j = h // 2, h % 2
                    for half, (c0, c1) in enumerate(((0, KC[0]), (S - KC[0], S))):
                        for a in range(2):
                            last = pe.matmul(ps_s[h % 2][0:T, 512 * half:512 * half + c1 - c0],
                                             qs[:, g, j, a, :], ks[par][:, g, c0:c1],
                                             start=(a == 0), stop=(a == 1))
                    last.then_inc(s_done, 1)

                def transposes(n, h):
                    pe.wait_ge(norm_done, n + 1)
                    for half in range(2):
                        wait(pe, taken, 2 * n - 1 + half)
                        for i in range(3):
                            t = 3 * half + i
                            last = pe.transpose(ps_t[half][:, i * T:(i + 1) * T], e[h % 4][:, t * P:(t + 1) * P],
                                                ident[0:T, 0:T])
                        last.then_inc(t_done, 1)

                def weighted_sum(b, par, m, at):
                    quad = QUADS * b + m
                    pe.wait_ge(taken, 8 * quad + 8)
                    if m == 0:
                        pe.wait_ge(v_done, ST * (b + 1))
                    out = ps_p[bank_of_quad(at)]
                    for i in range(ST):
                        for g in range(2):
                            c = (2 * m + g) * 2 * HD
                            last = pe.matmul(out[2 * HD * g:2 * HD * (g + 1), 0:2 * T], vs[par][:, i, c:c + 2 * HD],
                                             pT[m % 2][:, i, 2 * T * g:2 * T * (g + 1)],
                                             start=(i == 0), stop=(i == ST - 1), tile_position=(0, 2 * HD * g))
                    last.then_inc(pv_done, 1)

                def step(b, par, h):
                    n = H * b + h
                    scores(b, par, n, h)
                    if unit_here(b, h):
                        unit(b + 1, 1 - par, h)
                    if h % 4 == 3 and started(n, 7):
                        if isinstance(b, int) and b == B - 1:
                            pe.wait_ge(v_done, ST * B)
                            pe.wait_ge(o_done, QUADS * b - 1 + h // 4)
                        else:
                            unit_read(b + 1, h - 1 if h < U else U - 2)
                        if h > 3:
                            weighted_sum(b, par, h // 4 - 1, h)
                        else:
                            weighted_sum(b - 1, 1 - par, QUADS - 1, h)
                    if started(n, 2):
                        transposes(n - 2, h - 2)

                for u in range(U):
                    unit(0, 0, u)
                pe.wait_ge(consts, 9)
                batches(pe, step)
                transposes(H * B - 2, H - 2)
                transposes(H * B - 1, H - 1)
                pe.wait_ge(o_done, QUADS * B - 2)
                weighted_sum(B - 1, 1, QUADS - 1, 3)


def phase_feed_forward(nc, sem, o_d, x1_d, wo, bo, w_gate, w_up, w_down, out):
    PIECES = 3 * KD
    with ExitStack() as ctx:
        def sb(name, shape, dt=F32):
            return ctx.enter_context(nc.sbuf_tensor("E_" + name, shape, dt))

        def psum(name):
            return ctx.enter_context(nc.psum_tensor("E_" + name, [P, 512], F32))

        with nc.sbuf_tensor("E_w_f32", [P, PIECES, F], F32) as w_f32:
            pass
        w_f32r = sb("w_f32r", [P, PIECES, F], F32R)
        with nc.sbuf_tensor("E_w_int", [P, 2, F], I32) as w_int:
            pass
        hs = Split(sb, "hidden", [P, KF, GT])
        wos = Split(sb, "wo", [P, KD, D])
        acts = Split(sb, "acts", [P, KD, GT])
        oraw = [sb(f"oraw{i}", [P, GT]) for i in range(2)]
        x2 = sb("x2", [P, TT, D])
        x1b = [sb(f"x1b{i}", [P, D]) for i in range(2)]
        bo_b = sb("bo_b", [P, D])
        gated = [sb(f"gated{i}", [P, HALF]) for i in range(2)]
        r = {n: sb("r_" + n, [P, D]) for n in "ab"}
        stats = {n: sb("stats_" + n, [P, 6]) for n in "ab"}
        mv = {n: sb("mv_" + n, [P, 2]) for n in "ab"}
        var_eps = {n: sb("var_eps_" + n, [P, 1]) for n in "ab"}
        rstd = {n: sb("rstd_" + n, [P, 1]) for n in "ab"}
        y = [sb(f"y{i}", [P, D]) for i in range(2)]
        minus_half, ident = sb("minus_half", [P, 1]), sb("ident", [P, P])
        biggest, biggest1, biggest_all = sb("biggest", [P, PIECES]), sb("biggest1", [P, 1]), sb("biggest_all", [P, 1])
        inexact = sb("inexact", [P, 1], I32)
        ps_g, ps_u = [psum(f"ps_g{i}") for i in range(2)], [psum(f"ps_u{i}") for i in range(2)]
        ps_t = [psum(f"ps_t{i}") for i in range(2)]
        ps_y, ps_d = psum("ps_y"), psum("ps_d")

        wo_loaded, wo_high, wo_low = sem("E_wo_loaded"), sem("E_wo_high"), sem("E_wo_low")
        int_loaded = [sem("E_int_loaded0"), sem("E_int_loaded1")]
        int_max, int_done = sem("E_int_max"), sem("E_int_done")
        all_max, flagged, again_loaded, w_ready = (sem("E_" + n) for n in
                                                   ("all_max", "flagged", "again_loaded", "w_ready"))
        b_loaded, consts = sem("E_b_loaded"), sem("E_consts")
        o_loaded = [sem("E_o_loaded0"), sem("E_o_loaded1")]
        o_high, o_low = sem("E_o_high"), sem("E_o_low")
        x1_loaded, x1b_done = [sem("E_x1_loaded0"), sem("E_x1_loaded1")], sem("E_x1b_done")
        y_done, t_done, th_done, tl_done = (sem("E_" + n) for n in ("y_done", "t_done", "th_done", "tl_done"))
        gu_done, silu_done, h_done, hh_done, hl_done = (sem("E_" + n) for n in
                                                        ("gu_done", "silu_done", "h_done", "hh_done", "hl_done"))
        d_done = sem("E_d_done")
        sum_done = {n: sem("E_sum_" + n) for n in "ab"}
        stat_done = {n: sem("E_stat_" + n) for n in "ab"}
        mv_done = {n: sem("E_mv_" + n) for n in "ab"}
        eps_done = {n: sem("E_eps_" + n) for n in "ab"}
        rstd_done = {n: sem("E_rstd_" + n) for n in "ab"}
        norm_done = {n: sem("E_norm_" + n) for n in "ab"}
        stored, passed = [sem("E_stored0"), sem("E_stored1")], sem("E_passed")
        HU = 2 * KF

        def slot_count(g, i):
            return (TT - i % 2 + 1) // 2 * g + i // 2

        def piece(n):
            if n < 2 * KD:
                return (w_gate, w_up)[n // KD][n % KD * P:(n % KD + 1) * P, :]
            k = (n - 2 * KD) * (KF // KD)
            return w_down[k * P:(k + KF // KD) * P, :].rearrange("(a p) n -> p a n", p=P)

        def place(t, n):
            return t[:, n, :] if n < 2 * KD else t[:, n, :].rearrange("p (a n) -> p a n", n=D)

        with nc.Block() as block:

            @block.sync
            def _(sp):
                o_rows = o_d.rearrange("(k p) t -> p k t", p=P)

                def load_o(g):
                    for k in range(KD):
                        wait(sp, o_low, KD * g + k - 1)
                        sp.dma_start(oraw[k % 2][:, :], o_rows[:, k, col(g * GT, GT)]).then_inc(o_loaded[k % 2], 16)

                def load_x1(g, i):
                    if i % 2 == 0 or later(g) or i > 1:
                        wait(sp, sum_done["a"], TT * g + i - (0 if i == 0 else 1))
                    src = x1_d.rearrange("(t p) n -> t p n", p=P)
                    n = TT * g + i
                    sp.dma_start(x1b[i % 2][:, :], src[n] if isinstance(n, int) else
                                 src[bass.ds(n, 1)].rearrange("a p n -> (a p) n")).then_inc(x1_loaded[i % 2], 16)

                def store(g, i):
                    n = TT * g + i
                    sp.wait_ge(norm_done["b"], n + 1)
                    dst = out.rearrange("(t p) n -> t p n", p=P)
                    sp.dma_start(dst[n] if isinstance(n, int) else
                                 dst[bass.ds(n, 1)].rearrange("a p n -> (a p) n"), y[i % 2][:, :])\
                      .then_inc(stored[i % 2], 16)

                sp.dma_start(x2[:, 0:KD, :], wo.rearrange("(k p) n -> p k n", p=P)).then_inc(wo_loaded, 16)
                sp.dma_start(bo_b[:, :], bo.rearrange("(a n) -> a n", a=1).broadcast_to([P, D])).then_inc(b_loaded, 16)
                load_o(0)
                load_x1(0, 0)
                load_x1(0, 1)
                for n in range(PIECES):
                    wait(sp, int_max, n - 1)
                    wait(sp, int_done, n - 1)
                    sp.dma_start(w_int[:, n % 2, :].rearrange("p (a n) -> p a n", n=D) if n >= 2 * KD else
                                 w_int[:, n % 2, :], piece(n)).then_inc(int_loaded[n % 2], 16)
                for i in range(2, TT):
                    load_x1(0, i)
                sp.wait_ge(flagged, 1)
                with sp.If(sp.value_load(inexact[0:1, 0:1], min_val=0, max_val=1) == 1):
                    for n in range(PIECES):
                        sp.wait_ge(int_done, PIECES + n)
                        sp.dma_start(w_int[:, 0, :].rearrange("p (a n) -> p a n", n=D) if n >= 2 * KD else
                                     w_int[:, 0, :], piece(n)).then_inc(again_loaded, 16)
                load_o(1)

                def tiles(g):
                    for i in range(TT):
                        load_x1(g + 1, i)
                        store(g, i)

                with sp.Fori(0, NG - 2) as g:
                    tiles(g)
                    load_o(g + 2)
                tiles(NG - 2)
                for i in range(TT):
                    store(NG - 1, i)
                sp.wait_ge(stored[0], 16 * ((TT + 1) // 2) * NG)
                sp.wait_ge(stored[1], 16 * (TT // 2) * NG)

            @block.gpsimd
            def _(pool):
                pool.memset(minus_half[:, :], -0.5).then_inc(consts, 1)
                pool.memset(ident[:, :], 0.0).then_inc(consts, 1)
                pool.wait_ge(consts, 2)
                pool.affine_select(out=ident[:, :], in_=ident[:, :], compare_op=ALU.not_equal, fill=1.0,
                                   base=0, pattern=[[-1, P]], channel_multiplier=1).then_inc(consts, 1)
                pool.wait_ge(b_loaded, 16)

                def low_o(g):
                    for k in range(KD):
                        n = KD * g + k
                        pool.wait_ge(o_high, n + 1)
                        pool.wait_ge(o_loaded[k % 2], 32 * g + 16 * (k // 2) + 16)
                        pool.tensor_tensor(acts[1][:, k, :], oraw[k % 2][:, :], acts[0][:, k, :].bitcast(F32),
                                           ALU.subtract).then_inc(o_low, 1)

                def add_bias(g, i):
                    pool.wait_ge(x1_loaded[i % 2], 16 * slot_count(g, i) + 16)
                    pool.tensor_tensor(x1b[i % 2][:, :], x1b[i % 2][:, :], bo_b[:, :], ALU.add).then_inc(x1b_done, 1)

                def rstd_of(name, n):
                    pool.wait_ge(eps_done[name], n + 1)
                    wait(pool, norm_done[name], n)
                    pool.tensor_tensor(rstd[name][:, :], var_eps[name][:, :], minus_half[:, :], ALU.pow)\
                        .then_inc(rstd_done[name], 1)

                def low_h(g):
                    for c in range(KF):
                        for h in range(2):
                            n = HU * g + 2 * c + h
                            pool.wait_ge(hh_done, n + 1)
                            pool.wait_ge(h_done, n + 1)
                            if c == 0 and h == 0:
                                wait(pool, d_done, TT * g)
                            cols = slice(h * HALF, (h + 1) * HALF)
                            pool.tensor_tensor(hs[1][:, c, cols], gated[h][:, :], hs[0][:, c, cols].bitcast(F32),
                                               ALU.subtract).then_inc(hl_done, 1)

                low_o(0)
                for i in range(TT):
                    add_bias(0, i)
                    rstd_of("a", i)
                pool.wait_ge(all_max, 1)
                pool.partition_all_reduce(biggest_all[:, :], biggest1[:, :], P, bass.bass_isa.ReduceOp.max)\
                    .then_inc(all_max, 1)
                with pool.Fori(0, NG - 1) as g:
                    low_h(g)
                    low_o(g + 1)
                    for i in range(TT):
                        add_bias(g + 1, i)
                        rstd_of("b", TT * g + i)
                        rstd_of("a", TT * (g + 1) + i)
                low_h(NG - 1)
                for i in range(TT):
                    rstd_of("b", TT * (NG - 1) + i)

            @block.scalar
            def _(act):
                def high_o(g):
                    for k in range(KD):
                        act.wait_ge(o_loaded[k % 2], 32 * g + 16 * (k // 2) + 16)
                        if k == 0 and later(g):
                            act.wait_ge(gu_done, HU * g)
                        act.activation(acts[0][:, k, :], oraw[k % 2][:, :], ACT.Copy).then_inc(o_high, 1)

                def high_x2(g):
                    for i in range(TT):
                        n = TT * g + i
                        act.wait_ge(t_done, n + 1)
                        act.activation(acts[0][:, :, i * P:(i + 1) * P],
                                       ps_t[i % 2][:, :].rearrange("p (k c) -> p k c", k=KD), ACT.Copy)\
                           .then_inc(th_done, 1)

                def silu_and_high(g):
                    def high(n, c, h):
                        act.wait_ge(h_done, n + 1)
                        act.activation(hs[0][:, c, h * HALF:(h + 1) * HALF], gated[h][:, :], ACT.Copy)\
                           .then_inc(hh_done, 1)

                    for c in range(KF):
                        for h in range(2):
                            n = HU * g + 2 * c + h
                            act.wait_ge(gu_done, n + 1)
                            wait(act, hl_done, n if c + h == 0 else n - 1)
                            if c == 0 and h == 1:
                                wait(act, d_done, TT * g)
                            act.activation(gated[h][:, :], ps_g[h][:, 0:HALF], ACT.Silu, scale=FSCALE)\
                               .then_inc(silu_done, 1)
                            if (c, h) != (0, 0):
                                high(n - 1, c if h else c - 1, 1 - h)
                    high(HU * g + HU - 1, KF - 1, 1)

                act.wait_ge(wo_loaded, 16)
                act.activation(wos[0][:, :, :], x2[:, 0:KD, :], ACT.Copy).then_inc(wo_high, 1)
                high_o(0)

                def convert(n, source, tile, ready):
                    act.wait_ge(*ready)
                    act.activation(place(tile, n), source.rearrange("p (a n) -> p a n", n=D) if n >= 2 * KD else source,
                                   ACT.Copy).then_inc(int_done, 1)

                for n in range(PIECES):
                    convert(n, w_int[:, n % 2, :], w_f32r, (int_loaded[n % 2], 16 * (n // 2) + 16))
                act.wait_ge(flagged, 1)
                act.wait_ge(int_done, PIECES)
                with act.If(act.value_load(inexact[0:1, 0:1], min_val=0, max_val=1) == 1):
                    for n in range(PIECES):
                        convert(n, w_int[:, 0, :], w_f32, (again_loaded, 16 * n + 16))
                    act.wait_ge(int_done, 2 * PIECES)
                act.sem_inc(w_ready, 1)
                with act.Fori(0, NG - 1) as g:
                    high_x2(g)
                    silu_and_high(g)
                    high_o(g + 1)
                high_x2(NG - 1)
                silu_and_high(NG - 1)

            @block.vector
            def _(dve):
                def add_and_stats(name, n, add):
                    wait(dve, norm_done[name], n)
                    add(r[name][:, :]).then_inc(sum_done[name], 1)
                    dve.wait_ge(sum_done[name], n + 1)
                    dve.bn_stats(stats[name][:, :], r[name][:, :]).then_inc(stat_done[name], 1)
                    wait_apart(dve, stat_done[name], n + 1, passed)
                    dve.bn_aggr(mv[name][:, :], stats[name][:, :]).then_inc(mv_done[name], 1)
                    dve.wait_ge(mv_done[name], n + 1)
                    dve.tensor_scalar(var_eps[name][:, :], mv[name][:, 1:2], EPS, None, ALU.add)\
                       .then_inc(eps_done[name], 1)

                def normalise(name, n, dst):
                    dve.wait_ge(rstd_done[name], n + 1)
                    dve.tensor_scalar(dst, r[name][:, :], mv[name][:, 0:1], rstd[name][:, 0:1],
                                      ALU.subtract, ALU.mult).then_inc(norm_done[name], 1)

                def second_sum(g, i):
                    n = TT * g + i
                    dve.wait_ge(y_done, n + 1)
                    dve.wait_ge(x1b_done, n + 1)
                    add_and_stats("a", n, lambda dst: dve.tensor_tensor(dst, ps_y[:, :], x1b[i % 2][:, :], ALU.add))

                def third_sum(g, i):
                    n = TT * g + i
                    dve.wait_ge(d_done, n + 1)
                    add_and_stats("b", n, lambda dst: dve.scalar_tensor_tensor(
                        dst, ps_d[:, :], FSCALE, x2[:, i, :], ALU.mult, ALU.add))

                def third_norm(g, i):
                    wait(dve, stored[i % 2], 16 * slot_count(g, i))
                    normalise("b", TT * g + i, y[i % 2][:, :])

                def low_x2(g):
                    for i in range(TT):
                        n = TT * g + i
                        dve.wait_ge(t_done, n + 1)
                        dve.wait_ge(th_done, n + 1)
                        dve.tensor_tensor(acts[1][:, :, i * P:(i + 1) * P],
                                          ps_t[i % 2][:, :].rearrange("p (k c) -> p k c", k=KD),
                                          acts[0][:, :, i * P:(i + 1) * P].bitcast(F32), ALU.subtract)\
                           .then_inc(tl_done, 1)

                def gate(g):
                    for c in range(KF):
                        for h in range(2):
                            n = HU * g + 2 * c + h
                            dve.wait_ge(gu_done, n + 1)
                            dve.wait_ge(silu_done, n + 1)
                            dve.scalar_tensor_tensor(gated[h][:, :], ps_u[h][:, 0:HALF], FSCALE, gated[h][:, :],
                                                     ALU.mult, ALU.mult).then_inc(h_done, 1)

                dve.wait_ge(wo_high, 1)
                dve.wait_ge(wo_loaded, 16)
                dve.tensor_tensor(wos[1][:, :, :], x2[:, 0:KD, :], wos[0][:, :, :].bitcast(F32), ALU.subtract)\
                   .then_inc(wo_low, 1)
                dve.wait_ge(wo_low, 1)
                for n in range(PIECES):
                    dve.wait_ge(int_loaded[n % 2], 16 * (n // 2) + 16)
                    dve.tensor_reduce(biggest[:, n:n + 1], w_int[:, n % 2, :], AX.X, ALU.max,
                                      apply_absolute_value=True).then_inc(int_max, 1)
                dve.wait_ge(int_max, PIECES)
                dve.tensor_reduce(biggest1[:, :], biggest[:, :], AX.X, ALU.max).then_inc(all_max, 1)
                for i in range(TT):
                    second_sum(0, i)
                    normalise("a", i, x2[:, i, :])
                dve.wait_ge(all_max, 2)
                dve.tensor_scalar(inexact[:, :], biggest_all[:, :], EXACT, None, ALU.is_gt).then_inc(flagged, 1)
                with dve.Fori(0, NG - 1) as g:
                    low_x2(g)
                    gate(g)
                    for i in range(TT):
                        third_sum(g, i)
                        second_sum(g + 1, i)
                        third_norm(g, i)
                        normalise("a", TT * (g + 1) + i, x2[:, i, :])
                low_x2(NG - 1)
                gate(NG - 1)
                for i in range(TT):
                    third_sum(NG - 1, i)
                    third_norm(NG - 1, i)

            @block.tensor
            def _(pe):
                def project_o(g, i):
                    n = TT * g + i
                    if i == 0:
                        pe.wait_ge(o_low, KD * (g + 1))
                    wait(pe, sum_done["a"], n)
                    products(pe, ps_y[:, :], SPLIT, KD, lambda a, k: acts[a][:, k, i * P:(i + 1) * P],
                             lambda a, k: wos[a][:, k, :]).then_inc(y_done, 1)

                def transpose_x2(g):
                    for i in range(TT):
                        n = TT * g + i
                        pe.wait_ge(norm_done["a"], n + 1)
                        wait(pe, tl_done, n if i == 0 else n - 1)
                        for k in range(KD):
                            last = pe.transpose(ps_t[i % 2][:, k * P:(k + 1) * P], x2[:, i, k * P:(k + 1) * P],
                                                ident[:, :])
                        last.then_inc(t_done, 1)

                def feed_forward(w, view):
                    both = ((0, 0), (0, 1))

                    def gate_and_up(g):
                        pe.wait_ge(tl_done, TT * (g + 1))
                        for c in range(KF):
                            for h in range(2):
                                n = HU * g + 2 * c + h
                                wait(pe, h_done, n if c + h == 0 else n - 1)
                                for ps, first in ((ps_g, 0), (ps_u, KD)):
                                    last = products(pe, ps[h][:, 0:HALF], both, KD,
                                                    lambda a, k: w[:, first + k, c * P:(c + 1) * P],
                                                    lambda a, k: view(acts[a][:, k, h * HALF:(h + 1) * HALF]))
                                last.then_inc(gu_done, 1)

                    def down(g, i):
                        n = TT * g + i
                        if i == 0:
                            pe.wait_ge(hl_done, HU * (g + 1))
                        wait(pe, sum_done["b"], n)
                        products(pe, ps_d[:, :], ((0, 0), (1, 0)), KF,
                                 lambda a, k: view(hs[a][:, k, i * P:(i + 1) * P]),
                                 lambda a, k: w[:, 2 * KD + k // 3, k % 3 * D:(k % 3 + 1) * D]).then_inc(d_done, 1)

                    with pe.Fori(0, NG - 1) as g:
                        transpose_x2(g)
                        gate_and_up(g)
                        for i in range(TT):
                            down(g, i)
                            project_o(g + 1, i)
                    transpose_x2(NG - 1)
                    gate_and_up(NG - 1)
                    for i in range(TT):
                        down(NG - 1, i)

                pe.wait_ge(wo_low, 1)
                pe.wait_ge(consts, 3)
                for i in range(TT):
                    project_o(0, i)
                pe.wait_ge(flagged, 1)
                pe.wait_ge(w_ready, 1)
                pe.wait_ge(int_done, PIECES)
                with pe.If(pe.value_load(inexact[0:1, 0:1], min_val=0, max_val=1) == 1):
                    feed_forward(w_f32, lambda x: x.bitcast(F32))
                with pe.Else():
                    feed_forward(w_f32r, lambda x: x)


def build_decoder(nc, x, xT, ctxT, a_wq, a_wk, a_wv, a_wo, a_bo, a_w, a_v,
                  x_wq, x_bq, x_wk, x_bk, x_wv, x_bv, x_wo, x_bo, w_gate, w_up, w_down, out):
    with ExitStack() as ctx:
        def sem(name):
            return ctx.enter_context(nc.semaphore(name))

        def dram(name, shape):
            return nc.dram_tensor(name, shape, F32, kind="Internal").ap()

        q_d, k_d, v_d = dram("self_q", [D, N]), dram("self_k", [D, N]), dram("self_v", [N, D])
        o_d, x1_d = dram("self_o", [D, N]), dram("x1", [N, D])
        cq_d, co_d = dram("cross_q", [2, D, N]), dram("cross_o", [D, N])
        phase_qkv(nc, sem, xT, a_wq, a_wk, a_wv, q_d, k_d, v_d)
        phase_self_attention(nc, sem, q_d, k_d, v_d, a_w, a_v, o_d)
        phase_norm_and_queries(nc, sem, o_d, x, a_wo, a_bo, x_wq, x_bq, x1_d, cq_d)
        phase_cross_attention(nc, sem, ctxT, cq_d, x_wk, x_bk, x_wv, x_bv, co_d)
        phase_feed_forward(nc, sem, co_d, x1_d, x_wo, x_bo, w_gate, w_up, w_down, out)


def kernel(x, ctx_1024, L0_attn_Wq, L0_attn_Wk, L0_attn_Wv, L0_attn_Wo, L0_attn_bo, L0_attn_w, L0_attn_v,
           L0_xattn_Wq, L0_xattn_bq, L0_xattn_Wk, L0_xattn_bk, L0_xattn_Wv, L0_xattn_bv, L0_xattn_Wo, L0_xattn_bo,
           L0_ffn_w_gate, L0_ffn_w_up, L0_ffn_w_down):
    import numpy as np
    import concourse.bacc as bacc
    from concourse.bass_utils import run_bass_kernel_spmd

    def columns(bias):
        return np.asarray(bias).reshape(KD, P).T

    tokens = np.asarray(x).reshape(N, D)
    given = {
        "x": tokens, "xT": tokens.T, "ctxT": np.asarray(ctx_1024).transpose(0, 2, 1),
        "a_wq": L0_attn_Wq, "a_wk": L0_attn_Wk, "a_wv": L0_attn_Wv, "a_wo": L0_attn_Wo, "a_bo": L0_attn_bo,
        "a_w": L0_attn_w, "a_v": L0_attn_v,
        "x_wq": np.asarray(L0_xattn_Wq).T, "x_bq": columns(L0_xattn_bq),
        "x_wk": np.asarray(L0_xattn_Wk).T, "x_bk": columns(L0_xattn_bk),
        "x_wv": np.asarray(L0_xattn_Wv).T, "x_bv": columns(L0_xattn_bv),
        "x_wo": np.asarray(L0_xattn_Wo).T, "x_bo": L0_xattn_bo,
        "w_gate": np.asarray(L0_ffn_w_gate).T, "w_up": np.asarray(L0_ffn_w_up).T,
        "w_down": np.asarray(L0_ffn_w_down).T,
    }
    nc = bacc.Bacc("TRN2", target_bir_lowering=False, num_devices=1)
    arrays, args = {}, {}
    for name, a in given.items():
        arrays["in_" + name] = np.ascontiguousarray(a)
        args[name] = nc.dram_tensor("in_" + name, arrays["in_" + name].shape,
                                    mybir.dt.from_np(arrays["in_" + name].dtype), kind="ExternalInput").ap()
    args["out"] = nc.dram_tensor("out_0", [N, D], F32, kind="ExternalOutput").ap()
    build_decoder(nc, **args)
    r = run_bass_kernel_spmd(nc, [arrays], core_ids=[0])
    return r.results[0]["out_0"].reshape(B, T, D)
```

```python
from contextlib import ExitStack

import concourse.bass as bass
from concourse import mybir

B, T, S, D, H = 32, 100, 722, 512, 16
HD = D // H
F = 1536
P = 128
KD = D // P
KF = F // P
N = B * T
GT = 640
NG = N // GT
TT = GT // P
HALF = GT // 2
QUADS = H // 4
QT = 4 * T
EPS = 1e-5
FSCALE = 1.0 / 127.0
ISQ = float(HD) ** -0.5
EXACT = 4096.0
MASKED = -3.0e38

F32 = mybir.dt.float32
F32R = mybir.dt.float32r
I32 = mybir.dt.int32
ALU = mybir.AluOpType
ACT = mybir.ActivationFunctionType
AX = mybir.AxisListType


def wait(eng, sem, value):
    if isinstance(value, int) and value <= 0:
        return
    eng.wait_ge(sem, value)


def wait_apart(eng, sem, value, passed):
    wait(eng, sem, value)
    eng.sem_inc(passed, 1)


def later(g):
    return not isinstance(g, int) or g > 0


def col(base, width):
    return slice(base, base + width) if isinstance(base, int) else bass.ds(base, width)


def products(pe, out, terms, chunks, lhs, rhs):
    last = None
    for k in range(chunks):
        for n, (a, b) in enumerate(terms):
            last = pe.matmul(out, lhs(a, k), rhs(b, k),
                             start=(k == 0 and n == 0), stop=(k == chunks - 1 and n == len(terms) - 1))
    return last


SPLIT = ((0, 0), (0, 1), (1, 0))


class Split:

    def __init__(self, sb, name, shape):
        self.parts = [sb(name + "_high", shape, F32R), sb(name + "_low", shape, F32R)]

    def __getitem__(self, part):
        return self.parts[part]


def split_weights(raws, targets, staging, sem_loaded, sem_high, sem_low):

    every = range(len(raws))

    def load(sp, which=every):
        for n in which:
            wait(sp, sem_high, n - 1)
            wait(sp, sem_low, n - 1)
            sp.dma_start(staging[n % 2], raws[n]).then_inc(sem_loaded[n % 2], 16)

    def high(act, which=every):
        for n in which:
            wait(act, sem_loaded[n % 2], 16 * (n // 2 + 1))
            act.activation(targets[n][0][:, :, :], staging[n % 2], ACT.Copy).then_inc(sem_high, 1)

    def low(dve, which=every):
        for n in which:
            t = targets[n]
            wait(dve, sem_high, n + 1)
            wait(dve, sem_loaded[n % 2], 16 * (n // 2 + 1))
            dve.tensor_tensor(t[1][:, :, :], staging[n % 2], t[0][:, :, :].bitcast(F32),
                              ALU.subtract).then_inc(sem_low, 1)

    return load, high, low


def phase_qkv(nc, sem, xT, wq, wk, wv, q_d, k_d, v_d):
    UNITS = 2 * KD * 2 + TT
    RING = 7
    assert UNITS % RING == 0
    with ExitStack() as ctx:
        def sb(name, shape, dt=F32):
            return ctx.enter_context(nc.sbuf_tensor("A_" + name, shape, dt))

        W = [Split(sb, n, [P, KD, D]) for n in ("wq", "wk", "wv")]
        staging = [sb(f"wstage{i}", [P, KD, D]) for i in range(2)]
        xraw = sb("xraw", [P, KD, GT])
        xs = [Split(sb, f"x{i}", [P, KD, GT]) for i in range(2)]
        qk = [[sb(f"{n}{i}", [P, KD, GT]) for n in "qk"] for i in range(2)]
        vo = [sb(f"v{i}", [P, TT, D]) for i in range(2)]
        ps = [ctx.enter_context(nc.psum_tensor(f"A_ps{i}", [P, 512], F32)) for i in range(RING)]

        w_loaded = [sem("A_w_loaded0"), sem("A_w_loaded1")]
        w_high, w_low = sem("A_w_high"), sem("A_w_low")
        x_loaded, x_high, x_low = sem("A_x_loaded"), sem("A_x_high"), sem("A_x_low")
        unit_done, passed = sem("A_unit_done"), sem("A_passed")
        act_out, dve_out = sem("A_act_out"), sem("A_dve_out")
        stored = [sem("A_stored0"), sem("A_stored1")]

        def of_act(u):
            return u % 2 == 0

        ACTS = sum(of_act(u) for u in range(UNITS))
        DVES = UNITS - ACTS

        def count(u):
            return sum(of_act(v) == of_act(u) for v in range(u + 1))

        def wait_out(eng, g, u):
            if u < 0:
                if isinstance(g, int):
                    return
                g, u = g - 1, u + UNITS
            eng.wait_ge(act_out if of_act(u) else dve_out, g * (ACTS if of_act(u) else DVES) + count(u))

        def groups(eng, body):
            body(0, 0)
            with eng.Fori(0, (NG - 1) // 2) as i:
                for k in range(2):
                    body(2 * i + (1 + k), (1 + k) % 2)

        def unit_out(u, par):
            if u < 16:
                w, m, h = u // 8, u // 2 % 4, u % 2
                return qk[par][w][:, m, h * HALF:(h + 1) * HALF], ps[u % RING][:, 0:HALF]
            return vo[par][:, u - 16, :], ps[u % RING][:, 0:D]

        with nc.Block() as block:
            load_w, high_w, low_w = split_weights(
                [w.rearrange("(k p) n -> p k n", p=P) for w in (wq, wk, wv)], W,
                [s[:, :, :] for s in staging], w_loaded, w_high, w_low)

            @block.sync
            def _(sp):
                x_cols = xT.rearrange("(k p) t -> p k t", p=P)

                def load_x(g):
                    sp.dma_start(xraw[:, :, :], x_cols[:, :, col(g * GT, GT)]).then_inc(x_loaded, 16)

                def store(g, par):
                    wait_apart(sp, act_out, (g + 1) * ACTS, passed)
                    wait_apart(sp, dve_out, (g + 1) * DVES, passed)
                    for n, dst in ((0, q_d), (1, k_d)):
                        sp.dma_start(dst.rearrange("(m p) t -> p m t", p=P)[:, :, col(g * GT, GT)],
                                     qk[par][n][:, :, :]).then_inc(stored[par], 16)
                    sp.dma_start(v_d[col(g * GT, GT), :].rearrange("(i p) n -> p i n", p=P), vo[par][:, :, :])\
                      .then_inc(stored[par], 16)

                load_x(0)
                load_w(sp)

                def body(g, par):
                    if isinstance(g, int):
                        return
                    sp.wait_ge(x_low, g)
                    load_x(g)
                    store(g - 1, 1 - par)

                groups(sp, body)
                store(NG - 1, (NG - 1) % 2)
                sp.wait_ge(stored[0], 48 * ((NG + 1) // 2))
                sp.wait_ge(stored[1], 48 * (NG // 2))

            @block.gpsimd
            def _(pool):
                def body(g, par):
                    pool.wait_ge(x_loaded, 16 * g + 16)
                    wait_apart(pool, unit_done, (g - 1) * UNITS, passed)
                    pool.tensor_copy(xs[par][0][:, :, :], xraw[:, :, :]).then_inc(x_high, 1)
                    pool.wait_ge(x_high, g + 1)
                    pool.tensor_tensor(xs[par][1][:, :, :], xraw[:, :, :], xs[par][0][:, :, :].bitcast(F32),
                                       ALU.subtract).then_inc(x_low, 1)

                groups(pool, body)

            @block.scalar
            def _(act):
                high_w(act)

                def body(g, par):
                    if later(g):
                        act.wait_ge(stored[par], 24 * (g - par))
                    for u in range(0, UNITS, 2):
                        dst, src = unit_out(u, par)
                        act.wait_ge(unit_done, g * UNITS + u + 1)
                        act.activation(dst, src, ACT.Copy).then_inc(act_out, 1)

                groups(act, body)

            @block.vector
            def _(dve):
                low_w(dve)

                def body(g, par):
                    if later(g):
                        dve.wait_ge(stored[par], 24 * (g - par))
                    for u in range(1, UNITS, 2):
                        dst, src = unit_out(u, par)
                        dve.wait_ge(unit_done, g * UNITS + u + 1)
                        dve.tensor_copy(dst, src).then_inc(dve_out, 1)

                groups(dve, body)

            @block.tensor
            def _(pe):
                def body(g, par):
                    pe.wait_ge(x_low, g + 1)
                    for u in range(UNITS):
                        wait_out(pe, g, u - RING)
                        if isinstance(g, int):
                            pe.wait_ge(w_low, min(u // 8, 2) + 1)
                        x = xs[par]
                        if u < 16:
                            w, m, h = u // 8, u // 2 % 4, u % 2
                            last = products(pe, ps[u % RING][:, 0:HALF], SPLIT, KD,
                                            lambda a, k: W[w][a][:, k, m * P:(m + 1) * P],
                                            lambda b, k: x[b][:, k, h * HALF:(h + 1) * HALF])
                        else:
                            i = u - 16
                            last = products(pe, ps[u % RING][:, 0:D], SPLIT, KD,
                                            lambda a, k: x[a][:, k, i * P:(i + 1) * P],
                                            lambda b, k: W[2][b][:, k, :])
                        last.then_inc(unit_done, 1)

                groups(pe, body)


def phase_self_attention(nc, sem, q_d, k_d, v_d, w, v, o_d):
    PAIRS = B // 2
    PQ = 2 * QUADS
    STEPS = 2 * PQ
    with ExitStack() as ctx:
        def sb(name, shape, dt=F32):
            return ctx.enter_context(nc.sbuf_tensor("B_" + name, shape, dt))

        def psum(name):
            return ctx.enter_context(nc.psum_tensor("B_" + name, [P, 512], F32))

        qs = [sb(f"q{i}", [P, QUADS, 2, T]) for i in range(2)]
        kd = [sb(f"kdiag{i}", [P, QUADS, 4, 2, T]) for i in range(2)]
        vs = [sb(f"v{i}", [T, 2, D]) for i in range(2)]
        rhat = sb("rhat", [T, H, T])
        masked = sb("masked", [T, T])
        keep = sb("keep", [T, T])
        dist_i = sb("dist_i", [T, T], I32)
        dist = sb("dist", [T, T])
        arg = sb("arg", [T, H, T])
        wb, vb, neg_w, ev = (sb(n, [T, H]) for n in ("wb", "vb", "neg_w", "ev"))
        ident = sb("ident", [P, P])
        s_rel = [sb(f"s_rel{i}", [T, 4, T]) for i in range(2)]
        s_msk = [sb(f"s_msk{i}", [T, 4, T]) for i in range(2)]
        e = [sb(f"e{i}", [T, 4, T]) for i in range(4)]
        pn = [sb(f"pn{i}", [T, 4, T]) for i in range(2)]
        pT = [sb(f"pT{i}", [T, 4, T]) for i in range(2)]
        neg_max = sb("neg_max", [T, 4, 4])
        rowsum = sb("rowsum", [T, 4, 4])
        inv = sb("inv", [T, 4, 4])
        oo = [sb(f"o{i}", [P, 2, QUADS, 2, T]) for i in range(2)]
        ps_s = [psum(f"ps_s{i}") for i in range(2)]
        ps_t = [psum(f"ps_t{i}") for i in range(2)]
        ps_o = [psum(f"ps_o{i}") for i in range(2)]

        wv_loaded, consts, zeroed = sem("B_wv_loaded"), sem("B_consts"), sem("B_zeroed")
        table = sem("B_table")
        table_exp = sem("B_table_exp")
        qk_loaded = [sem("B_qk_loaded0"), sem("B_qk_loaded1")]
        v_loaded = [sem("B_v_loaded0"), sem("B_v_loaded1")]
        s_done, rel_done, max_done, msk_done = sem("B_s_done"), sem("B_rel_done"), sem("B_max_done"), sem("B_msk_done")
        exp_done, inv_done, norm_done = sem("B_exp_done"), sem("B_inv_done"), sem("B_norm_done")
        t_done, pT_done, pv_done, o_done = sem("B_t_done"), sem("B_pT_done"), sem("B_pv_done"), sem("B_o_done")
        stored, passed = [sem("B_stored0"), sem("B_stored1")], sem("B_passed")

        def quads(eng, step):
            for k in range(2):
                for j in range(PQ):
                    step(k, k, PQ * k + j, PQ * k + j)
            with eng.Fori(1, PAIRS // 2) as i:
                for k in range(2):
                    for j in range(PQ):
                        step(2 * i + k, k, PQ * (2 * i + k) + j, PQ * k + j)

        def place(s):
            return s // PQ % 2, s // QUADS % 2, s % QUADS

        def started(n, back):
            return not (isinstance(n, int) and n < back)

        with nc.Block() as block:

            @block.sync
            def _(sp):
                sp.dma_start(wb[:, :], w.rearrange("(a h) -> a h", a=1).broadcast_to([T, H])).then_inc(wv_loaded, 16)
                sp.dma_start(vb[:, :], v.rearrange("(a h) -> a h", a=1).broadcast_to([T, H])).then_inc(wv_loaded, 16)
                q_rows = q_d.rearrange("(m p) t -> p m t", p=P)
                k_rows = k_d.rearrange("(m p) t -> p m t", p=P)
                o_rows = o_d.rearrange("(m p) t -> p m t", p=P)

                def of_pair(rows, p):
                    return rows[:, :, col(p * 2 * T, 2 * T)]

                def flat(buf):
                    return buf.rearrange("p m b t -> p m (b t)")

                def load_qk(p, par):
                    sp.dma_start(flat(qs[par][:, :, :, :]), of_pair(q_rows, p)).then_inc(qk_loaded[par], 16)
                    for j in range(4):
                        rows = slice(HD * j, HD * (j + 1))
                        sp.dma_start(flat(kd[par][rows, :, j, :, :]), of_pair(k_rows[rows, :, :], p))\
                          .then_inc(qk_loaded[par], 16)

                def load_v(p, par):
                    sp.dma_start(vs[par][:, :, :], v_d[col(p * 2 * T, 2 * T), :].rearrange("(b t) n -> t b n", b=2))\
                      .then_inc(v_loaded[par], 16)

                def store(p, par):
                    wait_apart(sp, o_done, PQ * (p + 1), passed)
                    for r in range(4):
                        rows = slice(HD * r, HD * (r + 1))
                        sp.dma_start(of_pair(o_rows[rows, :, :], p), flat(oo[par][rows, r % 2, :, :, :]))\
                          .then_inc(stored[par], 16)

                sp.wait_ge(zeroed, 2)
                for p in range(2):
                    load_qk(p, p)
                    load_v(p, p)
                with sp.Fori(0, PAIRS // 2 - 1) as i:
                    for k in range(2):
                        p = 2 * i + k
                        sp.wait_ge(s_done, PQ * (p + 1))
                        load_qk(p + 2, k)
                        sp.wait_ge(pv_done, PQ * (p + 1))
                        load_v(p + 2, k)
                        store(p, k)
                for p in (PAIRS - 2, PAIRS - 1):
                    store(p, p % 2)
                for par in range(2):
                    sp.wait_ge(stored[par], 64 * (PAIRS // 2))

            @block.gpsimd
            def _(pool):
                for i in range(2):
                    pool.memset(kd[i][:, :, :, :, :], 0.0).then_inc(zeroed, 1)
                pool.iota(dist_i[:, :], [[-1, T]], base=0, channel_multiplier=1).then_inc(consts, 1)
                pool.memset(keep[:, :], ISQ).then_inc(consts, 1)
                pool.memset(masked[:, :], 0.0).then_inc(consts, 1)
                pool.memset(ident[:, :], 0.0).then_inc(consts, 1)
                pool.wait_ge(consts, 4)
                pool.affine_select(out=keep[:, :], in_=keep[:, :], compare_op=ALU.is_ge, fill=0.0,
                                   base=0, pattern=[[-1, T]], channel_multiplier=1).then_inc(consts, 1)
                pool.affine_select(out=masked[:, :], in_=masked[:, :], compare_op=ALU.is_ge, fill=MASKED,
                                   base=0, pattern=[[-1, T]], channel_multiplier=1).then_inc(consts, 1)
                pool.affine_select(out=ident[:, :], in_=ident[:, :], compare_op=ALU.not_equal, fill=1.0,
                                   base=0, pattern=[[-1, P]], channel_multiplier=1).then_inc(consts, 1)
                pool.wait_ge(consts, 7)

                def add_mask(n, s):
                    pool.wait_ge(rel_done, n + 1)
                    wait(pool, exp_done, 4 * n - 4)
                    pool.tensor_tensor(s_msk[s % 2][:, :, :], s_rel[s % 2][:, :, :],
                                       masked[:, :].unsqueeze(1).broadcast_to([T, 4, T]), ALU.add).then_inc(msk_done, 1)

                def normalise(n, s):
                    pool.wait_ge(inv_done, n + 1)
                    pool.wait_ge(exp_done, 4 * n + 4)
                    wait(pool, t_done, n - 1)
                    pool.tensor_tensor(pn[s % 2][:, :, :], e[s % 4][:, :, :],
                                       inv[:, s % 4, :].unsqueeze(2).broadcast_to([T, 4, T]), ALU.mult)\
                        .then_inc(norm_done, 1)

                def step(p, par, n, s):
                    add_mask(n, s)
                    if started(n, 2):
                        normalise(n - 2, s - 2)

                quads(pool, step)
                for back in (2, 1):
                    normalise(QUADS * B - back, STEPS - back)

            LAG = 6

            @block.scalar
            def _(act):
                act.wait_ge(wv_loaded, 32)
                act.activation(ev[:, :], vb[:, :], ACT.Exp).then_inc(table_exp, 1)
                act.wait_ge(table, 5)
                act.activation(arg[:, :, :], arg[:, :, :], ACT.Exp).then_inc(table_exp, 1)

                def exps(n, s):
                    act.wait_ge(msk_done, n + 1)
                    act.wait_ge(max_done, n + 1)
                    wait(act, norm_done, n - 3)
                    for j in range(4):
                        act.activation(e[s % 4][:, j, :], s_msk[s % 2][:, j, :], ACT.Exp,
                                       bias=neg_max[:, s % 4, j:j + 1],
                                       accum_out=rowsum[:, s % 4, j:j + 1]).then_inc(exp_done, 1)

                def take_result(p, n, s):
                    par, b, m = place(s)
                    act.wait_ge(pv_done, n + 1)
                    if s % PQ == 0 and not (isinstance(p, int) and p < 2):
                        act.wait_ge(stored[par], 32 * (p - par))
                    act.activation(oo[par][:, :, m, b, :], ps_o[m % 2][:, 0:2 * T].rearrange("p (a t) -> p a t", a=2),
                                   ACT.Copy).then_inc(o_done, 1)

                def step(p, par, n, s):
                    if started(n, LAG):
                        take_result(p if s % PQ >= LAG else p - 1, n - LAG, (s - LAG) % STEPS)
                    exps(n, s)

                quads(act, step)
                for back in range(LAG, 0, -1):
                    take_result(PAIRS - 1, QUADS * B - back, STEPS - back)

            @block.vector
            def _(dve):
                dve.wait_ge(wv_loaded, 32)
                dve.wait_ge(consts, 7)
                dve.tensor_scalar(neg_w[:, :], wb[:, :], -1.0, None, ALU.mult).then_inc(table, 1)
                dve.tensor_scalar(dist[:, :], dist_i[:, :], 0.0, None, ALU.max).then_inc(table, 1)
                dve.wait_ge(table, 2)
                for h in range(H):
                    last = dve.tensor_scalar(arg[:, h, :], dist[:, :], neg_w[:, h:h + 1], vb[:, h:h + 1],
                                             ALU.mult, ALU.add)
                last.then_inc(table, 3)
                dve.wait_ge(table_exp, 2)
                dve.tensor_scalar(arg[:, :, :], arg[:, :, :], 1.0, None, ALU.add).then_inc(table, 1)
                dve.tensor_scalar(ev[:, :], ev[:, :], 1.0, None, ALU.add).then_inc(table, 1)
                dve.wait_ge(table, 7)
                dve.reciprocal(rhat[:, :, :], arg[:, :, :]).then_inc(table, 1)
                dve.wait_ge(table, 8)
                dve.tensor_tensor(rhat[:, :, :], rhat[:, :, :], ev[:, :].unsqueeze(2).broadcast_to([T, H, T]),
                                  ALU.mult).then_inc(table, 1)
                dve.wait_ge(table, 9)
                dve.tensor_tensor(rhat[:, :, :], rhat[:, :, :], keep[:, :].unsqueeze(1).broadcast_to([T, H, T]),
                                  ALU.mult).then_inc(table, 1)
                dve.wait_ge(table, 10)

                def scale_max(n, s, m):
                    dve.wait_ge(s_done, n + 1)
                    wait(dve, msk_done, n - 1)
                    dve.scalar_tensor_tensor(
                        s_rel[s % 2][:, :, :], ps_s[s % 2][0:T, 0:QT].rearrange("p (j t) -> p j t", j=4), 0.0,
                        rhat[:, 4 * m:4 * m + 4, :], ALU.max, ALU.mult).then_inc(rel_done, 1)
                    dve.wait_ge(rel_done, n + 1)
                    wait(dve, exp_done, 4 * n - 12)
                    dve.tensor_reduce(neg_max[:, s % 4, :], s_rel[s % 2][:, :, :], AX.X, ALU.max, negate=True)\
                        .then_inc(max_done, 1)

                def invert(n, s):
                    dve.wait_ge(exp_done, 4 * n + 4)
                    wait(dve, norm_done, n - 3)
                    dve.reciprocal(inv[:, s % 4, :], rowsum[:, s % 4, :]).then_inc(inv_done, 1)

                def take_transposed(n, s):
                    dve.wait_ge(t_done, n + 1)
                    wait(dve, pv_done, n - 1)
                    dve.tensor_copy(pT[s % 2][:, :, :], ps_t[s % 2][0:T, 0:QT].rearrange("p (j t) -> p j t", j=4))\
                       .then_inc(pT_done, 1)

                def step(p, par, n, s):
                    if started(n, 5):
                        take_transposed(n - 5, s - 5)
                    scale_max(n, s, s % QUADS)
                    if started(n, 2):
                        invert(n - 2, s - 2)

                quads(dve, step)
                end = QUADS * B
                for back in range(5, 0, -1):
                    if back <= 2:
                        invert(end - back, STEPS - back)
                    take_transposed(end - back, STEPS - back)

            @block.tensor
            def _(pe):
                pe.wait_ge(consts, 7)

                def scores(p, par, n, s):
                    _, b, m = place(s)
                    if s % PQ == 0:
                        pe.wait_ge(qk_loaded[par], 40 * (p - par) + 80)
                    wait(pe, rel_done, n - 1)
                    pe.matmul(ps_s[s % 2][0:T, 0:QT], qs[par][:, m, b, :], kd[par][:, m, :, b, :],
                              start=True, stop=True).then_inc(s_done, 1)

                def transposes(n, s):
                    pe.wait_ge(norm_done, n + 1)
                    wait(pe, pT_done, n - 1)
                    for j in range(4):
                        last = pe.transpose(ps_t[s % 2][0:T, j * T:(j + 1) * T], pn[s % 2][:, j, :], ident[0:T, 0:T])
                    last.then_inc(t_done, 1)

                def weighted_sum(p, n, s):
                    par, b, m = place(s)
                    if s % PQ == 0:
                        pe.wait_ge(v_loaded[par], 8 * (p - par) + 16)
                    pe.wait_ge(pT_done, n + 1)
                    wait(pe, o_done, n - 1)
                    for g in range(2):
                        c = (2 * m + g) * 2 * HD
                        last = pe.matmul(ps_o[m % 2][2 * HD * g:2 * HD * (g + 1), 0:2 * T], vs[par][:, b, c:c + 2 * HD],
                                         pT[s % 2][:, 2 * g:2 * g + 2, :], start=True, stop=True,
                                         tile_position=(0, 2 * HD * g))
                    last.then_inc(pv_done, 1)

                def step(p, par, n, s):
                    scores(p, par, n, s)
                    if started(n, 4):
                        transposes(n - 4, s - 4)
                    if started(n, 5):
                        weighted_sum(p if s % PQ >= 5 else p - 1, n - 5, (s - 5) % STEPS)

                quads(pe, step)
                end = QUADS * B
                for back in range(5, 0, -1):
                    if back <= 4:
                        transposes(end - back, STEPS - back)
                    weighted_sum(PAIRS - 1, end - back, STEPS - back)


def phase_norm_and_queries(nc, sem, o_d, x, wo, bo, wq, bq, x1_d, cq_d):
    QU = KD * 2
    with ExitStack() as ctx:
        def sb(name, shape, dt=F32):
            return ctx.enter_context(nc.sbuf_tensor("C_" + name, shape, dt))

        def psum(name):
            return ctx.enter_context(nc.psum_tensor("C_" + name, [P, 512], F32))

        W = [Split(sb, n, [P, KD, D]) for n in ("wo", "wq")]
        staging = [sb(f"wstage{i}", [P, KD, D]) for i in range(2)]
        bo_b, bq_c = sb("bo_b", [P, D]), sb("bq_c", [P, KD])
        oraw, os = sb("oraw", [P, KD, GT]), Split(sb, "o", [P, KD, GT])
        xb = sb("xb", [P, TT, D])
        r = [sb(f"r{i}", [P, D]) for i in range(2)]
        stats = [sb(f"stats{i}", [P, 6]) for i in range(2)]
        mv = [sb(f"mv{i}", [P, 2]) for i in range(2)]
        var_eps = [sb(f"var_eps{i}", [P, 1]) for i in range(2)]
        rstd = [sb(f"rstd{i}", [P, 1]) for i in range(2)]
        minus_half = sb("minus_half", [P, 1])
        x1 = sb("x1", [P, TT, D])
        x1s = Split(sb, "x1s", [P, KD, GT])
        qf = [sb(f"qf{i}", [P, HALF]) for i in range(4)]
        qo = Split(sb, "qo", [P, KD, GT])
        ident = sb("ident", [P, P])
        ps_y = [psum(f"ps_y{i}") for i in range(2)]
        ps_t = [psum(f"ps_t{i}") for i in range(2)]
        ps_q = [psum(f"ps_q{i}") for i in range(4)]

        w_loaded = [sem("C_w_loaded0"), sem("C_w_loaded1")]
        w_high, w_low = sem("C_w_high"), sem("C_w_low")
        b_loaded, consts = sem("C_b_loaded"), sem("C_consts")
        o_loaded, o_high, o_low = sem("C_o_loaded"), sem("C_o_high"), sem("C_o_low")
        x_loaded, xb_done = sem("C_x_loaded"), sem("C_xb_done")
        y_done, r_done, stat_done, mv_done, eps_done = (sem("C_" + n) for n in
                                                        ("y_done", "r_done", "stat_done", "mv_done", "eps_done"))
        rstd_done, x1_done, x1_stored = sem("C_rstd_done"), sem("C_x1_done"), sem("C_x1_stored")
        t_done, th_done, tl_done = sem("C_t_done"), sem("C_th_done"), sem("C_tl_done")
        q_done, qf_done, qh_done, ql_done = sem("C_q_done"), sem("C_qf_done"), sem("C_qh_done"), sem("C_ql_done")
        q_stored, passed = sem("C_q_stored"), sem("C_passed")

        def former(n, i):
            return n if i == 0 else n - 1

        with nc.Block() as block:
            load_w, high_w, low_w = split_weights(
                [w.rearrange("(k p) n -> p k n", p=P) for w in (wo, wq)], W,
                [s[:, :, :] for s in staging], w_loaded, w_high, w_low)

            @block.sync
            def _(sp):
                def load_o(g):
                    if later(g):
                        sp.wait_ge(o_low, KD * g)
                    sp.dma_start(oraw[:, :, :], o_d.rearrange("(k p) t -> p k t", p=P)[:, :, col(g * GT, GT)])\
                      .then_inc(o_loaded, 16)

                def load_x(g):
                    if later(g):
                        sp.wait_ge(r_done, TT * g)
                    sp.dma_start(xb[:, :, :], x[col(g * GT, GT), :].rearrange("(i p) n -> p i n", p=P))\
                      .then_inc(x_loaded, 16)

                def store(g):
                    wait_apart(sp, x1_done, TT * (g + 1), passed)
                    sp.dma_start(x1_d[col(g * GT, GT), :].rearrange("(i p) n -> p i n", p=P), x1[:, :, :])\
                      .then_inc(x1_stored, 16)

                def store_q(g):
                    wait_apart(sp, ql_done, QU * (g + 1), passed)
                    wait_apart(sp, qh_done, QU * (g + 1), passed)
                    for part in range(2):
                        sp.dma_start(cq_d[part].rearrange("(m p) t -> p m t", p=P)[:, :, col(g * GT, GT)],
                                     qo[part][:, :, :].bitcast(F32)).then_inc(q_stored, 16)

                load_o(0)
                load_w(sp, [0])
                load_x(0)
                sp.dma_start(bo_b[:, :], bo.rearrange("(a n) -> a n", a=1).broadcast_to([P, D])).then_inc(b_loaded, 16)
                sp.dma_start(bq_c[:, :], bq).then_inc(b_loaded, 16)
                load_w(sp, [1])
                load_o(1)
                store(0)
                load_x(1)
                load_o(2)

                def body(g, ahead_x=True, ahead_o=True):
                    store(g + 1)
                    if ahead_x:
                        load_x(g + 2)
                    if ahead_o:
                        load_o(g + 3)
                    store_q(g)

                with sp.Fori(0, NG - 3) as g:
                    body(g)
                body(NG - 3, ahead_o=False)
                body(NG - 2, ahead_x=False, ahead_o=False)
                store_q(NG - 1)
                sp.wait_ge(x1_stored, 16 * NG)
                sp.wait_ge(q_stored, 32 * NG)

            @block.gpsimd
            def _(pool):
                pool.memset(minus_half[:, :], -0.5).then_inc(consts, 1)
                pool.memset(ident[:, :], 0.0).then_inc(consts, 1)
                pool.wait_ge(consts, 2)
                pool.affine_select(out=ident[:, :], in_=ident[:, :], compare_op=ALU.not_equal, fill=1.0,
                                   base=0, pattern=[[-1, P]], channel_multiplier=1).then_inc(consts, 1)
                pool.wait_ge(b_loaded, 32)

                def low_o(g, k):
                    if k == 0:
                        pool.wait_ge(o_high, g + 1)
                        pool.wait_ge(o_loaded, 16 * g + 16)
                        if later(g):
                            pool.wait_ge(y_done, TT * g)
                    pool.tensor_tensor(os[1][:, k, :], oraw[:, k, :], os[0][:, k, :].bitcast(F32),
                                       ALU.subtract).then_inc(o_low, 1)

                def norms(g):
                    for i in range(TT):
                        n, s = TT * g + i, i % 2
                        if i == 0:
                            pool.wait_ge(x_loaded, 16 * g + 16)
                        pool.tensor_tensor(xb[:, i, :], xb[:, i, :], bo_b[:, :], ALU.add).then_inc(xb_done, 1)
                        pool.wait_ge(eps_done, n + 1)
                        wait(pool, x1_done, former(n, i))
                        pool.tensor_tensor(rstd[s][:, :], var_eps[s][:, :], minus_half[:, :], ALU.pow)\
                            .then_inc(rstd_done, 1)

                def low_q(g, u):
                    n = QU * g + u
                    pool.wait_ge(qh_done, n + 1)
                    pool.wait_ge(qf_done, n + 1)
                    if later(g) and u == 0:
                        pool.wait_ge(q_stored, 32 * g)
                    pool.tensor_tensor(qo[1][:, u // 2, u % 2 * HALF:(u % 2 + 1) * HALF], qf[u % 4][:, :],
                                       qo[0][:, u // 2, u % 2 * HALF:(u % 2 + 1) * HALF].bitcast(F32),
                                       ALU.subtract).then_inc(ql_done, 1)

                def body(g, ahead=True):
                    norms(g + 1)
                    for u in range(QU):
                        low_q(g, u)
                        if ahead and u % 2 == 0:
                            low_o(g + 2, u // 2)

                for k in range(KD):
                    low_o(0, k)
                norms(0)
                for k in range(KD):
                    low_o(1, k)
                body(0)
                with pool.Fori(1, NG - 2) as g:
                    body(g)
                body(NG - 2, ahead=False)
                for u in range(QU):
                    low_q(NG - 1, u)

            @block.scalar
            def _(act):
                def high_o(g):
                    act.wait_ge(o_loaded, 16 * g + 16)
                    if later(g):
                        act.wait_ge(y_done, TT * g)
                    act.activation(os[0][:, :, :], oraw[:, :, :], ACT.Copy).then_inc(o_high, 1)

                def high_x1(g):
                    for i in range(TT):
                        n = TT * g + i
                        act.wait_ge(t_done, n + 1)
                        if later(g) and i == 0:
                            act.wait_ge(q_done, QU * g)
                        act.activation(x1s[0][:, :, i * P:(i + 1) * P],
                                       ps_t[i % 2][:, :].rearrange("p (k c) -> p k c", k=KD), ACT.Copy)\
                           .then_inc(th_done, 1)

                def high_q(g):
                    for u in range(QU):
                        act.wait_ge(qf_done, QU * g + u + 1)
                        if later(g) and u == 0:
                            act.wait_ge(q_stored, 32 * g)
                        act.activation(qo[0][:, u // 2, u % 2 * HALF:(u % 2 + 1) * HALF], qf[u % 4][:, :], ACT.Copy)\
                           .then_inc(qh_done, 1)

                def body(g, ahead=True):
                    high_x1(g)
                    if ahead:
                        high_o(g + 2)
                    high_q(g)

                high_o(0)
                high_w(act)
                high_o(1)
                body(0)
                with act.Fori(1, NG - 2) as g:
                    body(g)
                body(NG - 2, ahead=False)
                high_x1(NG - 1)
                high_q(NG - 1)

            @block.vector
            def _(dve):
                low_w(dve)

                def normalise(n, i, s):
                    dve.wait_ge(rstd_done, n + 1)
                    dve.tensor_scalar(x1[:, i, :], r[s][:, :], mv[s][:, 0:1], rstd[s][:, 0:1],
                                      ALU.subtract, ALU.mult).then_inc(x1_done, 1)

                def norm_tile(g, i):
                    n, s = TT * g + i, i % 2
                    dve.wait_ge(y_done, n + 1)
                    dve.wait_ge(xb_done, n + 1)
                    wait(dve, x1_done, former(n, i))
                    dve.tensor_tensor(r[s][:, :], ps_y[s][:, :], xb[:, i, :], ALU.add).then_inc(r_done, 1)
                    dve.wait_ge(r_done, n + 1)
                    dve.bn_stats(stats[s][:, :], r[s][:, :]).then_inc(stat_done, 1)
                    wait_apart(dve, stat_done, n + 1, passed)
                    dve.bn_aggr(mv[s][:, :], stats[s][:, :]).then_inc(mv_done, 1)
                    dve.wait_ge(mv_done, n + 1)
                    dve.tensor_scalar(var_eps[s][:, :], mv[s][:, 1:2], EPS, None, ALU.add).then_inc(eps_done, 1)
                    if later(g) and i == 1:
                        dve.wait_ge(x1_stored, 16 * g)
                    if i:
                        normalise(n - 1, i - 1, 1 - s)
                    if i == TT - 1:
                        normalise(n, i, s)

                def low_x1(g, i):
                    n = TT * g + i
                    dve.wait_ge(t_done, n + 1)
                    dve.wait_ge(th_done, n + 1)
                    dve.tensor_tensor(x1s[1][:, :, i * P:(i + 1) * P],
                                      ps_t[i % 2][:, :].rearrange("p (k c) -> p k c", k=KD),
                                      x1s[0][:, :, i * P:(i + 1) * P].bitcast(F32), ALU.subtract)\
                       .then_inc(tl_done, 1)

                def scale_q(g):
                    for u in range(QU):
                        n = QU * g + u
                        dve.wait_ge(q_done, n + 1)
                        wait(dve, ql_done, n - 3)
                        dve.tensor_scalar(qf[u % 4][:, :], ps_q[u % 4][:, 0:HALF], bq_c[:, u // 2:u // 2 + 1], ISQ,
                                          ALU.add, ALU.mult).then_inc(qf_done, 1)

                def body(g):
                    for i in range(TT):
                        low_x1(g, i)
                        norm_tile(g + 1, i)
                    scale_q(g)

                for i in range(TT):
                    norm_tile(0, i)
                dve.wait_ge(b_loaded, 32)
                body(0)
                with dve.Fori(1, NG - 1) as g:
                    body(g)
                for i in range(TT):
                    low_x1(NG - 1, i)
                scale_q(NG - 1)

            @block.tensor
            def _(pe):
                def project_o(g, i):
                    if i == 0:
                        pe.wait_ge(o_low, KD * (g + 1))
                    n = TT * g + i
                    wait(pe, r_done, former(n, i))
                    products(pe, ps_y[i % 2][:, :], SPLIT, KD,
                             lambda a, k: os[a][:, k, i * P:(i + 1) * P],
                             lambda b, k: W[0][b][:, k, :]).then_inc(y_done, 1)

                def transpose_x1(g, i):
                    n = TT * g + i
                    pe.wait_ge(x1_done, n + 1)
                    wait(pe, tl_done, former(n, i))
                    for k in range(KD):
                        last = pe.transpose(ps_t[i % 2][:, k * P:(k + 1) * P], x1[:, i, k * P:(k + 1) * P],
                                            ident[:, :])
                    last.then_inc(t_done, 1)

                def project_q(g):
                    pe.wait_ge(tl_done, TT * (g + 1))
                    for u in range(QU):
                        n, m, h = QU * g + u, u // 2, u % 2
                        wait(pe, qf_done, n - 3)
                        products(pe, ps_q[u % 4][:, 0:HALF], SPLIT, KD,
                                 lambda a, k: W[1][a][:, k, m * P:(m + 1) * P],
                                 lambda b, k: x1s[b][:, k, h * HALF:(h + 1) * HALF]).then_inc(q_done, 1)

                def body(g):
                    for i in range(TT):
                        transpose_x1(g, i)
                        project_o(g + 1, i)
                    project_q(g)

                pe.wait_ge(w_low, 2)
                pe.wait_ge(consts, 3)
                for i in range(TT):
                    project_o(0, i)
                body(0)
                with pe.Fori(1, NG - 1) as g:
                    body(g)
                for i in range(TT):
                    transpose_x1(NG - 1, i)
                project_q(NG - 1)


def phase_cross_attention(nc, sem, ctxT, cq_d, wk, bk, wv, bv, o_d):
    ST = -(-S // P)
    LAST = S - (ST - 1) * P
    KC = (S // 2 + 1, S // 2 - 1)
    SH = S // 2
    PAIRS = H // 2
    KU = 2 * QUADS
    U = KU + ST
    assert U <= H
    with ExitStack() as ctx:
        def sb(name, shape, dt=F32):
            return ctx.enter_context(nc.sbuf_tensor("D_" + name, shape, dt))

        W = [Split(sb, n, [P, KD, D]) for n in ("wk", "wv")]
        craw = [sb(f"craw{i}", [P, S]) for i in range(2)]
        cs = [Split(sb, f"ctx{i}", [P, KD, S]) for i in range(2)]
        ks = [sb(f"keys{i}", [P, PAIRS, S], F32R) for i in range(2)]
        vs = [sb(f"values{i}", [P, ST, D]) for i in range(2)]
        qs = sb("queries", [P, PAIRS, 2, 2, T], F32R)
        e = [sb(f"e{i}", [T, ST * P]) for i in range(4)]
        pT = [sb(f"pT{i}", [P, ST, QT]) for i in range(2)]
        oo = [sb(f"o{i}", [P, QUADS, 2 * T]) for i in range(2)]
        bk_c, bv_c = sb("bk_c", [P, KD]), sb("bv_c", [P, KD])
        neg_max, rowsum, inv = (sb(n, [T, 4]) for n in ("neg_max", "rowsum", "inv"))
        ident = sb("ident", [P, P])
        ps_s = [ctx.enter_context(nc.psum_tensor(f"D_ps_s{i}", [P, 1024], F32)) for i in range(2)]
        ps_t = [ctx.enter_context(nc.psum_tensor(f"D_ps_t{i}", [P, 512], F32)) for i in range(2)]
        ps_p = [ctx.enter_context(nc.psum_tensor(f"D_ps_p{i}", [P, 512], F32)) for i in range(2)]

        w_loaded = [sem("D_w_loaded0"), sem("D_w_loaded1")]
        w_high, w_low, b_loaded, consts = sem("D_w_high"), sem("D_w_low"), sem("D_b_loaded"), sem("D_consts")
        c_loaded = [sem("D_c_loaded0"), sem("D_c_loaded1")]
        c_high, c_low = sem("D_c_high"), sem("D_c_low")
        q_loaded = [sem("D_q_loaded0"), sem("D_q_loaded1")]
        u_done, kh_done, kl_done, v_done = sem("D_u_done"), sem("D_kh_done"), sem("D_kl_done"), sem("D_v_done")
        s_done, max_done, exp_done = sem("D_s_done"), sem("D_max_done"), sem("D_exp_done")
        inv_done, norm_done, t_done = sem("D_inv_done"), sem("D_norm_done"), sem("D_t_done")
        taken, pv_done, o_done = sem("D_taken"), sem("D_pv_done"), sem("D_o_done")
        stored, passed = [sem("D_stored0"), sem("D_stored1")], sem("D_passed")

        def both_banks(s):
            t = ps_s[s % 2][0:T, :]
            return bass.AP(t.tensor, t.offset, [list(t.ap[0]), [513, 2], [1, SH]])

        def batches(eng, step):
            for b in range(2):
                for h in range(H):
                    step(b, b, h)
            with eng.Fori(1, B // 2 - 1) as i:
                for k in range(2):
                    for h in range(H):
                        step(2 * i + k, k, h)
            for b in (B - 2, B - 1):
                for h in range(H):
                    step(b, b % 2, h)

        def bank(u):
            return (u + u // 4) % 2

        def bank_of_quad(h):
            return (h + h // 4 + 1) % 2 if h < U else 1

        def unit_here(b, h):
            return h < U and not (isinstance(b, int) and b == B - 1)

        def started(n, back):
            return not (isinstance(n, int) and n < back)

        with nc.Block() as block:
            staging = [t[:, :, :].rearrange("p a b -> p (a b)")[:, 0:KD * D].rearrange("p (k n) -> p k n", k=KD)
                       for t in pT]
            load_w, high_w, low_w = split_weights(
                [w.rearrange("(k p) n -> p k n", p=P) for w in (wk, wv)], W, staging, w_loaded, w_high, w_low)

            @block.sync
            def _(sp):
                c_rows = ctxT.rearrange("b (k p) t -> b p k t", p=P)
                o_rows = o_d.rearrange("(m p) t -> p m t", p=P)
                q_rows = cq_d.rearrange("a (g j r) t -> r j g a t", j=2, r=HD)

                def load_ctx(b, chunks=range(KD)):
                    for k in chunks:
                        n = KD * b + k
                        wait(sp, c_low, n - 1)
                        src = c_rows[b, :, k, :] if isinstance(b, int) else \
                            c_rows[bass.ds(b, 1), :, k, :].rearrange("a p t -> (a p) t")
                        sp.dma_start(craw[k % 2][:, :], src).then_inc(c_loaded[k % 2], 16)

                def load_q(b, half):
                    g = slice(PAIRS // 2 * half, PAIRS // 2 * (half + 1))
                    for c in range(2):
                        for j in range(2):
                            rows = slice(HD * (j + 2 * c), HD * (j + 2 * c + 1))
                            for a in range(2):
                                sp.dma_start(qs[rows, g, j, a, :].bitcast(F32),
                                             q_rows[:, j, g, a, col(b * T, T)]).then_inc(q_loaded[half], 16)

                def store(b, par):
                    wait_apart(sp, o_done, QUADS * (b + 1), passed)
                    for r in range(4):
                        sp.dma_start(o_rows[HD * r:HD * r + HD, :, col(b * T, T)],
                                     oo[par][HD * r:HD * r + HD, :, (r % 2) * T:(r % 2) * T + T])\
                          .then_inc(stored[par], 16)

                load_ctx(0, (0, 1))
                load_w(sp)
                sp.dma_start(bk_c[:, :], bk).then_inc(b_loaded, 16)
                sp.dma_start(bv_c[:, :], bv).then_inc(b_loaded, 16)
                load_ctx(0, (2, 3))
                sp.wait_ge(consts, 2)
                load_q(0, 0)
                load_q(0, 1)
                load_ctx(1)

                def body(b, par, first, last):
                    if not first:
                        sp.wait_ge(s_done, H * b)
                        load_q(b, 1)
                    if not last:
                        load_ctx(b + 2)
                    if not first:
                        store(b - 1, 1 - par)
                    if not (isinstance(b, int) and b == B - 1):
                        sp.wait_ge(s_done, H * b + H // 2)
                        load_q(b + 1, 0)

                body(0, 0, True, False)
                body(1, 1, False, False)
                with sp.Fori(1, B // 2 - 1) as i:
                    for k in range(2):
                        body(2 * i + k, k, False, False)
                body(B - 2, 0, False, True)
                body(B - 1, 1, False, True)
                store(B - 1, 1)
                for par in range(2):
                    sp.wait_ge(stored[par], 64 * (B // 2))

            @block.gpsimd
            def _(pool):
                pool.memset(ident[:, :], 0.0).then_inc(consts, 1)
                pool.memset(qs[:, :, :, :, :].bitcast(F32), 0.0).then_inc(consts, 1)
                pool.wait_ge(consts, 2)
                pool.affine_select(out=ident[:, :], in_=ident[:, :], compare_op=ALU.not_equal, fill=1.0,
                                   base=0, pattern=[[-1, P]], channel_multiplier=1).then_inc(consts, 1)
                for i in range(4):
                    pool.memset(e[i][:, S:ST * P], 0.0).then_inc(consts, 1)
                for i in range(2):
                    pool.memset(vs[i][:, ST - 1, :], 0.0).then_inc(consts, 1)

                def split(b, par):
                    for k in range(KD):
                        n = KD * b + k
                        if k == 0:
                            wait(pool, u_done, U * (b - 1))
                        wait_apart(pool, c_loaded[k % 2], 32 * b + 16 * (k // 2) + 16, passed)
                        pool.tensor_copy(cs[par][0][:, k, :], craw[k % 2][:, :]).then_inc(c_high, 1)
                        pool.wait_ge(c_high, n + 1)
                        pool.tensor_tensor(cs[par][1][:, k, :], craw[k % 2][:, :],
                                           cs[par][0][:, k, :].bitcast(F32), ALU.subtract).then_inc(c_low, 1)

                pool.wait_ge(c_low, KD)
                split(1, 1)
                with pool.Fori(1, B // 2) as i:
                    for k in range(2):
                        split(2 * i + k, k)

            def key_rows(u):
                return ((2 * (u // 2), slice(0, 64), slice(64, P)), (2 * (u // 2) + 1, slice(64, P), slice(0, 64)))

            def key_cols(u):
                return (0, KC[0]) if u % 2 == 0 else (KC[0], S)

            @block.scalar
            def _(act):
                def unit(b, par, u):
                    act.wait_ge(u_done, U * b + u + 1)
                    if u < KU:
                        c0, c1 = key_cols(u)
                        for pair, rows, _ in key_rows(u):
                            if u == 0:
                                wait(act, s_done, H * (b - 1))
                            act.activation(ks[par][rows, pair, c0:c1], ps_p[bank(u)][rows, 0:c1 - c0], ACT.Identity,
                                           bias=bk_c[rows, u // 2:u // 2 + 1]).then_inc(kh_done, 1)
                        return
                    i = u - KU
                    rows = P if i < ST - 1 else LAST
                    if i == 0:
                        wait(act, pv_done, QUADS * (b - 1))
                    act.activation(vs[par][0:rows, i, :], ps_p[bank(u)][0:rows, 0:D], ACT.Copy).then_inc(v_done, 1)

                def take_tiles(b, h):
                    n, quad = H * b + h, QUADS * b + h // 4
                    for half in range(2):
                        act.wait_ge(t_done, 2 * n + 1 + half)
                        if h % 4 == 0 and half == 0:
                            wait(act, pv_done, quad - 1)
                        act.activation(pT[h // 4 % 2][:, 3 * half:3 * half + 3, h % 4 * T:(h % 4 + 1) * T],
                                       ps_t[half][:, 0:3 * T].rearrange("p (a t) -> p a t", a=3),
                                       ACT.Copy).then_inc(taken, 1)

                def exps(n, h):
                    act.wait_ge(max_done, n + 1)
                    act.wait_ge(s_done, n + 1)
                    wait(act, t_done, 2 * n - 6)
                    wait(act, inv_done, n - 3)
                    act.activation(e[h % 4][:, 0:S].rearrange("p (a b) -> p a b", a=2), both_banks(h), ACT.Exp,
                                   bias=neg_max[:, h % 4:h % 4 + 1],
                                   accum_out=rowsum[:, h % 4:h % 4 + 1]).then_inc(exp_done, 1)

                def step(b, par, h):
                    exps(H * b + h, h)
                    if unit_here(b, h):
                        unit(b + 1, 1 - par, h)
                    if started(H * b + h, 2):
                        take_tiles(b, h - 2)

                def high_ctx(k):
                    act.wait_ge(c_loaded[k % 2], 16 * (k // 2) + 16)
                    act.activation(cs[0][0][:, k, :], craw[k % 2][:, :], ACT.Copy).then_inc(c_high, 1)

                high_ctx(0)
                high_ctx(1)
                high_w(act, [0])
                high_ctx(2)
                high_ctx(3)
                high_w(act, [1])
                act.wait_ge(w_low, 2)
                act.wait_ge(b_loaded, 32)
                act.wait_ge(consts, 9)
                for u in range(U):
                    unit(0, 0, u)
                batches(act, step)
                take_tiles(B - 1, H - 2)
                take_tiles(B - 1, H - 1)

            @block.vector
            def _(dve):
                def unit(b, par, u):
                    if u >= KU:
                        return
                    c0, c1 = key_cols(u)
                    for i, (pair, rows, low_rows) in enumerate(key_rows(u)):
                        dve.wait_ge(kh_done, 2 * (KU * b + u) + i + 1)
                        dve.wait_ge(u_done, U * b + u + 1)
                        if u == 0:
                            wait(dve, s_done, H * (b - 1))
                        dve.scalar_tensor_tensor(
                            ks[par][low_rows, pair, c0:c1], ps_p[bank(u)][rows, 0:c1 - c0], bk_c[rows, u // 2:u // 2 + 1],
                            ks[par][rows, pair, c0:c1].bitcast(F32), ALU.add, ALU.subtract).then_inc(kl_done, 1)

                def maximum(n, h):
                    dve.wait_ge(s_done, n + 1)
                    wait(dve, exp_done, n - 3)
                    dve.tensor_reduce(neg_max[:, h % 4:h % 4 + 1], both_banks(h), AX.XY, ALU.max, negate=True)\
                       .then_inc(max_done, 1)

                def normalise(n, h):
                    dve.wait_ge(exp_done, n + 1)
                    wait(dve, norm_done, n - 3)
                    dve.reciprocal(inv[:, h % 4:h % 4 + 1], rowsum[:, h % 4:h % 4 + 1]).then_inc(inv_done, 1)
                    dve.wait_ge(inv_done, n + 1)
                    dve.tensor_scalar(e[h % 4][:, 0:S], e[h % 4][:, 0:S], inv[:, h % 4:h % 4 + 1], None, ALU.mult)\
                       .then_inc(norm_done, 1)

                def take_result(b, par, m, at):
                    dve.wait_ge(pv_done, QUADS * b + m + 1)
                    if m == 0:
                        wait(dve, stored[par], 32 * (b - par))
                    dve.tensor_scalar(oo[par][:, m, :], ps_p[bank_of_quad(at)][:, 0:2 * T], bv_c[:, m:m + 1], None, ALU.add)\
                       .then_inc(o_done, 1)

                def step(b, par, h):
                    n = H * b + h
                    if h > 0 and unit_here(b, h - 1):
                        unit(b + 1, 1 - par, h - 1)
                    maximum(n, h)
                    if started(n, 1):
                        normalise(n - 1, h - 1)
                    if h % 4 == 0 and started(n, 8):
                        if h > 4:
                            take_result(b, par, h // 4 - 2, h - 1)
                        else:
                            take_result(b - 1, 1 - par, QUADS - 2 + h // 4, (h - 1) % H)

                def low_ctx(k):
                    dve.wait_ge(c_high, k + 1)
                    dve.wait_ge(c_loaded[k % 2], 16 * (k // 2) + 16)
                    dve.tensor_tensor(cs[0][1][:, k, :], craw[k % 2][:, :], cs[0][0][:, k, :].bitcast(F32),
                                      ALU.subtract).then_inc(c_low, 1)

                low_ctx(0)
                low_ctx(1)
                low_w(dve, [0])
                low_ctx(2)
                low_ctx(3)
                low_w(dve, [1])
                dve.wait_ge(w_high, 2)
                dve.wait_ge(b_loaded, 32)
                dve.wait_ge(consts, 9)
                for u in range(U):
                    unit(0, 0, u)
                batches(dve, step)
                normalise(H * B - 1, H - 1)
                take_result(B - 1, 1, QUADS - 2, H - 1)
                take_result(B - 1, 1, QUADS - 1, 3)

            @block.tensor
            def _(pe):
                def unit_read(b, u):
                    if 0 <= u < KU:
                        pe.wait_ge(kl_done, 2 * (KU * b + u + 1))
                    else:
                        wait(pe, v_done, ST * b + max(u - KU + 1, 0))

                def unit(b, par, u):
                    if u == 0:
                        pe.wait_ge(c_low, KD * (b + 1))
                    if isinstance(b, int) and b == 0 and u in (0, KU):
                        pe.wait_ge(w_low, 1 + u // KU)
                    unit_read(b, u - (1 if u % 4 == 0 else 2))
                    if u % 4 == 1:
                        wait(pe, o_done, QUADS * (b - 1) - 1 + u // 4)
                    c = cs[par]
                    if u < KU:
                        m, (c0, c1) = u // 2, key_cols(u)
                        last = products(pe, ps_p[bank(u)][:, 0:c1 - c0], SPLIT, KD,
                                        lambda a, k: W[0][a][:, k, m * P:(m + 1) * P],
                                        lambda a, k: c[a][:, k, c0:c1])
                    else:
                        i = u - KU
                        rows = P if i < ST - 1 else LAST
                        last = products(pe, ps_p[bank(u)][0:rows, 0:D], SPLIT, KD,
                                        lambda a, k: c[a][:, k, i * P:i * P + rows],
                                        lambda a, k: W[1][a][:, k, :])
                    last.then_inc(u_done, 1)

                def scores(b, par, n, h):
                    if h == 0:
                        pe.wait_ge(kl_done, 2 * KU * (b + 1))
                    if h % (H // 2) == 0:
                        pe.wait_ge(q_loaded[h // (H // 2)], 128 * (b + 1))
                    wait(pe, exp_done, n - 1)
                    g, j = h // 2, h % 2
                    for half, (c0, c1) in enumerate(((0, KC[0]), (S - KC[0], S))):
                        for a in range(2):
                            last = pe.matmul(ps_s[h % 2][0:T, 512 * half:512 * half + c1 - c0],
                                             qs[:, g, j, a, :], ks[par][:, g, c0:c1],
                                             start=(a == 0), stop=(a == 1))
                    last.then_inc(s_done, 1)

                def transposes(n, h):
                    pe.wait_ge(norm_done, n + 1)
                    for half in range(2):
                        wait(pe, taken, 2 * n - 1 + half)
                        for i in range(3):
                            t = 3 * half + i
                            last = pe.transpose(ps_t[half][:, i * T:(i + 1) * T], e[h % 4][:, t * P:(t + 1) * P],
                                                ident[0:T, 0:T])
                        last.then_inc(t_done, 1)

                def weighted_sum(b, par, m, at):
                    quad = QUADS * b + m
                    pe.wait_ge(taken, 8 * quad + 8)
                    if m == 0:
                        pe.wait_ge(v_done, ST * (b + 1))
                    out = ps_p[bank_of_quad(at)]
                    for i in range(ST):
                        for g in range(2):
                            c = (2 * m + g) * 2 * HD
                            last = pe.matmul(out[2 * HD * g:2 * HD * (g + 1), 0:2 * T], vs[par][:, i, c:c + 2 * HD],
                                             pT[m % 2][:, i, 2 * T * g:2 * T * (g + 1)],
                                             start=(i == 0), stop=(i == ST - 1), tile_position=(0, 2 * HD * g))
                    last.then_inc(pv_done, 1)

                def step(b, par, h):
                    n = H * b + h
                    scores(b, par, n, h)
                    if unit_here(b, h):
                        unit(b + 1, 1 - par, h)
                    if h % 4 == 3 and started(n, 7):
                        if isinstance(b, int) and b == B - 1:
                            pe.wait_ge(v_done, ST * B)
                            pe.wait_ge(o_done, QUADS * b - 1 + h // 4)
                        else:
                            unit_read(b + 1, h - 1 if h < U else U - 2)
                        if h > 3:
                            weighted_sum(b, par, h // 4 - 1, h)
                        else:
                            weighted_sum(b - 1, 1 - par, QUADS - 1, h)
                    if started(n, 2):
                        transposes(n - 2, h - 2)

                for u in range(U):
                    unit(0, 0, u)
                pe.wait_ge(consts, 9)
                batches(pe, step)
                transposes(H * B - 2, H - 2)
                transposes(H * B - 1, H - 1)
                pe.wait_ge(o_done, QUADS * B - 2)
                weighted_sum(B - 1, 1, QUADS - 1, 3)


def phase_feed_forward(nc, sem, o_d, x1_d, wo, bo, w_gate, w_up, w_down, out):
    PIECES = 3 * KD
    SLOTS = 4
    with ExitStack() as ctx:
        def sb(name, shape, dt=F32):
            return ctx.enter_context(nc.sbuf_tensor("E_" + name, shape, dt))

        def psum(name):
            return ctx.enter_context(nc.psum_tensor("E_" + name, [P, 512], F32))

        with nc.sbuf_tensor("E_w_f32", [P, PIECES, F], F32) as w_f32:
            pass
        w_f32r = sb("w_f32r", [P, PIECES, F], F32R)
        with nc.sbuf_tensor("E_w_int", [P, SLOTS, F], I32) as w_int:
            pass
        hs = Split(sb, "hidden", [P, KF, GT])
        wos = Split(sb, "wo", [P, KD, D])
        acts = Split(sb, "acts", [P, KD, GT])
        oraw = sb("oraw", [P, KD, GT])
        x2 = sb("x2", [P, TT, D])
        x1b = [sb(f"x1b{i}", [P, D]) for i in range(2)]
        bo_b = sb("bo_b", [P, D])
        gated = [sb(f"gated{i}", [P, HALF]) for i in range(2)]
        r = {n: sb("r_" + n, [P, D]) for n in "ab"}
        stats = {n: sb("stats_" + n, [P, 6]) for n in "ab"}
        mv = {n: sb("mv_" + n, [P, 2]) for n in "ab"}
        var_eps = {n: sb("var_eps_" + n, [P, 1]) for n in "ab"}
        rstd = {n: sb("rstd_" + n, [P, 1]) for n in "ab"}
        y = [sb(f"y{i}", [P, D]) for i in range(2)]
        minus_half, ident = sb("minus_half", [P, 1]), sb("ident", [P, P])
        biggest, biggest1, biggest_all = sb("biggest", [P, PIECES]), sb("biggest1", [P, 1]), sb("biggest_all", [P, 1])
        inexact = sb("inexact", [P, 1], I32)
        ps_g, ps_u = [psum(f"ps_g{i}") for i in range(2)], [psum(f"ps_u{i}") for i in range(2)]
        ps_t = [psum(f"ps_t{i}") for i in range(2)]
        ps_y, ps_d = psum("ps_y"), psum("ps_d")

        wo_loaded, wo_high, wo_low = sem("E_wo_loaded"), sem("E_wo_high"), sem("E_wo_low")
        int_loaded = [sem(f"E_int_loaded{i}") for i in range(SLOTS)]
        int_max, int_done = sem("E_int_max"), sem("E_int_done")
        all_max, flagged, again_loaded, w_ready = (sem("E_" + n) for n in
                                                   ("all_max", "flagged", "again_loaded", "w_ready"))
        b_loaded, consts = sem("E_b_loaded"), sem("E_consts")
        o_loaded = sem("E_o_loaded")
        o_high, o_low = sem("E_o_high"), sem("E_o_low")
        x1_loaded, x1b_done = [sem("E_x1_loaded0"), sem("E_x1_loaded1")], sem("E_x1b_done")
        y_done, t_done, th_done, tl_done = (sem("E_" + n) for n in ("y_done", "t_done", "th_done", "tl_done"))
        gu_done, silu_done, h_done, hh_done, hl_done = (sem("E_" + n) for n in
                                                        ("gu_done", "silu_done", "h_done", "hh_done", "hl_done"))
        d_done = sem("E_d_done")
        sum_done = {n: sem("E_sum_" + n) for n in "ab"}
        stat_done = {n: sem("E_stat_" + n) for n in "ab"}
        mv_done = {n: sem("E_mv_" + n) for n in "ab"}
        eps_done = {n: sem("E_eps_" + n) for n in "ab"}
        rstd_done = {n: sem("E_rstd_" + n) for n in "ab"}
        norm_done = {n: sem("E_norm_" + n) for n in "ab"}
        stored, passed = [sem("E_stored0"), sem("E_stored1")], sem("E_passed")
        HU = 2 * KF

        def unit(u):
            return 2 * (u // 4) + u % 2, u // 2 % 2

        def groups(eng, body):
            body(0)
            with eng.Fori(1, NG - 1) as g:
                body(g)

        def slot_count(g, i):
            return (TT - i % 2 + 1) // 2 * g + i // 2

        def piece(n):
            if n < 2 * KD:
                return (w_gate, w_up)[n // KD][n % KD * P:(n % KD + 1) * P, :]
            k = (n - 2 * KD) * (KF // KD)
            return w_down[k * P:(k + KF // KD) * P, :].rearrange("(a p) n -> p a n", p=P)

        def place(t, n):
            return t[:, n, :] if n < 2 * KD else t[:, n, :].rearrange("p (a n) -> p a n", n=D)

        with nc.Block() as block:

            @block.sync
            def _(sp):
                o_rows = o_d.rearrange("(k p) t -> p k t", p=P)

                def load_o(g):
                    if later(g):
                        sp.wait_ge(o_low, KD * g)
                    sp.dma_start(oraw[:, :, :], o_rows[:, :, col(g * GT, GT)]).then_inc(o_loaded, 16)

                def load_x1(g, i):
                    if i % 2 == 0 or later(g) or i > 1:
                        wait(sp, sum_done["a"], TT * g + i - (0 if i == 0 else 1))
                    src = x1_d.rearrange("(t p) n -> t p n", p=P)
                    n = TT * g + i
                    sp.dma_start(x1b[i % 2][:, :], src[n] if isinstance(n, int) else
                                 src[bass.ds(n, 1)].rearrange("a p n -> (a p) n")).then_inc(x1_loaded[i % 2], 16)

                def store(g, i):
                    n = TT * g + i
                    sp.wait_ge(norm_done["b"], n + 1)
                    dst = out.rearrange("(t p) n -> t p n", p=P)
                    sp.dma_start(dst[n] if isinstance(n, int) else
                                 dst[bass.ds(n, 1)].rearrange("a p n -> (a p) n"), y[i % 2][:, :])\
                      .then_inc(stored[i % 2], 16)

                sp.dma_start(x2[:, 0:KD, :], wo.rearrange("(k p) n -> p k n", p=P)).then_inc(wo_loaded, 16)
                sp.dma_start(bo_b[:, :], bo.rearrange("(a n) -> a n", a=1).broadcast_to([P, D])).then_inc(b_loaded, 16)
                load_o(0)
                load_x1(0, 0)
                load_x1(0, 1)
                for n in range(PIECES):
                    wait(sp, int_max, n - SLOTS + 1)
                    wait(sp, int_done, n - SLOTS + 1)
                    slot = w_int[:, n % SLOTS, :]
                    sp.dma_start(slot.rearrange("p (a n) -> p a n", n=D) if n >= 2 * KD else slot, piece(n))\
                      .then_inc(int_loaded[n % SLOTS], 16)
                    if n in (4, 6, 8):
                        load_x1(0, n // 2)
                sp.wait_ge(flagged, 1)
                with sp.If(sp.value_load(inexact[0:1, 0:1], min_val=0, max_val=1) == 1):
                    for n in range(PIECES):
                        sp.wait_ge(int_done, PIECES + n)
                        sp.dma_start(w_int[:, 0, :].rearrange("p (a n) -> p a n", n=D) if n >= 2 * KD else
                                     w_int[:, 0, :], piece(n)).then_inc(again_loaded, 16)
                load_o(1)

                def body(g, ahead=True):
                    for i in range(TT):
                        load_x1(g + 1, i)
                        if i == 0 and ahead:
                            load_o(g + 2)
                        store(g, i)

                body(0)
                with sp.Fori(1, NG - 2) as g:
                    body(g)
                body(NG - 2, ahead=False)
                for i in range(TT):
                    store(NG - 1, i)
                sp.wait_ge(stored[0], 16 * ((TT + 1) // 2) * NG)
                sp.wait_ge(stored[1], 16 * (TT // 2) * NG)

            @block.gpsimd
            def _(pool):
                pool.memset(minus_half[:, :], -0.5).then_inc(consts, 1)
                pool.memset(ident[:, :], 0.0).then_inc(consts, 1)
                pool.wait_ge(consts, 2)
                pool.affine_select(out=ident[:, :], in_=ident[:, :], compare_op=ALU.not_equal, fill=1.0,
                                   base=0, pattern=[[-1, P]], channel_multiplier=1).then_inc(consts, 1)
                pool.wait_ge(b_loaded, 16)

                def add_bias(g, i):
                    pool.wait_ge(x1_loaded[i % 2], 16 * slot_count(g, i) + 16)
                    pool.tensor_tensor(x1b[i % 2][:, :], x1b[i % 2][:, :], bo_b[:, :], ALU.add).then_inc(x1b_done, 1)

                def rstd_of(name, n):
                    pool.wait_ge(eps_done[name], n + 1)
                    wait(pool, norm_done[name], n)
                    pool.tensor_tensor(rstd[name][:, :], var_eps[name][:, :], minus_half[:, :], ALU.pow)\
                        .then_inc(rstd_done[name], 1)

                def low_h(g):
                    for u in range(HU):
                        n, (c, h) = HU * g + u, unit(u)
                        pool.wait_ge(hh_done, n + 1)
                        pool.wait_ge(h_done, n + 1)
                        cols = slice(h * HALF, (h + 1) * HALF)
                        pool.tensor_tensor(hs[1][:, c, cols], gated[u % 2][:, :], hs[0][:, c, cols].bitcast(F32),
                                           ALU.subtract).then_inc(hl_done, 1)

                def body(g):
                    low_h(g)
                    for i in range(TT):
                        add_bias(g + 1, i)
                        rstd_of("b", TT * g + i)
                        rstd_of("a", TT * (g + 1) + i)

                for i in range(TT):
                    add_bias(0, i)
                    rstd_of("a", i)
                pool.wait_ge(all_max, 1)
                pool.partition_all_reduce(biggest_all[:, :], biggest1[:, :], P, bass.bass_isa.ReduceOp.max)\
                    .then_inc(all_max, 1)
                groups(pool, body)
                low_h(NG - 1)
                for i in range(TT):
                    rstd_of("b", TT * (NG - 1) + i)

            @block.scalar
            def _(act):
                def high_o(g):
                    act.wait_ge(o_loaded, 16 * g + 16)
                    if later(g):
                        act.wait_ge(gu_done, HU * g)
                    for k in range(KD):
                        act.activation(acts[0][:, k, :], oraw[:, k, :], ACT.Copy).then_inc(o_high, 1)

                def high_x2(g, i):
                    act.wait_ge(t_done, TT * g + i + 1)
                    act.activation(acts[0][:, :, i * P:(i + 1) * P],
                                   ps_t[i % 2][:, :].rearrange("p (k c) -> p k c", k=KD), ACT.Copy)\
                       .then_inc(th_done, 1)

                def silu_and_high(g):
                    def high(u):
                        c, h = unit(u)
                        act.wait_ge(h_done, HU * g + u + 1)
                        act.activation(hs[0][:, c, h * HALF:(h + 1) * HALF], gated[u % 2][:, :], ACT.Copy)\
                           .then_inc(hh_done, 1)

                    for u in range(HU):
                        n = HU * g + u
                        act.wait_ge(gu_done, n + 1)
                        wait(act, hl_done, n - 1)
                        act.activation(gated[u % 2][:, :], ps_g[u % 2][:, 0:HALF], ACT.Silu, scale=FSCALE)\
                           .then_inc(silu_done, 1)
                        if u == 0:
                            high_x2(g, TT - 1)
                        else:
                            high(u - 1)
                    high(HU - 1)

                act.wait_ge(wo_loaded, 16)
                act.activation(wos[0][:, :, :], x2[:, 0:KD, :], ACT.Copy).then_inc(wo_high, 1)
                high_o(0)

                def convert(n, source, tile, ready):
                    act.wait_ge(*ready)
                    act.activation(place(tile, n), source.rearrange("p (a n) -> p a n", n=D) if n >= 2 * KD else source,
                                   ACT.Copy).then_inc(int_done, 1)

                for n in range(PIECES):
                    convert(n, w_int[:, n % SLOTS, :], w_f32r, (int_loaded[n % SLOTS], 16 * (n // SLOTS) + 16))
                    if n in (3, 5, 7, 9):
                        high_x2(0, (n - 3) // 2)
                act.wait_ge(flagged, 1)
                act.wait_ge(int_done, PIECES)
                with act.If(act.value_load(inexact[0:1, 0:1], min_val=0, max_val=1) == 1):
                    for n in range(PIECES):
                        convert(n, w_int[:, 0, :], w_f32, (again_loaded, 16 * n + 16))
                    act.wait_ge(int_done, 2 * PIECES)
                act.sem_inc(w_ready, 1)

                def body(g):
                    silu_and_high(g)
                    high_o(g + 1)
                    for i in range(TT - 1):
                        high_x2(g + 1, i)

                groups(act, body)
                silu_and_high(NG - 1)

            @block.vector
            def _(dve):
                def add_and_stats(name, n, add):
                    wait(dve, norm_done[name], n)
                    add(r[name][:, :]).then_inc(sum_done[name], 1)
                    dve.wait_ge(sum_done[name], n + 1)
                    dve.bn_stats(stats[name][:, :], r[name][:, :]).then_inc(stat_done[name], 1)
                    wait_apart(dve, stat_done[name], n + 1, passed)
                    dve.bn_aggr(mv[name][:, :], stats[name][:, :]).then_inc(mv_done[name], 1)
                    dve.wait_ge(mv_done[name], n + 1)
                    dve.tensor_scalar(var_eps[name][:, :], mv[name][:, 1:2], EPS, None, ALU.add)\
                       .then_inc(eps_done[name], 1)

                def normalise(name, n, dst):
                    dve.wait_ge(rstd_done[name], n + 1)
                    dve.tensor_scalar(dst, r[name][:, :], mv[name][:, 0:1], rstd[name][:, 0:1],
                                      ALU.subtract, ALU.mult).then_inc(norm_done[name], 1)

                def second_sum(g, i):
                    n = TT * g + i
                    dve.wait_ge(y_done, n + 1)
                    dve.wait_ge(x1b_done, n + 1)
                    add_and_stats("a", n, lambda dst: dve.tensor_tensor(dst, ps_y[:, :], x1b[i % 2][:, :], ALU.add))

                def third_sum(g, i):
                    n = TT * g + i
                    dve.wait_ge(d_done, n + 1)
                    add_and_stats("b", n, lambda dst: dve.scalar_tensor_tensor(
                        dst, ps_d[:, :], FSCALE, x2[:, i, :], ALU.mult, ALU.add))

                def third_norm(g, i):
                    wait(dve, stored[i % 2], 16 * slot_count(g, i))
                    normalise("b", TT * g + i, y[i % 2][:, :])

                def low_o(g):
                    for k in range(KD):
                        dve.wait_ge(o_high, KD * g + k + 1)
                        dve.wait_ge(o_loaded, 16 * g + 16)
                        dve.tensor_tensor(acts[1][:, k, :], oraw[:, k, :], acts[0][:, k, :].bitcast(F32),
                                          ALU.subtract).then_inc(o_low, 1)

                def low_x2(g, i):
                    n = TT * g + i
                    dve.wait_ge(t_done, n + 1)
                    dve.wait_ge(th_done, n + 1)
                    dve.tensor_tensor(acts[1][:, :, i * P:(i + 1) * P],
                                      ps_t[i % 2][:, :].rearrange("p (k c) -> p k c", k=KD),
                                      acts[0][:, :, i * P:(i + 1) * P].bitcast(F32), ALU.subtract)\
                       .then_inc(tl_done, 1)

                def gate(g):
                    for u in range(HU):
                        n = HU * g + u
                        dve.wait_ge(gu_done, n + 1)
                        dve.wait_ge(silu_done, n + 1)
                        dve.scalar_tensor_tensor(gated[u % 2][:, :], ps_u[u % 2][:, 0:HALF], FSCALE, gated[u % 2][:, :],
                                                 ALU.mult, ALU.mult).then_inc(h_done, 1)
                        if u == 0:
                            low_x2(g, TT - 1)

                def body(g):
                    gate(g)
                    low_o(g + 1)
                    for i in range(TT):
                        third_sum(g, i)
                        second_sum(g + 1, i)
                        third_norm(g, i)
                        normalise("a", TT * (g + 1) + i, x2[:, i, :])
                        if i:
                            low_x2(g + 1, i - 1)

                dve.wait_ge(wo_high, 1)
                dve.wait_ge(wo_loaded, 16)
                dve.tensor_tensor(wos[1][:, :, :], x2[:, 0:KD, :], wos[0][:, :, :].bitcast(F32), ALU.subtract)\
                   .then_inc(wo_low, 1)
                dve.wait_ge(wo_low, 1)
                low_o(0)
                for n in range(PIECES):
                    dve.wait_ge(int_loaded[n % SLOTS], 16 * (n // SLOTS) + 16)
                    dve.tensor_reduce(biggest[:, n:n + 1], w_int[:, n % SLOTS, :], AX.X, ALU.max,
                                      apply_absolute_value=True).then_inc(int_max, 1)
                    if n in (1, 3, 5, 7, 9):
                        second_sum(0, n // 2)
                        normalise("a", n // 2, x2[:, n // 2, :])
                        if n > 1:
                            low_x2(0, n // 2 - 1)
                dve.wait_ge(int_max, PIECES)
                dve.tensor_reduce(biggest1[:, :], biggest[:, :], AX.X, ALU.max).then_inc(all_max, 1)
                dve.wait_ge(all_max, 2)
                dve.tensor_scalar(inexact[:, :], biggest_all[:, :], EXACT, None, ALU.is_gt).then_inc(flagged, 1)
                groups(dve, body)
                gate(NG - 1)
                for i in range(TT):
                    third_sum(NG - 1, i)
                    third_norm(NG - 1, i)

            @block.tensor
            def _(pe):
                def project_o(g, i):
                    n = TT * g + i
                    if i == 0:
                        pe.wait_ge(o_low, KD * (g + 1))
                    wait(pe, sum_done["a"], n)
                    products(pe, ps_y[:, :], SPLIT, KD, lambda a, k: acts[a][:, k, i * P:(i + 1) * P],
                             lambda a, k: wos[a][:, k, :]).then_inc(y_done, 1)

                def transpose_x2(g, i):
                    n = TT * g + i
                    pe.wait_ge(norm_done["a"], n + 1)
                    wait(pe, tl_done, n if i == 0 else n - 1)
                    for k in range(KD):
                        last = pe.transpose(ps_t[i % 2][:, k * P:(k + 1) * P], x2[:, i, k * P:(k + 1) * P],
                                            ident[:, :])
                    last.then_inc(t_done, 1)

                def feed_forward(w, view):
                    both = ((0, 0), (0, 1))

                    def gate_and_up(g):
                        for u in range(HU):
                            n, (c, h) = HU * g + u, unit(u)
                            if u == 0:
                                pe.wait_ge(tl_done, TT * g + (HALF + P - 1) // P)
                            if u == 2:
                                pe.wait_ge(tl_done, TT * (g + 1))
                            wait(pe, h_done, n - 1)
                            for ps, first in ((ps_g, 0), (ps_u, KD)):
                                last = products(pe, ps[u % 2][:, 0:HALF], both, KD,
                                                lambda a, k: w[:, first + k, c * P:(c + 1) * P],
                                                lambda a, k: view(acts[a][:, k, h * HALF:(h + 1) * HALF]))
                            last.then_inc(gu_done, 1)
                            if u == 0:
                                transpose_x2(g, TT - 1)

                    def down(g, i):
                        n = TT * g + i
                        if i == 0:
                            pe.wait_ge(hl_done, HU * (g + 1) - 2)
                        if i == 2:
                            pe.wait_ge(hl_done, HU * (g + 1))
                        wait(pe, sum_done["b"], n)
                        products(pe, ps_d[:, :], ((0, 0), (1, 0)), KF,
                                 lambda a, k: view(hs[a][:, k, i * P:(i + 1) * P]),
                                 lambda a, k: w[:, 2 * KD + k // 3, k % 3 * D:(k % 3 + 1) * D]).then_inc(d_done, 1)

                    def body(g):
                        gate_and_up(g)
                        for i in range(TT):
                            down(g, i)
                            project_o(g + 1, i)
                            if i:
                                transpose_x2(g + 1, i - 1)

                    groups(pe, body)
                    gate_and_up(NG - 1)
                    for i in range(TT):
                        down(NG - 1, i)

                pe.wait_ge(wo_low, 1)
                pe.wait_ge(consts, 3)
                for i in range(TT):
                    project_o(0, i)
                    if i:
                        transpose_x2(0, i - 1)
                pe.wait_ge(flagged, 1)
                pe.wait_ge(w_ready, 1)
                pe.wait_ge(int_done, PIECES)
                with pe.If(pe.value_load(inexact[0:1, 0:1], min_val=0, max_val=1) == 1):
                    feed_forward(w_f32, lambda x: x.bitcast(F32))
                with pe.Else():
                    feed_forward(w_f32r, lambda x: x)


def build_decoder(nc, x, xT, ctxT, a_wq, a_wk, a_wv, a_wo, a_bo, a_w, a_v,
                  x_wq, x_bq, x_wk, x_bk, x_wv, x_bv, x_wo, x_bo, w_gate, w_up, w_down, out):
    with ExitStack() as ctx:
        def sem(name):
            return ctx.enter_context(nc.semaphore(name))

        def dram(name, shape):
            return nc.dram_tensor(name, shape, F32, kind="Internal").ap()

        q_d, k_d, v_d = dram("self_q", [D, N]), dram("self_k", [D, N]), dram("self_v", [N, D])
        o_d, x1_d = dram("self_o", [D, N]), dram("x1", [N, D])
        cq_d, co_d = dram("cross_q", [2, D, N]), dram("cross_o", [D, N])
        phase_qkv(nc, sem, xT, a_wq, a_wk, a_wv, q_d, k_d, v_d)
        phase_self_attention(nc, sem, q_d, k_d, v_d, a_w, a_v, o_d)
        phase_norm_and_queries(nc, sem, o_d, x, a_wo, a_bo, x_wq, x_bq, x1_d, cq_d)
        phase_cross_attention(nc, sem, ctxT, cq_d, x_wk, x_bk, x_wv, x_bv, co_d)
        phase_feed_forward(nc, sem, co_d, x1_d, x_wo, x_bo, w_gate, w_up, w_down, out)


def kernel(x, ctx_1024, L0_attn_Wq, L0_attn_Wk, L0_attn_Wv, L0_attn_Wo, L0_attn_bo, L0_attn_w, L0_attn_v,
           L0_xattn_Wq, L0_xattn_bq, L0_xattn_Wk, L0_xattn_bk, L0_xattn_Wv, L0_xattn_bv, L0_xattn_Wo, L0_xattn_bo,
           L0_ffn_w_gate, L0_ffn_w_up, L0_ffn_w_down):
    import numpy as np
    import concourse.bacc as bacc
    from concourse.bass_utils import run_bass_kernel_spmd

    def columns(bias):
        return np.asarray(bias).reshape(KD, P).T

    tokens = np.asarray(x).reshape(N, D)
    given = {
        "x": tokens, "xT": tokens.T, "ctxT": np.asarray(ctx_1024).transpose(0, 2, 1),
        "a_wq": L0_attn_Wq, "a_wk": L0_attn_Wk, "a_wv": L0_attn_Wv, "a_wo": L0_attn_Wo, "a_bo": L0_attn_bo,
        "a_w": L0_attn_w, "a_v": L0_attn_v,
        "x_wq": np.asarray(L0_xattn_Wq).T, "x_bq": columns(L0_xattn_bq),
        "x_wk": np.asarray(L0_xattn_Wk).T, "x_bk": columns(L0_xattn_bk),
        "x_wv": np.asarray(L0_xattn_Wv).T, "x_bv": columns(L0_xattn_bv),
        "x_wo": np.asarray(L0_xattn_Wo).T, "x_bo": L0_xattn_bo,
        "w_gate": np.asarray(L0_ffn_w_gate).T, "w_up": np.asarray(L0_ffn_w_up).T,
        "w_down": np.asarray(L0_ffn_w_down).T,
    }
    nc = bacc.Bacc("TRN2", target_bir_lowering=False, num_devices=1)
    arrays, args = {}, {}
    for name, a in given.items():
        arrays["in_" + name] = np.ascontiguousarray(a)
        args[name] = nc.dram_tensor("in_" + name, arrays["in_" + name].shape,
                                    mybir.dt.from_np(arrays["in_" + name].dtype), kind="ExternalInput").ap()
    args["out"] = nc.dram_tensor("out_0", [N, D], F32, kind="ExternalOutput").ap()
    build_decoder(nc, **args)
    r = run_bass_kernel_spmd(nc, [arrays], core_ids=[0])
    return r.results[0]["out_0"].reshape(B, T, D)
```

```python
from contextlib import ExitStack

import concourse.bass as bass
from concourse import mybir

B, T, S, D, H = 32, 100, 722, 512, 16
HD = D // H
F = 1536
P = 128
KD = D // P
KF = F // P
N = B * T
GT = 640
NG = N // GT
TT = GT // P
HALF = GT // 2
QUADS = H // 4
QT = 4 * T
EPS = 1e-5
FSCALE = 1.0 / 127.0
ISQ = float(HD) ** -0.5
EXACT = 4096.0
MASK = 1.5 * 2.0 ** 127

F32 = mybir.dt.float32
F32R = mybir.dt.float32r
I32 = mybir.dt.int32
ALU = mybir.AluOpType
ACT = mybir.ActivationFunctionType
AX = mybir.AxisListType


def wait(eng, sem, value):
    if isinstance(value, int) and value <= 0:
        return
    eng.wait_ge(sem, value)


def wait_apart(eng, sem, value, passed):
    wait(eng, sem, value)
    eng.sem_inc(passed, 1)


def later(g):
    return not isinstance(g, int) or g > 0


def col(base, width):
    return slice(base, base + width) if isinstance(base, int) else bass.ds(base, width)


def products(pe, out, terms, chunks, lhs, rhs):
    last = None
    for k in range(chunks):
        for n, (a, b) in enumerate(terms):
            last = pe.matmul(out, lhs(a, k), rhs(b, k),
                             start=(k == 0 and n == 0), stop=(k == chunks - 1 and n == len(terms) - 1))
    return last


SPLIT = ((0, 0), (0, 1), (1, 0))


class Split:

    def __init__(self, sb, name, shape):
        self.parts = [sb(name + "_high", shape, F32R), sb(name + "_low", shape, F32R)]

    def __getitem__(self, part):
        return self.parts[part]


def split_weights(raws, targets, staging, sem_loaded, sem_high, sem_low, present=0):
    every = range(len(raws))

    def loaded(n):
        return 16 * ((n - present) // 2 + 1) if n >= present else 0

    def load(sp, which=every):
        for n in which:
            wait(sp, sem_high, KD * (n - 1))
            wait(sp, sem_low, KD * (n - 1))
            sp.dma_start(staging[n % 2], raws[n]).then_inc(sem_loaded[n % 2], 16)

    def high(act, which=every, chunks=range(KD)):
        for n in which:
            for k in chunks:
                wait(act, sem_loaded[n % 2], loaded(n))
                act.activation(targets[n][0][:, k, :], staging[n % 2][:, k, :], ACT.Copy).then_inc(sem_high, 1)

    def low(dve, which=every, chunks=range(KD)):
        for n in which:
            for k in chunks:
                wait(dve, sem_high, KD * n + k + 1)
                wait(dve, sem_loaded[n % 2], loaded(n))
                dve.tensor_tensor(targets[n][1][:, k, :], staging[n % 2][:, k, :],
                                  targets[n][0][:, k, :].bitcast(F32), ALU.subtract).then_inc(sem_low, 1)

    return load, high, low


def phase_qkv(nc, sem, xT, wq, wk, wv, w, v, q_d, k_d, v_d, rhat_d):
    UNITS = 2 * KD * 2 + TT
    RING = 7
    assert UNITS % RING == 0
    with ExitStack() as ctx:
        def sb(name, shape, dt=F32):
            return ctx.enter_context(nc.sbuf_tensor("A_" + name, shape, dt))

        W = [Split(sb, n, [P, KD, D]) for n in ("wq", "wk", "wv")]
        staging = [sb(f"wstage{i}", [P, KD, D]) for i in range(2)]
        xraw = sb("xraw", [P, KD, GT])
        xs = [Split(sb, f"x{i}", [P, KD, GT]) for i in range(2)]
        qk = [[sb(f"{n}{i}", [P, KD, GT]) for n in "qk"] for i in range(2)]
        vo = [sb(f"v{i}", [P, TT, D]) for i in range(2)]
        wb, vb, neg_w, ev = (sb(n, [T, H]) for n in ("wb", "vb", "neg_w", "ev"))
        dist_i, dist = sb("dist_i", [T, T], I32), sb("dist", [T, T])
        rhat = sb("rhat", [T, H, T])
        ps = [ctx.enter_context(nc.psum_tensor(f"A_ps{i}", [P, 512], F32)) for i in range(RING)]

        w_loaded = [sem("A_w_loaded0"), sem("A_w_loaded1")]
        w_high, w_low = sem("A_w_high"), sem("A_w_low")
        x_loaded, x_high, x_low = sem("A_x_loaded"), sem("A_x_high"), sem("A_x_low")
        unit_done, passed = sem("A_unit_done"), sem("A_passed")
        act_out, dve_out = sem("A_act_out"), sem("A_dve_out")
        stored = [sem("A_stored0"), sem("A_stored1")]
        wv_loaded, consts, rhat_stored = sem("A_wv_loaded"), sem("A_consts"), sem("A_rhat_stored")
        arg_done, arg_exp, rhat_step = sem("A_arg_done"), sem("A_arg_exp"), sem("A_rhat_step")
        rhat_done, first_high = sem("A_rhat_done"), sem("A_first_high")

        def of_act(u):
            return u % 2 == 0

        ACTS = sum(of_act(u) for u in range(UNITS))
        DVES = UNITS - ACTS
        ARGS = 2 + H

        def count(u):
            return sum(of_act(v) == of_act(u) for v in range(u + 1))

        def wait_out(eng, g, u):
            if u < 0:
                if not later(g):
                    return
                g, u = g - 1, u + UNITS
            eng.wait_ge(act_out if of_act(u) else dve_out, g * (ACTS if of_act(u) else DVES) + count(u))

        def groups(eng, body):
            body(0, 0)
            body(1, 1)
            with eng.Fori(1, NG // 2) as i:
                for k in range(2):
                    body(2 * i + k, k)
            body(NG - 1, (NG - 1) % 2)

        def unit_out(u, par):
            if u < 16:
                w, m, h = u // 8, u // 2 % 4, u % 2
                return qk[par][w][:, m, h * HALF:(h + 1) * HALF], ps[u % RING][:, 0:HALF]
            return vo[par][:, u - 16, :], ps[u % RING][:, 0:D]

        with nc.Block() as block:
            load_w, high_w, low_w = split_weights(
                [w.rearrange("(k p) n -> p k n", p=P) for w in (wq, wk, wv)], W,
                [s[:, :, :] for s in staging], w_loaded, w_high, w_low)

            @block.sync
            def _(sp):
                x_cols = xT.rearrange("(k p) t -> p k t", p=P)

                def load_x(g):
                    sp.dma_start(xraw[:, :, :], x_cols[:, :, col(g * GT, GT)]).then_inc(x_loaded, 16)

                def store(g, par):
                    for n, dst in ((0, q_d), (1, k_d)):
                        wait_apart(sp, act_out, g * ACTS + 4 * (n + 1), passed)
                        wait_apart(sp, dve_out, g * DVES + 4 * (n + 1), passed)
                        sp.dma_start(dst.rearrange("(m p) t -> p m t", p=P)[:, :, col(g * GT, GT)],
                                     qk[par][n][:, :, :]).then_inc(stored[par], 16)
                    wait_apart(sp, act_out, (g + 1) * ACTS, passed)
                    wait_apart(sp, dve_out, (g + 1) * DVES, passed)
                    sp.dma_start(v_d[col(g * GT, GT), :].rearrange("(i p) n -> p i n", p=P), vo[par][:, :, :])\
                      .then_inc(stored[par], 16)

                load_x(0)
                load_w(sp, [0, 1])
                for row, dst in ((w, wb), (v, vb)):
                    sp.dma_start(dst[:, :], row.rearrange("(a h) -> a h", a=1).broadcast_to([T, H]))\
                      .then_inc(wv_loaded, 16)
                load_w(sp, [2])

                def body(g, par):
                    if not later(g):
                        return
                    sp.wait_ge(x_low, g)
                    load_x(g)
                    store(g - 1, 1 - par)

                groups(sp, body)
                sp.wait_ge(rhat_done, 1)
                sp.dma_start(rhat_d.rearrange("t (h s) -> t h s", h=H), rhat[:, :, :]).then_inc(rhat_stored, 16)
                store(NG - 1, (NG - 1) % 2)
                sp.wait_ge(rhat_stored, 16)
                sp.wait_ge(stored[0], 48 * ((NG + 1) // 2))
                sp.wait_ge(stored[1], 48 * (NG // 2))

            @block.gpsimd
            def _(pool):
                def body(g, par):
                    if not later(g):
                        pool.iota(dist_i[:, :], [[-1, T]], base=0, channel_multiplier=1).then_inc(consts, 1)
                        return
                    pool.wait_ge(x_loaded, 16 * g + 16)
                    if not isinstance(g, int) or g > 1:
                        wait_apart(pool, unit_done, (g - 1) * UNITS, passed)
                    pool.tensor_copy(xs[par][0][:, :, :], xraw[:, :, :]).then_inc(x_high, 1)
                    pool.wait_ge(x_high, g)
                    pool.tensor_tensor(xs[par][1][:, :, :], xraw[:, :, :], xs[par][0][:, :, :].bitcast(F32),
                                       ALU.subtract).then_inc(x_low, 1)

                groups(pool, body)
                pool.wait_ge(rhat_step, 2 * QUADS + 1)
                pool.affine_select(out=rhat[:, :, :], in_=rhat[:, :, :], compare_op=ALU.is_ge, fill=-1.0,
                                   base=0, pattern=[[0, H], [-1, T]], channel_multiplier=1).then_inc(rhat_done, 1)

            @block.scalar
            def _(act):
                act.wait_ge(x_loaded, 16)
                for k in range(KD):
                    act.activation(xs[0][0][:, k, :], xraw[:, k, :], ACT.Copy).then_inc(first_high, 1)
                high_w(act)

                def table_exp(m):
                    if m == 0:
                        act.wait_ge(wv_loaded, 32)
                        act.activation(ev[:, :], vb[:, :], ACT.Exp).then_inc(arg_exp, 1)
                    act.wait_ge(arg_done, 2 + 4 * (m + 1))
                    heads = rhat[:, 4 * m:4 * m + 4, :]
                    act.activation(heads, heads, ACT.Exp).then_inc(arg_exp, 1)

                def body(g, par):
                    if not isinstance(g, int) or g > 1:
                        act.wait_ge(stored[par], 24 * (g - par))
                    for u in range(0, UNITS, 2):
                        dst, src = unit_out(u, par)
                        act.wait_ge(unit_done, g * UNITS + u + 1)
                        act.activation(dst, src, ACT.Copy).then_inc(act_out, 1)
                        if not later(g) and u % 4 == 2 and u // 4 < QUADS:
                            table_exp(u // 4)

                groups(act, body)

            @block.vector
            def _(dve):
                dve.wait_ge(x_loaded, 16)
                for k in range(KD):
                    dve.wait_ge(first_high, k + 1)
                    last = dve.tensor_tensor(xs[0][1][:, k, :], xraw[:, k, :], xs[0][0][:, k, :].bitcast(F32),
                                             ALU.subtract)
                last.then_inc(x_low, 1)
                low_w(dve)

                def table_arguments(m):
                    if m == 0:
                        dve.wait_ge(wv_loaded, 32)
                        dve.wait_ge(consts, 1)
                        dve.tensor_scalar(neg_w[:, :], wb[:, :], -1.0, None, ALU.mult).then_inc(arg_done, 1)
                        dve.tensor_scalar(dist[:, :], dist_i[:, :], 0.0, None, ALU.max).then_inc(arg_done, 1)
                        dve.wait_ge(arg_done, 2)
                    for h in range(4 * m, 4 * m + 4):
                        dve.tensor_scalar(rhat[:, h, :], dist[:, :], neg_w[:, h:h + 1], vb[:, h:h + 1],
                                          ALU.mult, ALU.add).then_inc(arg_done, 1)

                def table_rest(m):
                    heads, done = rhat[:, 4 * m:4 * m + 4, :], 2 * m
                    dve.wait_ge(arg_exp, m + 2)
                    if m == 0:
                        dve.tensor_scalar(ev[:, :], ev[:, :], 1.0, ISQ, ALU.add, ALU.mult).then_inc(rhat_step, 1)
                    dve.tensor_scalar(heads, heads, 1.0, None, ALU.add).then_inc(arg_done, 1)
                    dve.wait_ge(arg_done, ARGS + m + 1)
                    dve.reciprocal(heads, heads).then_inc(rhat_step, 1)
                    dve.wait_ge(rhat_step, done + 2)
                    dve.tensor_tensor(heads, heads, ev[:, 4 * m:4 * m + 4].unsqueeze(2).broadcast_to([T, 4, T]),
                                      ALU.mult).then_inc(rhat_step, 1)

                def body(g, par):
                    if not isinstance(g, int) or g > 1:
                        dve.wait_ge(stored[par], 24 * (g - par))
                    for u in range(1, UNITS, 2):
                        dst, src = unit_out(u, par)
                        dve.wait_ge(unit_done, g * UNITS + u + 1)
                        dve.tensor_copy(dst, src).then_inc(dve_out, 1)
                        if not later(g) and u // 4 < QUADS:
                            if u == 1:
                                for m in range(QUADS):
                                    table_arguments(m)
                            if u % 4 == 3:
                                table_rest(u // 4)

                groups(dve, body)

            @block.tensor
            def _(pe):
                def body(g, par):
                    pe.wait_ge(x_low, g + 1)
                    for u in range(UNITS):
                        wait_out(pe, g, u - RING)
                        if not later(g):
                            pe.wait_ge(w_low, KD * (min(u // 8, 2) + 1))
                        x = xs[par]
                        if u < 16:
                            w, m, h = u // 8, u // 2 % 4, u % 2
                            last = products(pe, ps[u % RING][:, 0:HALF], SPLIT, KD,
                                            lambda a, k: W[w][a][:, k, m * P:(m + 1) * P],
                                            lambda b, k: x[b][:, k, h * HALF:(h + 1) * HALF])
                        else:
                            i = u - 16
                            last = products(pe, ps[u % RING][:, 0:D], SPLIT, KD,
                                            lambda a, k: x[a][:, k, i * P:(i + 1) * P],
                                            lambda b, k: W[2][b][:, k, :])
                        last.then_inc(unit_done, 1)

                groups(pe, body)


def phase_self_attention(nc, sem, q_d, k_d, v_d, rhat_d, o_d, next_w, staging):
    PAIRS = B // 2
    PQ = 2 * QUADS
    STEPS = 2 * PQ
    with ExitStack() as ctx:
        def sb(name, shape, dt=F32):
            return ctx.enter_context(nc.sbuf_tensor("B_" + name, shape, dt))

        def psum(name):
            return ctx.enter_context(nc.psum_tensor("B_" + name, [P, 512], F32))

        qs = [sb(f"q{i}", [P, QUADS, 2, T]) for i in range(2)]
        kd = [sb(f"kdiag{i}", [P, QUADS, 4, 2, T]) for i in range(2)]
        vs = [sb(f"v{i}", [T, 2, D]) for i in range(2)]
        rhat = sb("rhat", [T, H, T])
        ident = sb("ident", [P, P])
        ident_r = sb("ident_r", [T, T], F32R)
        mask_raw = sb("mask_raw", [T, 4, T])
        mask = sb("mask", [T, 4, T], F32R)
        s_rel = [sb(f"s_rel{i}", [T, 4, T]) for i in range(4)]
        e = [sb(f"e{i}", [T, 4, T]) for i in range(4)]
        pn = [sb(f"pn{i}", [T, 4, T]) for i in range(2)]
        pT = [sb(f"pT{i}", [T, 4, T]) for i in range(2)]
        neg_max = sb("neg_max", [T, 4, 4])
        rowsum = sb("rowsum", [T, 4, 4])
        inv = sb("inv", [T, 4, 4])
        oo = [sb(f"o{i}", [P, 2, QUADS, 2, T]) for i in range(2)]
        ps_s = [psum(f"ps_s{i}") for i in range(2)]
        ps_t = [psum(f"ps_t{i}") for i in range(2)]
        ps_o = [psum(f"ps_o{i}") for i in range(2)]

        rhat_loaded, consts, zeroed = sem("B_rhat_loaded"), sem("B_consts"), sem("B_zeroed")
        w_loaded = sem("B_w_loaded")
        qk_loaded = [sem("B_qk_loaded0"), sem("B_qk_loaded1")]
        v_loaded = [sem("B_v_loaded0"), sem("B_v_loaded1")]
        s_done, rel_done, max_done = sem("B_s_done"), sem("B_rel_done"), sem("B_max_done")
        exp_done, inv_done, norm_done = sem("B_exp_done"), sem("B_inv_done"), sem("B_norm_done")
        t_done, pT_done, pv_done, o_done = sem("B_t_done"), sem("B_pT_done"), sem("B_pv_done"), sem("B_o_done")
        stored, passed = [sem("B_stored0"), sem("B_stored1")], sem("B_passed")

        def quads(eng, step):
            for k in range(2):
                for j in range(PQ):
                    step(k, k, PQ * k + j, PQ * k + j)
            with eng.Fori(1, PAIRS // 2) as i:
                for k in range(2):
                    for j in range(PQ):
                        step(2 * i + k, k, PQ * (2 * i + k) + j, PQ * k + j)

        def place(s):
            return s // PQ % 2, s // QUADS % 2, s % QUADS

        def started(n, back):
            return not (isinstance(n, int) and n < back)

        with nc.Block() as block:
            @block.sync
            def _(sp):
                q_rows = q_d.rearrange("(m p) t -> p m t", p=P)
                k_rows = k_d.rearrange("(m p) t -> p m t", p=P)
                o_rows = o_d.rearrange("(m p) t -> p m t", p=P)

                def of_pair(rows, p):
                    return rows[:, :, col(p * 2 * T, 2 * T)]

                def flat(buf):
                    return buf.rearrange("p m b t -> p m (b t)")

                def load_qk(p, par):
                    sp.dma_start(flat(qs[par][:, :, :, :]), of_pair(q_rows, p)).then_inc(qk_loaded[par], 16)
                    for j in range(4):
                        rows = slice(HD * j, HD * (j + 1))
                        sp.dma_start(flat(kd[par][rows, :, j, :, :]), of_pair(k_rows[rows, :, :], p))\
                          .then_inc(qk_loaded[par], 16)

                def load_v(p, par):
                    sp.dma_start(vs[par][:, :, :], v_d[col(p * 2 * T, 2 * T), :].rearrange("(b t) n -> t b n", b=2))\
                      .then_inc(v_loaded[par], 16)

                def store(p, par):
                    wait_apart(sp, o_done, PQ * (p + 1), passed)
                    for r in range(4):
                        rows = slice(HD * r, HD * (r + 1))
                        sp.dma_start(of_pair(o_rows[rows, :, :], p), flat(oo[par][rows, r % 2, :, :, :]))\
                          .then_inc(stored[par], 16)

                for p in range(2):
                    sp.wait_ge(zeroed, p + 1)
                    load_qk(p, p)
                    if p == 0:
                        sp.dma_start(rhat[:, :, :], rhat_d.rearrange("t (h s) -> t h s", h=H)).then_inc(rhat_loaded, 16)
                    load_v(p, p)
                for raw, dst in zip(next_w, staging):
                    sp.dma_start(dst[:, :, :], raw.rearrange("(k p) n -> p k n", p=P)).then_inc(w_loaded, 16)
                with sp.Fori(0, PAIRS // 2 - 1) as i:
                    for k in range(2):
                        p = 2 * i + k
                        sp.wait_ge(s_done, PQ * (p + 1))
                        load_qk(p + 2, k)
                        sp.wait_ge(pv_done, PQ * (p + 1))
                        load_v(p + 2, k)
                        store(p, k)
                for p in (PAIRS - 2, PAIRS - 1):
                    store(p, p % 2)
                for par in range(2):
                    sp.wait_ge(stored[par], 64 * (PAIRS // 2))
                sp.wait_ge(w_loaded, 32)

            @block.gpsimd
            def _(pool):
                for i in range(2):
                    pool.memset(kd[i][:, :, :, :, :], 0.0).then_inc(zeroed, 1)
                pool.memset(mask_raw[:, :, :], 0.0).then_inc(consts, 1)
                pool.memset(ident[:, :], 0.0).then_inc(consts, 1)
                pool.wait_ge(consts, 2)
                pool.affine_select(out=mask_raw[:, :, :], in_=mask_raw[:, :, :], compare_op=ALU.is_ge,
                                   fill=MASK, base=0, pattern=[[0, 4], [-1, T]], channel_multiplier=1)\
                    .then_inc(consts, 1)
                pool.affine_select(out=ident[:, :], in_=ident[:, :], compare_op=ALU.not_equal, fill=1.0,
                                   base=0, pattern=[[-1, P]], channel_multiplier=1).then_inc(consts, 1)

                def normalise(n, s):
                    pool.wait_ge(inv_done, n + 1)
                    pool.wait_ge(exp_done, 4 * n + 4)
                    wait(pool, t_done, n - 1)
                    pool.tensor_tensor(pn[s % 2][:, :, :], e[s % 4][:, :, :],
                                       inv[:, s % 4, :].unsqueeze(2).broadcast_to([T, 4, T]), ALU.mult)\
                        .then_inc(norm_done, 1)

                def step(p, par, n, s):
                    if started(n, 2):
                        normalise(n - 2, s - 2)

                quads(pool, step)
                for back in (2, 1):
                    normalise(QUADS * B - back, STEPS - back)

            LAG = 5

            @block.scalar
            def _(act):
                def exps(n, s):
                    act.wait_ge(rel_done, n + 1)
                    act.wait_ge(max_done, n + 1)
                    wait(act, norm_done, n - 3)
                    for j in range(4):
                        act.activation(e[s % 4][:, j, :], s_rel[s % 4][:, j, :], ACT.Exp,
                                       bias=neg_max[:, s % 4, j:j + 1],
                                       accum_out=rowsum[:, s % 4, j:j + 1]).then_inc(exp_done, 1)

                def take_result(p, n, s):
                    par, b, m = place(s)
                    act.wait_ge(pv_done, n + 1)
                    if s % PQ == 0 and not (isinstance(p, int) and p < 2):
                        act.wait_ge(stored[par], 32 * (p - par))
                    act.activation(oo[par][:, :, m, b, :], ps_o[m % 2][:, 0:2 * T].rearrange("p (a t) -> p a t", a=2),
                                   ACT.Copy).then_inc(o_done, 1)

                def step(p, par, n, s):
                    if started(n, LAG):
                        take_result(p if s % PQ >= LAG else p - 1, n - LAG, (s - LAG) % STEPS)
                    exps(n, s)

                quads(act, step)
                for back in range(LAG, 0, -1):
                    take_result(PAIRS - 1, QUADS * B - back, STEPS - back)

            @block.vector
            def _(dve):
                dve.wait_ge(consts, 4)
                dve.tensor_copy(mask[:, :, :], mask_raw[:, :, :]).then_inc(consts, 1)
                dve.tensor_copy(ident_r[:, :], ident[0:T, 0:T]).then_inc(consts, 1)
                dve.wait_ge(rhat_loaded, 16)

                def scale_max(n, s, m):
                    dve.wait_ge(s_done, n + 1)
                    wait(dve, exp_done, 4 * n - 12)
                    dve.scalar_tensor_tensor(
                        s_rel[s % 4][:, :, :], ps_s[s % 2][0:T, 0:QT].rearrange("p (j t) -> p j t", j=4), 0.0,
                        rhat[:, 4 * m:4 * m + 4, :], ALU.max, ALU.mult).then_inc(rel_done, 1)
                    dve.wait_ge(rel_done, n + 1)
                    wait(dve, exp_done, 4 * n - 12)
                    dve.tensor_reduce(neg_max[:, s % 4, :], s_rel[s % 4][:, :, :], AX.X, ALU.max, negate=True)\
                        .then_inc(max_done, 1)

                def invert(n, s):
                    dve.wait_ge(exp_done, 4 * n + 4)
                    wait(dve, norm_done, n - 3)
                    dve.reciprocal(inv[:, s % 4, :], rowsum[:, s % 4, :]).then_inc(inv_done, 1)

                def take_transposed(n, s):
                    dve.wait_ge(t_done, n + 1)
                    wait(dve, pv_done, n - 1)
                    dve.tensor_copy(pT[s % 2][:, :, :], ps_t[s % 2][0:T, 0:QT].rearrange("p (j t) -> p j t", j=4))\
                       .then_inc(pT_done, 1)

                def step(p, par, n, s):
                    scale_max(n, s, s % QUADS)
                    if started(n, 2):
                        invert(n - 2, s - 2)
                    if started(n, 4):
                        take_transposed(n - 4, s - 4)

                quads(dve, step)
                end = QUADS * B
                for back in range(4, 0, -1):
                    if back <= 2:
                        invert(end - back, STEPS - back)
                    take_transposed(end - back, STEPS - back)

            @block.tensor
            def _(pe):
                pe.wait_ge(consts, 6)

                def scores(p, par, n, s):
                    _, b, m = place(s)
                    if s % PQ == 0:
                        pe.wait_ge(qk_loaded[par], 40 * (p - par) + 80)
                    wait(pe, rel_done, n - 1)
                    pe.matmul(ps_s[s % 2][0:T, 0:QT], qs[par][:, m, b, :], kd[par][:, m, :, b, :], start=True, stop=False)
                    pe.matmul(ps_s[s % 2][0:T, 0:QT], ident_r[:, :], mask[:, :, :], start=False, stop=True)\
                      .then_inc(s_done, 1)

                def transposes(n, s):
                    pe.wait_ge(norm_done, n + 1)
                    wait(pe, pT_done, n - 1)
                    for j in range(4):
                        last = pe.transpose(ps_t[s % 2][0:T, j * T:(j + 1) * T], pn[s % 2][:, j, :], ident[0:T, 0:T])
                    last.then_inc(t_done, 1)

                def weighted_sum(p, n, s):
                    par, b, m = place(s)
                    if s % PQ == 0:
                        pe.wait_ge(v_loaded[par], 8 * (p - par) + 16)
                    pe.wait_ge(pT_done, n + 1)
                    wait(pe, o_done, n - 1)
                    for g in range(2):
                        c = (2 * m + g) * 2 * HD
                        last = pe.matmul(ps_o[m % 2][2 * HD * g:2 * HD * (g + 1), 0:2 * T], vs[par][:, b, c:c + 2 * HD],
                                         pT[s % 2][:, 2 * g:2 * g + 2, :], start=True, stop=True,
                                         tile_position=(0, 2 * HD * g))
                    last.then_inc(pv_done, 1)

                def step(p, par, n, s):
                    scores(p, par, n, s)
                    if started(n, 4):
                        transposes(n - 4, s - 4)
                    if started(n, 5):
                        weighted_sum(p if s % PQ >= 5 else p - 1, n - 5, (s - 5) % STEPS)

                quads(pe, step)
                end = QUADS * B
                for back in range(5, 0, -1):
                    if back <= 4:
                        transposes(end - back, STEPS - back)
                    weighted_sum(PAIRS - 1, end - back, STEPS - back)


def phase_norm_and_queries(nc, sem, o_d, x, W, bo, bq, x1_d, cq_d, raws, next_w, staging, w_gate, w_up, w_down, biggest):
    QU = KD * 2
    with ExitStack() as ctx:
        def sb(name, shape, dt=F32):
            return ctx.enter_context(nc.sbuf_tensor("C_" + name, shape, dt))

        def psum(name):
            return ctx.enter_context(nc.psum_tensor("C_" + name, [P, 512], F32))

        bo_b, bq_c = sb("bo_b", [P, D]), sb("bq_c", [P, KD])
        oraw, os = sb("oraw", [P, KD, GT]), Split(sb, "o", [P, KD, GT])
        xb = sb("xb", [P, TT, D])
        r = [sb(f"r{i}", [P, D]) for i in range(2)]
        stats = [sb(f"stats{i}", [P, 6]) for i in range(2)]
        mv = [sb(f"mv{i}", [P, 2]) for i in range(2)]
        var_eps = [sb(f"var_eps{i}", [P, 1]) for i in range(2)]
        rstd = [sb(f"rstd{i}", [P, 1]) for i in range(2)]
        minus_half = sb("minus_half", [P, 1])
        x1 = sb("x1", [P, TT, D])
        x1s = Split(sb, "x1s", [P, KD, GT])
        qf = [sb(f"qf{i}", [P, HALF]) for i in range(4)]
        qo = Split(sb, "qo", [P, KD, GT])
        ident = sb("ident", [P, P])
        ints = [sb(f"ints{j}", [P, F], I32) for j in range(3)]
        piece_max = sb("piece_max", [P, 3])
        ps_y = [psum(f"ps_y{i}") for i in range(2)]
        ps_t = [psum(f"ps_t{i}") for i in range(2)]
        ps_q = [psum(f"ps_q{i}") for i in range(4)]

        b_loaded, consts = sem("C_b_loaded"), sem("C_consts")
        w_loaded = [sem("C_w_loaded0"), sem("C_w_loaded1")]
        w_high, w_low = sem("C_w_high"), sem("C_w_low")
        o_loaded = [sem(f"C_o_loaded{k}") for k in range(KD)]
        o_high, o_low = sem("C_o_high"), sem("C_o_low")
        x_loaded, xb_done = sem("C_x_loaded"), sem("C_xb_done")
        y_done, r_done, stat_done, mv_done, eps_done = (sem("C_" + n) for n in
                                                        ("y_done", "r_done", "stat_done", "mv_done", "eps_done"))
        rstd_done, x1_done, x1_stored = sem("C_rstd_done"), sem("C_x1_done"), sem("C_x1_stored")
        t_done, th_done, tl_done = sem("C_t_done"), sem("C_th_done"), sem("C_tl_done")
        q_done, qf_done, qh_done, ql_done = sem("C_q_done"), sem("C_qf_done"), sem("C_qh_done"), sem("C_ql_done")
        q_stored, passed = sem("C_q_stored"), sem("C_passed")
        int_loaded, int_max = [sem(f"C_int_loaded{j}") for j in range(3)], sem("C_int_max")
        biggest_done = sem("C_biggest_done")
        assert KD <= NG - 1

        def former(n, i):
            return n if i == 0 else n - 1

        with nc.Block() as block:
            load_w, high_w, low_w = split_weights([r.rearrange("(k p) n -> p k n", p=P) for r in raws], W + next_w,
                                                  [t[:, :, :] for t in staging], w_loaded, w_high, w_low, present=2)

            @block.sync
            def _(sp):
                def load_o(g):
                    if later(g):
                        sp.wait_ge(o_low, KD * g)
                    for k in range(KD):
                        sp.dma_start(oraw[:, k, :], o_d.rearrange("(k p) t -> p k t", p=P)[:, k, col(g * GT, GT)])\
                          .then_inc(o_loaded[k], 16)

                def load_x(g):
                    if later(g):
                        sp.wait_ge(r_done, TT * g)
                    sp.dma_start(xb[:, :, :], x[col(g * GT, GT), :].rearrange("(i p) n -> p i n", p=P))\
                      .then_inc(x_loaded, 16)

                def store(g):
                    wait_apart(sp, x1_done, TT * (g + 1), passed)
                    sp.dma_start(x1_d[col(g * GT, GT), :].rearrange("(i p) n -> p i n", p=P), x1[:, :, :])\
                      .then_inc(x1_stored, 16)

                def store_q(g):
                    for m in range(KD):
                        for done in (ql_done, qh_done):
                            wait_apart(sp, done, QU * g + 2 * (m + 1), passed)
                        for part in range(2):
                            sp.dma_start(cq_d[part].rearrange("(m p) t -> p m t", p=P)[:, m, col(g * GT, GT)],
                                         qo[part][:, m, :].bitcast(F32)).then_inc(q_stored, 16)

                def load_ints(g):
                    for j, w in enumerate((w_gate, w_up, w_down)):
                        if later(g):
                            sp.wait_ge(biggest_done, 3 * (g - 1) + j + 1)
                        if j < 2:
                            src, dst = w[col(g * P, P), :], ints[j][:, :]
                        else:
                            src = w[col(g * (KF // KD * P), KF // KD * P), :].rearrange("(a p) n -> p a n", p=P)
                            dst = ints[j][:, :].rearrange("p (a n) -> p a n", n=D)
                        sp.dma_start(dst, src).then_inc(int_loaded[j], 16)

                load_o(0)
                load_x(0)
                sp.dma_start(bo_b[:, :], bo.rearrange("(a n) -> a n", a=1).broadcast_to([P, D])).then_inc(b_loaded, 16)
                sp.dma_start(bq_c[:, :], bq).then_inc(b_loaded, 16)
                load_o(1)
                store(0)
                load_x(1)
                load_o(2)
                load_w(sp, [2, 3])
                load_ints(0)

                def body(g, ahead_x=True, ahead_o=True):
                    store(g + 1)
                    if ahead_x:
                        load_x(g + 2)
                    if ahead_o:
                        load_o(g + 3)
                    store_q(g)
                    if ahead_x:
                        load_ints(g + 1)

                with sp.Fori(0, NG - 3) as g:
                    body(g)
                body(NG - 3, ahead_o=False)
                body(NG - 2, ahead_x=False, ahead_o=False)
                store_q(NG - 1)
                sp.wait_ge(x1_stored, 16 * NG)
                sp.wait_ge(q_stored, 128 * NG)

            def low_o(eng, g, k):
                eng.wait_ge(o_high, KD * g + k + 1)
                eng.wait_ge(o_loaded[k], 16 * g + 16)
                if later(g):
                    eng.wait_ge(y_done, TT * g)
                eng.tensor_tensor(os[1][:, k, :], oraw[:, k, :], os[0][:, k, :].bitcast(F32),
                                  ALU.subtract).then_inc(o_low, 1)

            @block.gpsimd
            def _(pool):
                pool.memset(minus_half[:, :], -0.5).then_inc(consts, 1)
                pool.memset(ident[:, :], 0.0).then_inc(consts, 1)
                pool.wait_ge(consts, 2)
                pool.affine_select(out=ident[:, :], in_=ident[:, :], compare_op=ALU.not_equal, fill=1.0,
                                   base=0, pattern=[[-1, P]], channel_multiplier=1).then_inc(consts, 1)
                pool.wait_ge(b_loaded, 32)

                def add_bias(g, i):
                    if i == 0:
                        pool.wait_ge(x_loaded, 16 * g + 16)
                    pool.tensor_tensor(xb[:, i, :], xb[:, i, :], bo_b[:, :], ALU.add).then_inc(xb_done, 1)

                def norms(g):
                    add_bias(g, 0)
                    add_bias(g, 1)
                    for i in range(TT):
                        n, s = TT * g + i, i % 2
                        pool.wait_ge(eps_done, n + 1)
                        wait(pool, x1_done, former(n, i))
                        pool.tensor_tensor(rstd[s][:, :], var_eps[s][:, :], minus_half[:, :], ALU.pow)\
                            .then_inc(rstd_done, 1)
                        if i + 2 < TT:
                            add_bias(g, i + 2)

                def low_q(g, u):
                    n = QU * g + u
                    pool.wait_ge(qh_done, n + 1)
                    pool.wait_ge(qf_done, n + 1)
                    if later(g) and u == 0:
                        pool.wait_ge(q_stored, 128 * g)
                    pool.tensor_tensor(qo[1][:, u // 2, u % 2 * HALF:(u % 2 + 1) * HALF], qf[u % 4][:, :],
                                       qo[0][:, u // 2, u % 2 * HALF:(u % 2 + 1) * HALF].bitcast(F32),
                                       ALU.subtract).then_inc(ql_done, 1)

                def body(g, ahead=True):
                    norms(g + 1)
                    for u in range(QU):
                        low_q(g, u)
                        if ahead and u % 2 == 0 and u // 2 < KD // 2:
                            low_o(pool, g + 2, u // 2)

                norms(0)
                body(0)
                with pool.Fori(1, NG - 2) as g:
                    body(g)
                body(NG - 2, ahead=False)
                for u in range(QU):
                    low_q(NG - 1, u)

            @block.scalar
            def _(act):
                def high_o(g):
                    for k in range(KD):
                        act.wait_ge(o_loaded[k], 16 * g + 16)
                        if later(g) and k == 0:
                            act.wait_ge(y_done, TT * g)
                        act.activation(os[0][:, k, :], oraw[:, k, :], ACT.Copy).then_inc(o_high, 1)

                def high_x1(g):
                    for i in range(TT):
                        n = TT * g + i
                        act.wait_ge(t_done, n + 1)
                        if later(g) and i == 0:
                            act.wait_ge(q_done, QU * g)
                        act.activation(x1s[0][:, :, i * P:(i + 1) * P],
                                       ps_t[i % 2][:, :].rearrange("p (k c) -> p k c", k=KD), ACT.Copy)\
                           .then_inc(th_done, 1)

                def high_q(g):
                    for u in range(QU):
                        act.wait_ge(qf_done, QU * g + u + 1)
                        if later(g) and u == 0:
                            act.wait_ge(q_stored, 128 * g)
                        act.activation(qo[0][:, u // 2, u % 2 * HALF:(u % 2 + 1) * HALF], qf[u % 4][:, :], ACT.Copy)\
                           .then_inc(qh_done, 1)

                def body(g, ahead=True):
                    high_x1(g)
                    if ahead:
                        high_o(g + 2)
                    high_q(g)

                high_w(act, [0])
                high_o(0)
                high_w(act, [1])
                high_o(1)
                body(0)
                high_w(act, [2, 3])
                with act.Fori(1, NG - 2) as g:
                    body(g)
                body(NG - 2, ahead=False)
                high_x1(NG - 1)
                high_q(NG - 1)

            @block.vector
            def _(dve):
                def normalise(n, i, s):
                    dve.wait_ge(rstd_done, n + 1)
                    dve.tensor_scalar(x1[:, i, :], r[s][:, :], mv[s][:, 0:1], rstd[s][:, 0:1],
                                      ALU.subtract, ALU.mult).then_inc(x1_done, 1)

                def norm_tile(g, i):
                    n, s = TT * g + i, i % 2
                    dve.wait_ge(y_done, n + 1)
                    dve.wait_ge(xb_done, n + 1)
                    wait(dve, x1_done, former(n, i))
                    dve.tensor_tensor(r[s][:, :], ps_y[s][:, :], xb[:, i, :], ALU.add).then_inc(r_done, 1)
                    dve.wait_ge(r_done, n + 1)
                    dve.bn_stats(stats[s][:, :], r[s][:, :]).then_inc(stat_done, 1)
                    wait_apart(dve, stat_done, n + 1, passed)
                    dve.bn_aggr(mv[s][:, :], stats[s][:, :]).then_inc(mv_done, 1)
                    dve.wait_ge(mv_done, n + 1)
                    dve.tensor_scalar(var_eps[s][:, :], mv[s][:, 1:2], EPS, None, ALU.add).then_inc(eps_done, 1)
                    if later(g) and i == 1:
                        dve.wait_ge(x1_stored, 16 * g)
                    if i:
                        normalise(n - 1, i - 1, 1 - s)
                    if i == TT - 1:
                        normalise(n, i, s)

                def low_x1(g, i):
                    n = TT * g + i
                    dve.wait_ge(t_done, n + 1)
                    dve.wait_ge(th_done, n + 1)
                    dve.tensor_tensor(x1s[1][:, :, i * P:(i + 1) * P],
                                      ps_t[i % 2][:, :].rearrange("p (k c) -> p k c", k=KD),
                                      x1s[0][:, :, i * P:(i + 1) * P].bitcast(F32), ALU.subtract)\
                       .then_inc(tl_done, 1)

                def look_at_ints(g, j):
                    dve.wait_ge(int_loaded[j], 16 * g + 16)
                    if not later(g):
                        dve.tensor_reduce(biggest[:, j:j + 1], ints[j][:, :], AX.X, ALU.max,
                                          apply_absolute_value=True).then_inc(biggest_done, 1)
                        return
                    dve.tensor_reduce(piece_max[:, j:j + 1], ints[j][:, :], AX.X, ALU.max,
                                      apply_absolute_value=True).then_inc(int_max, 1)
                    dve.wait_ge(int_max, 3 * (g - 1) + j + 1)
                    dve.wait_ge(biggest_done, 3 * (g - 1) + j + 1)
                    dve.tensor_tensor(biggest[:, j:j + 1], biggest[:, j:j + 1], piece_max[:, j:j + 1], ALU.max)\
                       .then_inc(biggest_done, 1)

                def scale_q(g, ahead=True):
                    for u in range(QU):
                        if ahead and u % 2 == 0 and u // 2 >= KD // 2:
                            low_o(dve, g + 2, u // 2)
                        if u in (1, 3, 5) and not (isinstance(g, int) and g >= KD):
                            look_at_ints(g, u // 2)
                        n = QU * g + u
                        dve.wait_ge(q_done, n + 1)
                        wait(dve, ql_done, n - 3)
                        dve.tensor_scalar(qf[u % 4][:, :], ps_q[u % 4][:, 0:HALF], bq_c[:, u // 2:u // 2 + 1], ISQ,
                                          ALU.add, ALU.mult).then_inc(qf_done, 1)

                def body(g, ahead=True):
                    for i in range(TT):
                        low_x1(g, i)
                        norm_tile(g + 1, i)
                    scale_q(g, ahead)

                low_w(dve, [0])
                for k in range(KD):
                    low_o(dve, 0, k)
                low_w(dve, [1])
                for i in range(TT):
                    if i == TT - 1:
                        for k in range(KD):
                            low_o(dve, 1, k)
                    norm_tile(0, i)
                dve.wait_ge(b_loaded, 32)
                body(0)
                low_w(dve, [2, 3])
                with dve.Fori(1, NG - 2) as g:
                    body(g)
                body(NG - 2, ahead=False)
                for i in range(TT):
                    low_x1(NG - 1, i)
                scale_q(NG - 1, ahead=False)

            @block.tensor
            def _(pe):
                def project_o(g, i):
                    if i == 0:
                        pe.wait_ge(o_low, KD * (g + 1))
                    n = TT * g + i
                    wait(pe, r_done, former(n, i))
                    products(pe, ps_y[i % 2][:, :], SPLIT, KD,
                             lambda a, k: os[a][:, k, i * P:(i + 1) * P],
                             lambda b, k: W[0][b][:, k, :]).then_inc(y_done, 1)

                def transpose_x1(g, i):
                    n = TT * g + i
                    pe.wait_ge(x1_done, n + 1)
                    wait(pe, tl_done, former(n, i))
                    for k in range(KD):
                        last = pe.transpose(ps_t[i % 2][:, k * P:(k + 1) * P], x1[:, i, k * P:(k + 1) * P],
                                            ident[:, :])
                    last.then_inc(t_done, 1)

                def project_q(g):
                    pe.wait_ge(tl_done, TT * (g + 1))
                    for u in range(QU):
                        n, m, h = QU * g + u, u // 2, u % 2
                        wait(pe, qf_done, n - 3)
                        products(pe, ps_q[u % 4][:, 0:HALF], SPLIT, KD,
                                 lambda a, k: W[1][a][:, k, m * P:(m + 1) * P],
                                 lambda b, k: x1s[b][:, k, h * HALF:(h + 1) * HALF]).then_inc(q_done, 1)

                def body(g):
                    for i in range(TT):
                        transpose_x1(g, i)
                        project_o(g + 1, i)
                    if not later(g):
                        pe.wait_ge(w_low, 2 * KD)
                    project_q(g)

                pe.wait_ge(w_low, KD)
                pe.wait_ge(consts, 3)
                for i in range(TT):
                    project_o(0, i)
                body(0)
                with pe.Fori(1, NG - 1) as g:
                    body(g)
                for i in range(TT):
                    transpose_x1(NG - 1, i)
                project_q(NG - 1)


def phase_cross_attention(nc, sem, ctxT, cq_d, W, bk, bv, o_d):
    ST = -(-S // P)
    LAST = S - (ST - 1) * P
    KC = (S // 2 + 1, S // 2 - 1)
    SH = S // 2
    PAIRS = H // 2
    KU = 2 * QUADS
    U = KU + ST
    assert U <= H
    with ExitStack() as ctx:
        def sb(name, shape, dt=F32):
            return ctx.enter_context(nc.sbuf_tensor("D_" + name, shape, dt))

        craw = [sb(f"craw{i}", [P, S]) for i in range(2)]
        cs = [Split(sb, f"ctx{i}", [P, KD, S]) for i in range(2)]
        ks = [sb(f"keys{i}", [P, PAIRS, S], F32R) for i in range(2)]
        vs = [sb(f"values{i}", [P, ST, D]) for i in range(2)]
        qs = sb("queries", [P, PAIRS, 2, 2, T], F32R)
        e = [sb(f"e{i}", [T, ST * P]) for i in range(4)]
        pT = [sb(f"pT{i}", [P, ST, QT]) for i in range(2)]
        oo = [sb(f"o{i}", [P, QUADS, 2 * T]) for i in range(2)]
        bk_c, bv_c = sb("bk_c", [P, KD]), sb("bv_c", [P, KD])
        neg_max, rowsum, inv = (sb(n, [T, 4]) for n in ("neg_max", "rowsum", "inv"))
        ident = sb("ident", [P, P])
        ps_s = [ctx.enter_context(nc.psum_tensor(f"D_ps_s{i}", [P, 1024], F32)) for i in range(2)]
        ps_t = [ctx.enter_context(nc.psum_tensor(f"D_ps_t{i}", [P, 512], F32)) for i in range(2)]
        ps_p = [ctx.enter_context(nc.psum_tensor(f"D_ps_p{i}", [P, 512], F32)) for i in range(2)]

        b_loaded, consts = sem("D_b_loaded"), sem("D_consts")
        c_loaded = [sem("D_c_loaded0"), sem("D_c_loaded1")]
        first_loaded = [sem(f"D_first_loaded{k}") for k in range(KD)]
        c_high, c_low = sem("D_c_high"), sem("D_c_low")
        q_loaded = [sem("D_q_loaded0"), sem("D_q_loaded1")]
        u_done, kh_done, kl_done, v_done = sem("D_u_done"), sem("D_kh_done"), sem("D_kl_done"), sem("D_v_done")
        s_done, max_done, exp_done = sem("D_s_done"), sem("D_max_done"), sem("D_exp_done")
        inv_done, norm_done, t_done = sem("D_inv_done"), sem("D_norm_done"), sem("D_t_done")
        taken, pv_done, o_done = sem("D_taken"), sem("D_pv_done"), sem("D_o_done")
        stored, passed = [sem("D_stored0"), sem("D_stored1")], sem("D_passed")

        def both_banks(s):
            t = ps_s[s % 2][0:T, :]
            return bass.AP(t.tensor, t.offset, [list(t.ap[0]), [513, 2], [1, SH]])

        def batches(eng, step):
            for b in range(2):
                for h in range(H):
                    step(b, b, h)
            with eng.Fori(1, B // 2 - 1) as i:
                for k in range(2):
                    for h in range(H):
                        step(2 * i + k, k, h)
            for b in (B - 2, B - 1):
                for h in range(H):
                    step(b, b % 2, h)

        def bank(u):
            return (u + u // 4) % 2

        def bank_of_quad(h):
            return (h + h // 4 + 1) % 2 if h < U else 1

        def unit_here(b, h):
            return h < U and not (isinstance(b, int) and b == B - 1)

        def started(n, back):
            return not (isinstance(n, int) and n < back)

        with nc.Block() as block:
            spare = vs[1][:, :, :].rearrange("p a n -> p (a n)")
            first_raw = [craw[0][:, :], craw[1][:, :], spare[:, 0:S], spare[:, S:2 * S]]
            assert 2 * S <= (ST - 1) * D

            @block.sync
            def _(sp):
                c_rows = ctxT.rearrange("b (k p) t -> b p k t", p=P)
                o_rows = o_d.rearrange("(m p) t -> p m t", p=P)
                q_rows = cq_d.rearrange("a (g j r) t -> r j g a t", j=2, r=HD)

                def load_ctx(b):
                    for k in range(KD):
                        n = KD * b + k
                        wait(sp, c_low, n - 1)
                        src = c_rows[b, :, k, :] if isinstance(b, int) else \
                            c_rows[bass.ds(b, 1), :, k, :].rearrange("a p t -> (a p) t")
                        sp.dma_start(craw[k % 2][:, :], src).then_inc(c_loaded[k % 2], 16)

                def load_q(b, half):
                    g = slice(PAIRS // 2 * half, PAIRS // 2 * (half + 1))
                    for c in range(2):
                        for j in range(2):
                            rows = slice(HD * (j + 2 * c), HD * (j + 2 * c + 1))
                            for a in range(2):
                                sp.dma_start(qs[rows, g, j, a, :].bitcast(F32),
                                             q_rows[:, j, g, a, col(b * T, T)]).then_inc(q_loaded[half], 16)

                def store(b, par):
                    wait_apart(sp, o_done, QUADS * (b + 1), passed)
                    for r in range(4):
                        sp.dma_start(o_rows[HD * r:HD * r + HD, :, col(b * T, T)],
                                     oo[par][HD * r:HD * r + HD, :, (r % 2) * T:(r % 2) * T + T])\
                          .then_inc(stored[par], 16)

                for k in range(KD):
                    sp.dma_start(first_raw[k], c_rows[0, :, k, :]).then_inc(first_loaded[k], 16)
                sp.dma_start(bk_c[:, :], bk).then_inc(b_loaded, 16)
                sp.dma_start(bv_c[:, :], bv).then_inc(b_loaded, 16)
                sp.wait_ge(consts, 2)
                load_q(0, 0)
                load_q(0, 1)
                load_ctx(1)

                def body(b, par, first, last):
                    if not first:
                        sp.wait_ge(s_done, H * b)
                        load_q(b, 1)
                    if not last:
                        load_ctx(b + 2)
                    if not first:
                        store(b - 1, 1 - par)
                    if not (isinstance(b, int) and b == B - 1):
                        sp.wait_ge(s_done, H * b + H // 2)
                        load_q(b + 1, 0)

                body(0, 0, True, False)
                body(1, 1, False, False)
                with sp.Fori(1, B // 2 - 1) as i:
                    for k in range(2):
                        body(2 * i + k, k, False, False)
                body(B - 2, 0, False, True)
                body(B - 1, 1, False, True)
                store(B - 1, 1)
                for par in range(2):
                    sp.wait_ge(stored[par], 64 * (B // 2))

            @block.gpsimd
            def _(pool):
                pool.memset(ident[:, :], 0.0).then_inc(consts, 1)
                pool.memset(qs[:, :, :, :, :].bitcast(F32), 0.0).then_inc(consts, 1)
                pool.wait_ge(consts, 2)
                pool.affine_select(out=ident[:, :], in_=ident[:, :], compare_op=ALU.not_equal, fill=1.0,
                                   base=0, pattern=[[-1, P]], channel_multiplier=1).then_inc(consts, 1)
                for i in range(4):
                    pool.memset(e[i][:, S:ST * P], 0.0).then_inc(consts, 1)
                for i in range(2):
                    pool.memset(vs[i][:, ST - 1, :], 0.0).then_inc(consts, 1)

                def split(b, par):
                    for k in range(KD):
                        n = KD * b + k
                        if k == 0:
                            wait(pool, u_done, U * (b - 1))
                        wait_apart(pool, c_loaded[k % 2], 32 * (b - 1) + 16 * (k // 2) + 16, passed)
                        pool.tensor_copy(cs[par][0][:, k, :], craw[k % 2][:, :]).then_inc(c_high, 1)
                        pool.wait_ge(c_high, n + 1)
                        pool.tensor_tensor(cs[par][1][:, k, :], craw[k % 2][:, :],
                                           cs[par][0][:, k, :].bitcast(F32), ALU.subtract).then_inc(c_low, 1)

                pool.wait_ge(c_low, KD)
                split(1, 1)
                with pool.Fori(1, B // 2) as i:
                    for k in range(2):
                        split(2 * i + k, k)

            def key_rows(u):
                return ((2 * (u // 2), slice(0, 64), slice(64, P)), (2 * (u // 2) + 1, slice(64, P), slice(0, 64)))

            def key_cols(u):
                return (0, KC[0]) if u % 2 == 0 else (KC[0], S)

            @block.scalar
            def _(act):
                def unit(b, par, u):
                    act.wait_ge(u_done, U * b + u + 1)
                    if u < KU:
                        c0, c1 = key_cols(u)
                        for pair, rows, _ in key_rows(u):
                            if u == 0:
                                wait(act, s_done, H * (b - 1))
                            act.activation(ks[par][rows, pair, c0:c1], ps_p[bank(u)][rows, 0:c1 - c0], ACT.Identity,
                                           bias=bk_c[rows, u // 2:u // 2 + 1]).then_inc(kh_done, 1)
                        return
                    i = u - KU
                    rows = P if i < ST - 1 else LAST
                    if i == 0:
                        wait(act, pv_done, QUADS * (b - 1))
                    act.activation(vs[par][0:rows, i, :], ps_p[bank(u)][0:rows, 0:D], ACT.Copy).then_inc(v_done, 1)

                def take_tiles(b, h):
                    n, quad = H * b + h, QUADS * b + h // 4
                    for half in range(2):
                        act.wait_ge(t_done, 2 * n + 1 + half)
                        if h % 4 == 0 and half == 0:
                            wait(act, pv_done, quad - 1)
                        act.activation(pT[h // 4 % 2][:, 3 * half:3 * half + 3, h % 4 * T:(h % 4 + 1) * T],
                                       ps_t[half][:, 0:3 * T].rearrange("p (a t) -> p a t", a=3),
                                       ACT.Copy).then_inc(taken, 1)

                def exps(n, h):
                    act.wait_ge(max_done, n + 1)
                    act.wait_ge(s_done, n + 1)
                    wait(act, t_done, 2 * n - 6)
                    wait(act, inv_done, n - 3)
                    act.activation(e[h % 4][:, 0:S].rearrange("p (a b) -> p a b", a=2), both_banks(h), ACT.Exp,
                                   bias=neg_max[:, h % 4:h % 4 + 1],
                                   accum_out=rowsum[:, h % 4:h % 4 + 1]).then_inc(exp_done, 1)

                def step(b, par, h):
                    exps(H * b + h, h)
                    if unit_here(b, h):
                        unit(b + 1, 1 - par, h)
                    if started(H * b + h, 2):
                        take_tiles(b, h - 2)

                def high_ctx(k):
                    act.wait_ge(first_loaded[k], 16)
                    act.activation(cs[0][0][:, k, :], first_raw[k], ACT.Copy).then_inc(c_high, 1)

                for k in range(KD):
                    high_ctx(k)
                act.wait_ge(b_loaded, 32)
                act.wait_ge(consts, 9)
                for u in range(U):
                    unit(0, 0, u)
                batches(act, step)
                take_tiles(B - 1, H - 2)
                take_tiles(B - 1, H - 1)

            @block.vector
            def _(dve):
                def unit(b, par, u):
                    if u >= KU:
                        return
                    c0, c1 = key_cols(u)
                    for i, (pair, rows, low_rows) in enumerate(key_rows(u)):
                        dve.wait_ge(kh_done, 2 * (KU * b + u) + i + 1)
                        dve.wait_ge(u_done, U * b + u + 1)
                        if u == 0:
                            wait(dve, s_done, H * (b - 1))
                        dve.scalar_tensor_tensor(
                            ks[par][low_rows, pair, c0:c1], ps_p[bank(u)][rows, 0:c1 - c0], bk_c[rows, u // 2:u // 2 + 1],
                            ks[par][rows, pair, c0:c1].bitcast(F32), ALU.add, ALU.subtract).then_inc(kl_done, 1)

                def maximum(n, h):
                    dve.wait_ge(s_done, n + 1)
                    wait(dve, exp_done, n - 3)
                    dve.tensor_reduce(neg_max[:, h % 4:h % 4 + 1], both_banks(h), AX.XY, ALU.max, negate=True)\
                       .then_inc(max_done, 1)

                def normalise(n, h):
                    dve.wait_ge(exp_done, n + 1)
                    wait(dve, norm_done, n - 3)
                    dve.reciprocal(inv[:, h % 4:h % 4 + 1], rowsum[:, h % 4:h % 4 + 1]).then_inc(inv_done, 1)
                    dve.wait_ge(inv_done, n + 1)
                    dve.tensor_scalar(e[h % 4][:, 0:S], e[h % 4][:, 0:S], inv[:, h % 4:h % 4 + 1], None, ALU.mult)\
                       .then_inc(norm_done, 1)

                def take_result(b, par, m, at):
                    dve.wait_ge(pv_done, QUADS * b + m + 1)
                    if m == 0:
                        wait(dve, stored[par], 32 * (b - par))
                    dve.tensor_scalar(oo[par][:, m, :], ps_p[bank_of_quad(at)][:, 0:2 * T], bv_c[:, m:m + 1], None, ALU.add)\
                       .then_inc(o_done, 1)

                def step(b, par, h):
                    n = H * b + h
                    if h > 0 and unit_here(b, h - 1):
                        unit(b + 1, 1 - par, h - 1)
                    maximum(n, h)
                    if started(n, 1):
                        normalise(n - 1, h - 1)
                    if h % 4 == 0 and started(n, 8):
                        if h > 4:
                            take_result(b, par, h // 4 - 2, h - 1)
                        else:
                            take_result(b - 1, 1 - par, QUADS - 2 + h // 4, (h - 1) % H)

                def low_ctx(k):
                    dve.wait_ge(c_high, k + 1)
                    dve.wait_ge(first_loaded[k], 16)
                    dve.tensor_tensor(cs[0][1][:, k, :], first_raw[k], cs[0][0][:, k, :].bitcast(F32),
                                      ALU.subtract).then_inc(c_low, 1)

                for k in range(KD):
                    low_ctx(k)
                dve.wait_ge(b_loaded, 32)
                dve.wait_ge(consts, 9)
                for u in range(U):
                    unit(0, 0, u)
                batches(dve, step)
                normalise(H * B - 1, H - 1)
                take_result(B - 1, 1, QUADS - 2, H - 1)
                take_result(B - 1, 1, QUADS - 1, 3)

            @block.tensor
            def _(pe):
                def unit_read(b, u):
                    if 0 <= u < KU:
                        pe.wait_ge(kl_done, 2 * (KU * b + u + 1))
                    else:
                        wait(pe, v_done, ST * b + max(u - KU + 1, 0))

                def unit(b, par, u):
                    if u == 0:
                        pe.wait_ge(c_low, KD * (b + 1))
                    unit_read(b, u - (1 if u % 4 == 0 else 2))
                    if u % 4 == 1:
                        wait(pe, o_done, QUADS * (b - 1) - 1 + u // 4)
                    c = cs[par]
                    if u < KU:
                        m, (c0, c1) = u // 2, key_cols(u)
                        last = products(pe, ps_p[bank(u)][:, 0:c1 - c0], SPLIT, KD,
                                        lambda a, k: W[0][a][:, k, m * P:(m + 1) * P],
                                        lambda a, k: c[a][:, k, c0:c1])
                    else:
                        i = u - KU
                        rows = P if i < ST - 1 else LAST
                        last = products(pe, ps_p[bank(u)][0:rows, 0:D], SPLIT, KD,
                                        lambda a, k: c[a][:, k, i * P:i * P + rows],
                                        lambda a, k: W[1][a][:, k, :])
                    last.then_inc(u_done, 1)

                def scores(b, par, n, h):
                    if h == 0:
                        pe.wait_ge(kl_done, 2 * KU * (b + 1))
                    if h % (H // 2) == 0:
                        pe.wait_ge(q_loaded[h // (H // 2)], 128 * (b + 1))
                    wait(pe, exp_done, n - 1)
                    g, j = h // 2, h % 2
                    for half, (c0, c1) in enumerate(((0, KC[0]), (S - KC[0], S))):
                        for a in range(2):
                            last = pe.matmul(ps_s[h % 2][0:T, 512 * half:512 * half + c1 - c0],
                                             qs[:, g, j, a, :], ks[par][:, g, c0:c1],
                                             start=(a == 0), stop=(a == 1))
                    last.then_inc(s_done, 1)

                def transposes(n, h):
                    pe.wait_ge(norm_done, n + 1)
                    for half in range(2):
                        wait(pe, taken, 2 * n - 1 + half)
                        for i in range(3):
                            t = 3 * half + i
                            last = pe.transpose(ps_t[half][:, i * T:(i + 1) * T], e[h % 4][:, t * P:(t + 1) * P],
                                                ident[0:T, 0:T])
                        last.then_inc(t_done, 1)

                def weighted_sum(b, par, m, at):
                    quad = QUADS * b + m
                    pe.wait_ge(taken, 8 * quad + 8)
                    if m == 0:
                        pe.wait_ge(v_done, ST * (b + 1))
                    out = ps_p[bank_of_quad(at)]
                    for i in range(ST):
                        for g in range(2):
                            c = (2 * m + g) * 2 * HD
                            last = pe.matmul(out[2 * HD * g:2 * HD * (g + 1), 0:2 * T], vs[par][:, i, c:c + 2 * HD],
                                             pT[m % 2][:, i, 2 * T * g:2 * T * (g + 1)],
                                             start=(i == 0), stop=(i == ST - 1), tile_position=(0, 2 * HD * g))
                    last.then_inc(pv_done, 1)

                def step(b, par, h):
                    n = H * b + h
                    scores(b, par, n, h)
                    if unit_here(b, h):
                        unit(b + 1, 1 - par, h)
                    if h % 4 == 3 and started(n, 7):
                        if isinstance(b, int) and b == B - 1:
                            pe.wait_ge(v_done, ST * B)
                            pe.wait_ge(o_done, QUADS * b - 1 + h // 4)
                        else:
                            unit_read(b + 1, h - 1 if h < U else U - 2)
                        if h > 3:
                            weighted_sum(b, par, h // 4 - 1, h)
                        else:
                            weighted_sum(b - 1, 1 - par, QUADS - 1, h)
                    if started(n, 2):
                        transposes(n - 2, h - 2)

                for u in range(U):
                    unit(0, 0, u)
                pe.wait_ge(consts, 9)
                batches(pe, step)
                transposes(H * B - 2, H - 2)
                transposes(H * B - 1, H - 1)
                pe.wait_ge(o_done, QUADS * B - 2)
                weighted_sum(B - 1, 1, QUADS - 1, 3)


def phase_feed_forward(nc, sem, o_d, x1_d, wo, bo, w_gate, w_up, w_down, biggest, out):
    PIECES = 3 * KD
    SLOTS = 4
    with ExitStack() as ctx:
        def sb(name, shape, dt=F32):
            return ctx.enter_context(nc.sbuf_tensor("E_" + name, shape, dt))

        def psum(name):
            return ctx.enter_context(nc.psum_tensor("E_" + name, [P, 512], F32))

        with nc.sbuf_tensor("E_w_f32", [P, PIECES, F], F32) as w_f32:
            pass
        w_f32r = sb("w_f32r", [P, PIECES, F], F32R)
        with nc.sbuf_tensor("E_below", [P, 2 * KF * GT - SLOTS * F], F32):
            with nc.sbuf_tensor("E_w_int", [P, SLOTS, F], I32) as w_int:
                pass
        hs = Split(sb, "hidden", [P, KF, GT])
        wos = Split(sb, "wo", [P, KD, D])
        acts = Split(sb, "acts", [P, KD, GT])
        oraw = sb("oraw", [P, KD, GT])
        x2 = sb("x2", [P, TT, D])
        x1b = [sb(f"x1b{i}", [P, D]) for i in range(2)]
        bo_b = sb("bo_b", [P, D])
        gated = [sb(f"gated{i}", [P, HALF]) for i in range(2)]
        r = {n: sb("r_" + n, [P, D]) for n in "ab"}
        stats = {n: sb("stats_" + n, [P, 6]) for n in "ab"}
        mv = {n: sb("mv_" + n, [P, 2]) for n in "ab"}
        var_eps = {n: sb("var_eps_" + n, [P, 1]) for n in "ab"}
        rstd = {n: sb("rstd_" + n, [P, 1]) for n in "ab"}
        y = [sb(f"y{i}", [P, D]) for i in range(2)]
        minus_half, ident = sb("minus_half", [P, 1]), sb("ident", [P, P])
        biggest1, biggest_all = sb("biggest1", [P, 1]), sb("biggest_all", [P, 1])
        inexact = sb("inexact", [P, 1], I32)
        ps_g, ps_u = [psum(f"ps_g{i}") for i in range(2)], [psum(f"ps_u{i}") for i in range(2)]
        ps_t = [psum(f"ps_t{i}") for i in range(2)]
        ps_y, ps_d = psum("ps_y"), psum("ps_d")

        wo_loaded, wo_high, wo_low = sem("E_wo_loaded"), sem("E_wo_high"), sem("E_wo_low")
        int_loaded = [sem(f"E_int_loaded{i}") for i in range(SLOTS)]
        int_done = sem("E_int_done")
        all_max, flagged = sem("E_all_max"), sem("E_flagged")
        b_loaded, consts = sem("E_b_loaded"), sem("E_consts")
        o_loaded = sem("E_o_loaded")
        o_high, o_low = sem("E_o_high"), sem("E_o_low")
        x1_loaded, x1b_done = [sem("E_x1_loaded0"), sem("E_x1_loaded1")], sem("E_x1b_done")
        y_done, t_done, th_done, tl_done = (sem("E_" + n) for n in ("y_done", "t_done", "th_done", "tl_done"))
        gu_done, silu_done, h_done, hh_done, hl_done = (sem("E_" + n) for n in
                                                        ("gu_done", "silu_done", "h_done", "hh_done", "hl_done"))
        d_done = sem("E_d_done")
        sum_done = {n: sem("E_sum_" + n) for n in "ab"}
        stat_done = {n: sem("E_stat_" + n) for n in "ab"}
        mv_done = {n: sem("E_mv_" + n) for n in "ab"}
        eps_done = {n: sem("E_eps_" + n) for n in "ab"}
        rstd_done = {n: sem("E_rstd_" + n) for n in "ab"}
        norm_done = {n: sem("E_norm_" + n) for n in "ab"}
        stored, passed = [sem("E_stored0"), sem("E_stored1")], sem("E_passed")
        HU = 2 * KF

        def unit(u):
            return 2 * (u // 4) + u % 2, u // 2 % 2

        def groups(eng, body):
            body(0)
            with eng.Fori(1, NG - 1) as g:
                body(g)

        def slot_count(g, i):
            return (TT - i % 2 + 1) // 2 * g + i // 2

        def piece(n):
            if n < 2 * KD:
                return (w_gate, w_up)[n // KD][n % KD * P:(n % KD + 1) * P, :]
            k = (n - 2 * KD) * (KF // KD)
            return w_down[k * P:(k + KF // KD) * P, :].rearrange("(a p) n -> p a n", p=P)

        def place(t, n):
            return t[:, n, :] if n < 2 * KD else t[:, n, :].rearrange("p (a n) -> p a n", n=D)

        with nc.Block() as block:

            @block.sync
            def _(sp):
                o_rows = o_d.rearrange("(k p) t -> p k t", p=P)

                def load_o(g):
                    if later(g):
                        sp.wait_ge(o_low, KD * g)
                    sp.dma_start(oraw[:, :, :], o_rows[:, :, col(g * GT, GT)]).then_inc(o_loaded, 16)

                def load_x1(g, i):
                    if i % 2 == 0 or later(g) or i > 1:
                        wait(sp, sum_done["a"], TT * g + i - (0 if i == 0 else 1))
                    src = x1_d.rearrange("(t p) n -> t p n", p=P)
                    n = TT * g + i
                    sp.dma_start(x1b[i % 2][:, :], src[n] if isinstance(n, int) else
                                 src[bass.ds(n, 1)].rearrange("a p n -> (a p) n")).then_inc(x1_loaded[i % 2], 16)

                def store(g, i):
                    n = TT * g + i
                    sp.wait_ge(norm_done["b"], n + 1)
                    dst = out.rearrange("(t p) n -> t p n", p=P)
                    sp.dma_start(dst[n] if isinstance(n, int) else
                                 dst[bass.ds(n, 1)].rearrange("a p n -> (a p) n"), y[i % 2][:, :])\
                      .then_inc(stored[i % 2], 16)

                sp.dma_start(x2[:, 0:KD, :], wo.rearrange("(k p) n -> p k n", p=P)).then_inc(wo_loaded, 16)
                sp.dma_start(bo_b[:, :], bo.rearrange("(a n) -> a n", a=1).broadcast_to([P, D])).then_inc(b_loaded, 16)
                load_o(0)
                load_x1(0, 0)
                load_x1(0, 1)
                for n in range(PIECES):
                    wait(sp, int_done, n - SLOTS + 1)
                    slot = w_int[:, n % SLOTS, :]
                    sp.dma_start(slot.rearrange("p (a n) -> p a n", n=D) if n >= 2 * KD else slot, piece(n))\
                      .then_inc(int_loaded[n % SLOTS], 16)
                    if n in (4, 6, 8):
                        load_x1(0, n // 2)
                load_o(1)

                def body(g, ahead=True):
                    for i in range(TT):
                        load_x1(g + 1, i)
                        if i == 0 and ahead:
                            load_o(g + 2)
                        store(g, i)

                body(0)
                with sp.Fori(1, NG - 2) as g:
                    body(g)
                body(NG - 2, ahead=False)
                for i in range(TT):
                    store(NG - 1, i)
                sp.wait_ge(stored[0], 16 * ((TT + 1) // 2) * NG)
                sp.wait_ge(stored[1], 16 * (TT // 2) * NG)

            @block.gpsimd
            def _(pool):
                pool.memset(minus_half[:, :], -0.5).then_inc(consts, 1)
                pool.memset(ident[:, :], 0.0).then_inc(consts, 1)
                pool.wait_ge(consts, 2)
                pool.affine_select(out=ident[:, :], in_=ident[:, :], compare_op=ALU.not_equal, fill=1.0,
                                   base=0, pattern=[[-1, P]], channel_multiplier=1).then_inc(consts, 1)
                pool.wait_ge(b_loaded, 16)

                def add_bias(g, i):
                    pool.wait_ge(x1_loaded[i % 2], 16 * slot_count(g, i) + 16)
                    pool.tensor_tensor(x1b[i % 2][:, :], x1b[i % 2][:, :], bo_b[:, :], ALU.add).then_inc(x1b_done, 1)

                def rstd_of(name, n):
                    pool.wait_ge(eps_done[name], n + 1)
                    wait(pool, norm_done[name], n)
                    pool.tensor_tensor(rstd[name][:, :], var_eps[name][:, :], minus_half[:, :], ALU.pow)\
                        .then_inc(rstd_done[name], 1)

                def low_h(g):
                    for u in range(HU):
                        n, (c, h) = HU * g + u, unit(u)
                        pool.wait_ge(hh_done, n + 1)
                        pool.wait_ge(h_done, n + 1)
                        cols = slice(h * HALF, (h + 1) * HALF)
                        pool.tensor_tensor(hs[1][:, c, cols], gated[u % 2][:, :], hs[0][:, c, cols].bitcast(F32),
                                           ALU.subtract).then_inc(hl_done, 1)

                def body(g):
                    low_h(g)
                    for i in range(TT):
                        add_bias(g + 1, i)
                        rstd_of("b", TT * g + i)
                        rstd_of("a", TT * (g + 1) + i)

                pool.wait_ge(all_max, 1)
                pool.partition_all_reduce(biggest_all[:, :], biggest1[:, :], P, bass.bass_isa.ReduceOp.max)\
                    .then_inc(all_max, 1)
                for i in range(TT):
                    add_bias(0, i)
                    rstd_of("a", i)
                groups(pool, body)
                low_h(NG - 1)
                for i in range(TT):
                    rstd_of("b", TT * (NG - 1) + i)

            @block.scalar
            def _(act):
                def high_o(g):
                    act.wait_ge(o_loaded, 16 * g + 16)
                    if later(g):
                        act.wait_ge(gu_done, HU * g)
                    for k in range(KD):
                        act.activation(acts[0][:, k, :], oraw[:, k, :], ACT.Copy).then_inc(o_high, 1)

                def high_x2(g, i):
                    act.wait_ge(t_done, TT * g + i + 1)
                    act.activation(acts[0][:, :, i * P:(i + 1) * P],
                                   ps_t[i % 2][:, :].rearrange("p (k c) -> p k c", k=KD), ACT.Copy)\
                       .then_inc(th_done, 1)

                def silu_and_high(g, convert):
                    def high(u):
                        c, h = unit(u)
                        act.wait_ge(h_done, HU * g + u + 1)
                        act.activation(hs[0][:, c, h * HALF:(h + 1) * HALF], gated[u % 2][:, :], ACT.Copy)\
                           .then_inc(hh_done, 1)

                    for u in range(HU):
                        n = HU * g + u
                        act.wait_ge(gu_done, n + 1)
                        wait(act, hl_done, n - 1)
                        act.activation(gated[u % 2][:, :], ps_g[u % 2][:, 0:HALF], ACT.Silu, scale=FSCALE)\
                           .then_inc(silu_done, 1)
                        if u == 0:
                            high_x2(g, TT - 1)
                        else:
                            high(u - 1)
                        if not later(g) and u in (1, 3, 5, 7):
                            convert(2 * KD + u // 2)
                    high(HU - 1)

                act.wait_ge(wo_loaded, 16)
                act.activation(wos[0][:, :, :], x2[:, 0:KD, :], ACT.Copy).then_inc(wo_high, 1)
                high_o(0)

                def with_weights(tile):
                    def convert(n):
                        slot = w_int[:, n % SLOTS, :]
                        act.wait_ge(int_loaded[n % SLOTS], 16 * (n // SLOTS) + 16)
                        act.activation(place(tile, n), slot.rearrange("p (a n) -> p a n", n=D) if n >= 2 * KD else slot,
                                       ACT.Copy).then_inc(int_done, 1)

                    def body(g):
                        silu_and_high(g, convert)
                        high_o(g + 1)
                        for i in range(TT - 1):
                            high_x2(g + 1, i)

                    for n in range(2 * KD):
                        convert(n)
                        if n in (1, 3, 5, 7):
                            high_x2(0, n // 2)
                    groups(act, body)
                    silu_and_high(NG - 1, convert)

                act.wait_ge(flagged, 1)
                with act.If(act.value_load(inexact[0:1, 0:1], min_val=0, max_val=1) == 1):
                    with_weights(w_f32)
                with act.Else():
                    with_weights(w_f32r)

            @block.vector
            def _(dve):
                def add_and_stats(name, n, add):
                    wait(dve, norm_done[name], n)
                    add(r[name][:, :]).then_inc(sum_done[name], 1)
                    dve.wait_ge(sum_done[name], n + 1)
                    dve.bn_stats(stats[name][:, :], r[name][:, :]).then_inc(stat_done[name], 1)
                    wait_apart(dve, stat_done[name], n + 1, passed)
                    dve.bn_aggr(mv[name][:, :], stats[name][:, :]).then_inc(mv_done[name], 1)
                    dve.wait_ge(mv_done[name], n + 1)
                    dve.tensor_scalar(var_eps[name][:, :], mv[name][:, 1:2], EPS, None, ALU.add)\
                       .then_inc(eps_done[name], 1)

                def normalise(name, n, dst):
                    dve.wait_ge(rstd_done[name], n + 1)
                    dve.tensor_scalar(dst, r[name][:, :], mv[name][:, 0:1], rstd[name][:, 0:1],
                                      ALU.subtract, ALU.mult).then_inc(norm_done[name], 1)

                def second_sum(g, i):
                    n = TT * g + i
                    dve.wait_ge(y_done, n + 1)
                    dve.wait_ge(x1b_done, n + 1)
                    add_and_stats("a", n, lambda dst: dve.tensor_tensor(dst, ps_y[:, :], x1b[i % 2][:, :], ALU.add))

                def third_sum(g, i):
                    n = TT * g + i
                    dve.wait_ge(d_done, n + 1)
                    add_and_stats("b", n, lambda dst: dve.scalar_tensor_tensor(
                        dst, ps_d[:, :], FSCALE, x2[:, i, :], ALU.mult, ALU.add))

                def third_norm(g, i):
                    wait(dve, stored[i % 2], 16 * slot_count(g, i))
                    normalise("b", TT * g + i, y[i % 2][:, :])

                def low_o(g):
                    for k in range(KD):
                        dve.wait_ge(o_high, KD * g + k + 1)
                        dve.wait_ge(o_loaded, 16 * g + 16)
                        dve.tensor_tensor(acts[1][:, k, :], oraw[:, k, :], acts[0][:, k, :].bitcast(F32),
                                          ALU.subtract).then_inc(o_low, 1)

                def low_x2(g, i):
                    n = TT * g + i
                    dve.wait_ge(t_done, n + 1)
                    dve.wait_ge(th_done, n + 1)
                    dve.tensor_tensor(acts[1][:, :, i * P:(i + 1) * P],
                                      ps_t[i % 2][:, :].rearrange("p (k c) -> p k c", k=KD),
                                      acts[0][:, :, i * P:(i + 1) * P].bitcast(F32), ALU.subtract)\
                       .then_inc(tl_done, 1)

                def gate(g):
                    for u in range(HU):
                        n = HU * g + u
                        dve.wait_ge(gu_done, n + 1)
                        dve.wait_ge(silu_done, n + 1)
                        dve.scalar_tensor_tensor(gated[u % 2][:, :], ps_u[u % 2][:, 0:HALF], FSCALE, gated[u % 2][:, :],
                                                 ALU.mult, ALU.mult).then_inc(h_done, 1)
                        if u == 0:
                            low_x2(g, TT - 1)

                def body(g):
                    gate(g)
                    low_o(g + 1)
                    for i in range(TT):
                        third_sum(g, i)
                        second_sum(g + 1, i)
                        third_norm(g, i)
                        normalise("a", TT * (g + 1) + i, x2[:, i, :])
                        if i:
                            low_x2(g + 1, i - 1)

                dve.tensor_reduce(biggest1[:, :], biggest[:, :], AX.X, ALU.max).then_inc(all_max, 1)
                dve.wait_ge(all_max, 2)
                dve.tensor_scalar(inexact[:, :], biggest_all[:, :], EXACT, None, ALU.is_gt).then_inc(flagged, 1)
                dve.wait_ge(wo_high, 1)
                dve.wait_ge(wo_loaded, 16)
                dve.tensor_tensor(wos[1][:, :, :], x2[:, 0:KD, :], wos[0][:, :, :].bitcast(F32), ALU.subtract)\
                   .then_inc(wo_low, 1)
                dve.wait_ge(wo_low, 1)
                low_o(0)
                for i in range(TT):
                    second_sum(0, i)
                    normalise("a", i, x2[:, i, :])
                    if i:
                        low_x2(0, i - 1)
                groups(dve, body)
                gate(NG - 1)
                for i in range(TT):
                    third_sum(NG - 1, i)
                    third_norm(NG - 1, i)

            @block.tensor
            def _(pe):
                def project_o(g, i):
                    n = TT * g + i
                    if i == 0:
                        pe.wait_ge(o_low, KD * (g + 1))
                    wait(pe, sum_done["a"], n)
                    products(pe, ps_y[:, :], SPLIT, KD, lambda a, k: acts[a][:, k, i * P:(i + 1) * P],
                             lambda a, k: wos[a][:, k, :]).then_inc(y_done, 1)

                def transpose_x2(g, i):
                    n = TT * g + i
                    pe.wait_ge(norm_done["a"], n + 1)
                    wait(pe, tl_done, n if i == 0 else n - 1)
                    for k in range(KD):
                        last = pe.transpose(ps_t[i % 2][:, k * P:(k + 1) * P], x2[:, i, k * P:(k + 1) * P],
                                            ident[:, :])
                    last.then_inc(t_done, 1)

                def feed_forward(w, view):
                    both = ((0, 0), (0, 1))

                    def gate_and_up(g):
                        for u in range(HU):
                            n, (c, h) = HU * g + u, unit(u)
                            if u == 0:
                                pe.wait_ge(tl_done, TT * g + (HALF + P - 1) // P)
                            if u == 2:
                                pe.wait_ge(tl_done, TT * (g + 1))
                            wait(pe, h_done, n - 1)
                            for ps, first in ((ps_g, 0), (ps_u, KD)):
                                last = products(pe, ps[u % 2][:, 0:HALF], both, KD,
                                                lambda a, k: w[:, first + k, c * P:(c + 1) * P],
                                                lambda a, k: view(acts[a][:, k, h * HALF:(h + 1) * HALF]))
                            last.then_inc(gu_done, 1)
                            if u == 0:
                                transpose_x2(g, TT - 1)

                    def down(g, i):
                        n = TT * g + i
                        if not later(g) and i == 0:
                            pe.wait_ge(int_done, PIECES)
                        if i == 0:
                            pe.wait_ge(hl_done, HU * (g + 1) - 2)
                        if i == 2:
                            pe.wait_ge(hl_done, HU * (g + 1))
                        wait(pe, sum_done["b"], n)
                        products(pe, ps_d[:, :], ((0, 0), (1, 0)), KF,
                                 lambda a, k: view(hs[a][:, k, i * P:(i + 1) * P]),
                                 lambda a, k: w[:, 2 * KD + k // 3, k % 3 * D:(k % 3 + 1) * D]).then_inc(d_done, 1)

                    def body(g):
                        gate_and_up(g)
                        for i in range(TT):
                            down(g, i)
                            project_o(g + 1, i)
                            if i:
                                transpose_x2(g + 1, i - 1)

                    groups(pe, body)
                    gate_and_up(NG - 1)
                    for i in range(TT):
                        down(NG - 1, i)

                pe.wait_ge(wo_low, 1)
                pe.wait_ge(consts, 3)
                for i in range(TT):
                    project_o(0, i)
                    if i:
                        transpose_x2(0, i - 1)
                pe.wait_ge(flagged, 1)
                pe.wait_ge(int_done, 2 * KD)
                with pe.If(pe.value_load(inexact[0:1, 0:1], min_val=0, max_val=1) == 1):
                    feed_forward(w_f32, lambda x: x.bitcast(F32))
                with pe.Else():
                    feed_forward(w_f32r, lambda x: x)


def build_decoder(nc, x, xT, ctxT, a_wq, a_wk, a_wv, a_wo, a_bo, a_w, a_v,
                  x_wq, x_bq, x_wk, x_bk, x_wv, x_bv, x_wo, x_bo, w_gate, w_up, w_down, out):
    with ExitStack() as ctx:
        def sem(name):
            return ctx.enter_context(nc.semaphore(name))

        def dram(name, shape):
            return nc.dram_tensor(name, shape, F32, kind="Internal").ap()

        q_d, k_d, v_d = dram("self_q", [D, N]), dram("self_k", [D, N]), dram("self_v", [N, D])
        o_d, x1_d = dram("self_o", [D, N]), dram("x1", [N, D])
        cq_d, co_d = dram("cross_q", [2, D, N]), dram("cross_o", [D, N])
        rhat_d = dram("rhat", [T, H * T])
        biggest = ctx.enter_context(nc.sbuf_tensor("biggest", [P, 3], F32))

        def weights(held, names):
            return [Split(lambda n, shape, dt: held.enter_context(nc.sbuf_tensor(n, shape, dt)), n, [P, KD, D])
                    for n in names]

        phase_qkv(nc, sem, xT, a_wq, a_wk, a_wv, a_w, a_v, q_d, k_d, v_d, rhat_d)
        with ExitStack() as outer:
            cross_w = weights(outer, ("cross_wk", "cross_wv"))
            with ExitStack() as inner:
                norm_w = weights(inner, ("self_wo", "cross_wq"))
                staging = [inner.enter_context(nc.sbuf_tensor(f"wstage{i}", [P, KD, D], F32)) for i in range(2)]
                phase_self_attention(nc, sem, q_d, k_d, v_d, rhat_d, o_d, (a_wo, x_wq), staging)
                phase_norm_and_queries(nc, sem, o_d, x, norm_w, a_bo, x_bq, x1_d, cq_d,
                                       (a_wo, x_wq, x_wk, x_wv), cross_w, staging,
                                       w_gate, w_up, w_down, biggest)
            phase_cross_attention(nc, sem, ctxT, cq_d, cross_w, x_bk, x_bv, co_d)
        phase_feed_forward(nc, sem, co_d, x1_d, x_wo, x_bo, w_gate, w_up, w_down, biggest, out)


def kernel(x, ctx_1024, L0_attn_Wq, L0_attn_Wk, L0_attn_Wv, L0_attn_Wo, L0_attn_bo, L0_attn_w, L0_attn_v,
           L0_xattn_Wq, L0_xattn_bq, L0_xattn_Wk, L0_xattn_bk, L0_xattn_Wv, L0_xattn_bv, L0_xattn_Wo, L0_xattn_bo,
           L0_ffn_w_gate, L0_ffn_w_up, L0_ffn_w_down):
    import numpy as np
    import concourse.bacc as bacc
    from concourse.bass_utils import run_bass_kernel_spmd

    def columns(bias):
        return np.asarray(bias).reshape(KD, P).T

    tokens = np.asarray(x).reshape(N, D)
    given = {
        "x": tokens, "xT": tokens.T, "ctxT": np.asarray(ctx_1024).transpose(0, 2, 1),
        "a_wq": L0_attn_Wq, "a_wk": L0_attn_Wk, "a_wv": L0_attn_Wv, "a_wo": L0_attn_Wo, "a_bo": L0_attn_bo,
        "a_w": L0_attn_w, "a_v": L0_attn_v,
        "x_wq": np.asarray(L0_xattn_Wq).T, "x_bq": columns(L0_xattn_bq),
        "x_wk": np.asarray(L0_xattn_Wk).T, "x_bk": columns(L0_xattn_bk),
        "x_wv": np.asarray(L0_xattn_Wv).T, "x_bv": columns(L0_xattn_bv),
        "x_wo": np.asarray(L0_xattn_Wo).T, "x_bo": L0_xattn_bo,
        "w_gate": np.asarray(L0_ffn_w_gate).T, "w_up": np.asarray(L0_ffn_w_up).T,
        "w_down": np.asarray(L0_ffn_w_down).T,
    }
    nc = bacc.Bacc("TRN2", target_bir_lowering=False, num_devices=1)
    arrays, args = {}, {}
    for name, a in given.items():
        arrays["in_" + name] = np.ascontiguousarray(a)
        args[name] = nc.dram_tensor("in_" + name, arrays["in_" + name].shape,
                                    mybir.dt.from_np(arrays["in_" + name].dtype), kind="ExternalInput").ap()
    args["out"] = nc.dram_tensor("out_0", [N, D], F32, kind="ExternalOutput").ap()
    build_decoder(nc, **args)
    r = run_bass_kernel_spmd(nc, [arrays], core_ids=[0])
    return r.results[0]["out_0"].reshape(B, T, D)
```
